# Optimizing a Trainium2 kernel written in Bass

```python
import numpy as np
import jax
import jax.numpy as jnp

def _softmax(x, axis=-1):
    return jax.nn.softmax(x, axis=axis)

def _gelu(x):
    return jax.nn.gelu(x, approximate=True)

def _silu(x):
    return jax.nn.silu(x)

def _sigmoid(x):
    return jax.nn.sigmoid(x)

def _layernorm(x, axis=-1, eps=1e-05):
    m = jnp.mean(x, axis=axis, keepdims=True)
    v = jnp.var(x, axis=axis, keepdims=True)
    return (x - m) / jnp.sqrt(v + eps)

def _scatter_add(tgt, idx, src, axis=0):
    return tgt.at[idx].add(src)

def _segment_sum(src, seg, n):
    return jax.ops.segment_sum(src, seg, n)
kernel_name = 'mk_decoder_postln_d1_seqx_r8_17dfec'

def setup_inputs(seed: int=0):
    np.random.seed(seed)
    _w = jnp.asarray

    def _rec_inputs():
        import jax
        import jax.numpy as jnp
        _rk = jax.random.key(seed)
        x = -0.0003929 + 0.9999 * jax.random.normal(jax.random.fold_in(_rk, 1), (8, 256, 128), jnp.float32)
        _lenS = 256 - jax.random.randint(jax.random.fold_in(_rk, 7), (8,), 0, max(1, 256 // 4) + 1, jnp.int32)
        _lenS2 = 1601 - jax.random.randint(jax.random.fold_in(_rk, 8), (8,), 0, max(1, 1601 // 4) + 1, jnp.int32)
        _ctx_1024P = jax.random.normal(jax.random.fold_in(_rk, 11), (8, 16, 128), jnp.float32)
        _ctx_1024c = jax.random.dirichlet(jax.random.fold_in(_rk, 511), 0.3 * jnp.ones((16,), jnp.float32), (8, 1601))
        _ctx_1024t = jnp.einsum('bsk,bkd->bsd', _ctx_1024c, _ctx_1024P)
        _ctx_1024t = _ctx_1024t * jax.lax.rsqrt(jnp.mean(jnp.square(_ctx_1024t)) + 1e-12) * 0.953939
        ctx_1024 = -1.39393e-06 + 0.999914 * (_ctx_1024t + 0.3 * jax.random.normal(jax.random.fold_in(_rk, 611), (8, 1601, 128), jnp.float32))
        return (x, ctx_1024)
    x, ctx_1024 = _rec_inputs()

    def _L0_attn_setup():
        import jax, jax.numpy as jnp
        import numpy as np
        import math
        D_MODEL = 128
        N_HEAD = 16
        N_BR = 4
        DH = D_MODEL // N_HEAD
        H_TOT = N_BR * N_HEAD
        B, T = (1, 128)
        SCALE = math.pi / math.sqrt(3.0)
        ATTNSCALE = DH ** (-0.5)

        def _rope(x):
            t_len, d = (x.shape[2], x.shape[-1])
            inv_freq = 1.0 / 10000.0 ** (jnp.arange(0, d, 2, dtype=jnp.float32) / d)
            freqs = jnp.arange(t_len, dtype=jnp.float32)[:, None] * inv_freq[None, :]
            cos, sin = (jnp.cos(freqs), jnp.sin(freqs))
            x1, x2 = (x[..., 0::2], x[..., 1::2])
            return jnp.concatenate([-x2 * sin + x1 * cos, x1 * sin + x2 * cos], axis=-1)
        key = jax.random.key(seed)
        ks = jax.random.split(key, 12)
        s = D_MODEL ** (-0.5)
        return {'X': jax.random.normal(ks[0], (B, T, D_MODEL), jnp.float32), 'W_Q': jax.random.normal(ks[1], (D_MODEL, D_MODEL * N_BR), jnp.float32) * s, 'b_Q': jax.random.normal(ks[2], (D_MODEL * N_BR,), jnp.float32) * 0.02, 'W_K': jax.random.normal(ks[3], (D_MODEL, D_MODEL), jnp.float32) * s, 'b_K': jax.random.normal(ks[4], (D_MODEL,), jnp.float32) * 0.02, 'W_V': jax.random.normal(ks[5], (D_MODEL, D_MODEL), jnp.float32) * s, 'b_V': jax.random.normal(ks[6], (D_MODEL,), jnp.float32) * 0.02, 'sink_scalars': jax.random.uniform(ks[7], (H_TOT,), jnp.float32, 0.0, 0.1), 'v_nulls': jax.random.normal(ks[8], (N_BR, D_MODEL), jnp.float32) * 0.02, 'W_O': jax.random.normal(ks[9], (N_BR, D_MODEL, D_MODEL), jnp.float32) * s, 'W_O_bias': jax.random.normal(ks[10], (N_BR, D_MODEL), jnp.float32) * 0.02}
    _L0_attn_all = _L0_attn_setup()
    _L0_attn_in = {k: v for k, v in _L0_attn_all.items() if k in ('W_Q', 'b_Q', 'W_K', 'b_K', 'W_V', 'b_V', 'sink_scalars', 'v_nulls', 'W_O', 'W_O_bias')}
    del _L0_attn_all

    def _L0_xattn_setup():
        import jax, jax.numpy as jnp
        import numpy as np
        EMBED_DIM = 128
        Q_HEADS = 16
        KV_HEADS = 8
        HEAD_DIM = EMBED_DIM // Q_HEADS
        KV_EMBED = HEAD_DIM * KV_HEADS
        GROUPS = Q_HEADS // KV_HEADS
        LN_EPS = 1e-05
        RMS_EPS = 1e-06

        def _rms_norm(x):
            return x * jax.lax.rsqrt(jnp.mean(jnp.square(x), axis=-1, keepdims=True) + RMS_EPS)

        def _act_quant(x):
            scale = 127.0 / jnp.maximum(jnp.max(jnp.abs(x), axis=-1, keepdims=True), 1e-05)
            return jnp.clip(jnp.round(x * scale), -128.0, 127.0) / scale

        def _weight_quant(w):
            scale = 1.0 / jnp.maximum(jnp.mean(jnp.abs(w)), 1e-05)
            return jnp.clip(jnp.round(w * scale), -1.0, 1.0) / scale

        def _ste(a, q):
            return a + jax.lax.stop_gradient(q - a)

        def bit_linear(x, w):
            xn = _rms_norm(x)
            xq = _ste(xn, _act_quant(xn))
            wq = _ste(w, _weight_quant(w))
            return jnp.einsum('bni,oi->bno', xq, wq)
        key = jax.random.key(seed)
        ks = jax.random.split(key, 6)
        B, N, S, D = (16, 128, 32, EMBED_DIM)
        s = D ** (-0.5)
        return {'x': jax.random.normal(ks[0], (B, N, D), jnp.float32), 'y': jax.random.normal(ks[1], (B, S, D), jnp.float32), 'wq': jax.random.normal(ks[2], (D, D), jnp.float32) * s, 'wk': jax.random.normal(ks[3], (KV_EMBED, D), jnp.float32) * s, 'wv': jax.random.normal(ks[4], (KV_EMBED, D), jnp.float32) * s, 'wo': jax.random.normal(ks[5], (D, D), jnp.float32) * s, 'ln_gamma': jnp.ones((D,), jnp.float32), 'ln_beta': jnp.zeros((D,), jnp.float32)}
    _L0_xattn_all = _L0_xattn_setup()
    _L0_xattn_in = {k: v for k, v in _L0_xattn_all.items() if k in ('wq', 'wk', 'wv', 'wo', 'ln_gamma', 'ln_beta')}
    del _L0_xattn_all

    def _L0_ffn_setup():
        import jax, jax.numpy as jnp
        import numpy as np
        B, S, H, F, E = (1, 256, 128, 256, 8)

        def _swiglu(x, wg, wu, wd):
            return jax.nn.silu(x @ wg.T) * (x @ wu.T) @ wd.T
        key = jax.random.key(seed)
        ks = jax.random.split(key, 8)
        sc = 1.0 / np.sqrt(H)
        scf = 1.0 / np.sqrt(F)
        return {'hidden_states': jax.random.normal(ks[0], (B, S, H), jnp.float32), 'gate_w': jax.random.normal(ks[1], (E, H), jnp.float32) * sc, 'shared_gate': jax.random.normal(ks[2], (F, H), jnp.float32) * sc, 'shared_up': jax.random.normal(ks[3], (F, H), jnp.float32) * sc, 'shared_down': jax.random.normal(ks[4], (H, F), jnp.float32) * scf, 'r_gate': jax.random.normal(ks[5], (E, F, H), jnp.float32) * sc, 'r_up': jax.random.normal(ks[6], (E, F, H), jnp.float32) * sc, 'r_down': jax.random.normal(ks[7], (E, H, F), jnp.float32) * scf}
    _L0_ffn_all = _L0_ffn_setup()
    _L0_ffn_in = {k: v for k, v in _L0_ffn_all.items() if k in ('gate_w', 'shared_gate', 'shared_up', 'shared_down', 'r_gate', 'r_up', 'r_down')}
    del _L0_ffn_all
    return {'x': x, 'ctx_1024': ctx_1024, 'L0_attn_W_Q': _L0_attn_in['W_Q'], 'L0_attn_b_Q': _L0_attn_in['b_Q'], 'L0_attn_W_K': _L0_attn_in['W_K'], 'L0_attn_b_K': _L0_attn_in['b_K'], 'L0_attn_W_V': _L0_attn_in['W_V'], 'L0_attn_b_V': _L0_attn_in['b_V'], 'L0_attn_sink_scalars': _L0_attn_in['sink_scalars'], 'L0_attn_v_nulls': _L0_attn_in['v_nulls'], 'L0_attn_W_O': _L0_attn_in['W_O'], 'L0_attn_W_O_bias': _L0_attn_in['W_O_bias'], 'L0_xattn_wq': _L0_xattn_in['wq'], 'L0_xattn_wk': _L0_xattn_in['wk'], 'L0_xattn_wv': _L0_xattn_in['wv'], 'L0_xattn_wo': _L0_xattn_in['wo'], 'L0_xattn_ln_gamma': _L0_xattn_in['ln_gamma'], 'L0_xattn_ln_beta': _L0_xattn_in['ln_beta'], 'L0_ffn_gate_w': _L0_ffn_in['gate_w'], 'L0_ffn_shared_gate': _L0_ffn_in['shared_gate'], 'L0_ffn_shared_up': _L0_ffn_in['shared_up'], 'L0_ffn_shared_down': _L0_ffn_in['shared_down'], 'L0_ffn_r_gate': _L0_ffn_in['r_gate'], 'L0_ffn_r_up': _L0_ffn_in['r_up'], 'L0_ffn_r_down': _L0_ffn_in['r_down']}

def reference(x, ctx_1024, L0_attn_W_Q, L0_attn_b_Q, L0_attn_W_K, L0_attn_b_K, L0_attn_W_V, L0_attn_b_V, L0_attn_sink_scalars, L0_attn_v_nulls, L0_attn_W_O, L0_attn_W_O_bias, L0_xattn_wq, L0_xattn_wk, L0_xattn_wv, L0_xattn_wo, L0_xattn_ln_gamma, L0_xattn_ln_beta, L0_ffn_gate_w, L0_ffn_shared_gate, L0_ffn_shared_up, L0_ffn_shared_down, L0_ffn_r_gate, L0_ffn_r_up, L0_ffn_r_down):
    import jax
    import jax.numpy as jnp

    def _L0_attn_ref(X, W_Q, b_Q, W_K, b_K, W_V, b_V, sink_scalars, v_nulls, W_O, W_O_bias):
        import jax, jax.numpy as jnp
        import numpy as np
        import math
        D_MODEL = 128
        N_HEAD = 16
        N_BR = 4
        DH = D_MODEL // N_HEAD
        H_TOT = N_BR * N_HEAD
        B, T = (1, 128)
        SCALE = math.pi / math.sqrt(3.0)
        ATTNSCALE = DH ** (-0.5)

        def _rope(x):
            t_len, d = (x.shape[2], x.shape[-1])
            inv_freq = 1.0 / 10000.0 ** (jnp.arange(0, d, 2, dtype=jnp.float32) / d)
            freqs = jnp.arange(t_len, dtype=jnp.float32)[:, None] * inv_freq[None, :]
            cos, sin = (jnp.cos(freqs), jnp.sin(freqs))
            x1, x2 = (x[..., 0::2], x[..., 1::2])
            return jnp.concatenate([-x2 * sin + x1 * cos, x1 * sin + x2 * cos], axis=-1)
        Bv, Tv, C = X.shape
        q = (X @ W_Q + b_Q).reshape(Bv, Tv, H_TOT, DH).transpose(0, 2, 1, 3)
        k_base = (X @ W_K + b_K).reshape(Bv, Tv, N_HEAD, DH).transpose(0, 2, 1, 3)
        v_base = (X @ W_V + b_V).reshape(Bv, Tv, N_HEAD, DH).transpose(0, 2, 1, 3)
        k = jnp.tile(k_base, (1, N_BR, 1, 1))
        v = jnp.tile(v_base, (1, N_BR, 1, 1))
        q, k = (_rope(q), _rope(k))
        scores = jnp.einsum('bhtd,bhsd->bhts', q, k) * ATTNSCALE
        key_self = jnp.clip(jnp.sum(k * k, axis=-1), 1e-06, None)
        w = jax.nn.softplus(scores / jnp.sqrt(key_self)[:, :, None, :])
        causal = jnp.tril(jnp.ones((Tv, Tv), bool))
        w = jnp.where(causal, w, 0.0)
        w = w * jax.nn.sigmoid(SCALE * w)
        sinks = sink_scalars.reshape(1, H_TOT, 1, 1)
        w = jnp.where(w < sinks, 0.0, w)
        total = jnp.sum(w, axis=-1, keepdims=True) + sinks + 1e-06
        probs_tokens = w / total
        probs_sink = sinks / total
        out = jnp.einsum('bhts,bhsd->bhtd', probs_tokens, v)
        v_null = v_nulls.reshape(H_TOT, DH)[None, :, None, :]
        out = out + probs_sink * v_null
        context = out.reshape(Bv, N_BR, N_HEAD, Tv, DH).transpose(0, 1, 3, 2, 4)
        context = context.reshape(Bv, N_BR, Tv, C)
        y = jnp.einsum('bntc,ncd->bntd', context, W_O) + W_O_bias[None, :, None, :]
        return y.mean(axis=1)

    def _L0_xattn_ref(x, y, wq, wk, wv, wo, ln_gamma, ln_beta):
        import jax, jax.numpy as jnp
        import numpy as np
        EMBED_DIM = 128
        Q_HEADS = 16
        KV_HEADS = 8
        HEAD_DIM = EMBED_DIM // Q_HEADS
        KV_EMBED = HEAD_DIM * KV_HEADS
        GROUPS = Q_HEADS // KV_HEADS
        LN_EPS = 1e-05
        RMS_EPS = 1e-06

        def _rms_norm(x):
            return x * jax.lax.rsqrt(jnp.mean(jnp.square(x), axis=-1, keepdims=True) + RMS_EPS)

        def _act_quant(x):
            scale = 127.0 / jnp.maximum(jnp.max(jnp.abs(x), axis=-1, keepdims=True), 1e-05)
            return jnp.clip(jnp.round(x * scale), -128.0, 127.0) / scale

        def _weight_quant(w):
            scale = 1.0 / jnp.maximum(jnp.mean(jnp.abs(w)), 1e-05)
            return jnp.clip(jnp.round(w * scale), -1.0, 1.0) / scale

        def _ste(a, q):
            return a + jax.lax.stop_gradient(q - a)

        def bit_linear(x, w):
            xn = _rms_norm(x)
            xq = _ste(xn, _act_quant(xn))
            wq = _ste(w, _weight_quant(w))
            return jnp.einsum('bni,oi->bno', xq, wq)
        B, N, D = x.shape
        S = y.shape[1]
        q = bit_linear(x, wq).reshape(B, N, Q_HEADS, HEAD_DIM)
        k = bit_linear(y, wk).reshape(B, S, KV_HEADS, HEAD_DIM)
        v = bit_linear(y, wv).reshape(B, S, KV_HEADS, HEAD_DIM)
        q = jnp.transpose(q, (0, 2, 1, 3)) / HEAD_DIM ** 0.5
        q = q.reshape(B, KV_HEADS, GROUPS, N, HEAD_DIM)
        k = jnp.transpose(k, (0, 2, 1, 3))
        v = jnp.transpose(v, (0, 2, 1, 3))
        scores = jnp.einsum('bhgnd,bhsd->bhgns', q, k)
        attn = jax.nn.softmax(scores, axis=-1)
        out = jnp.einsum('bhgns,bhsd->bhgnd', attn, v)
        out = jnp.transpose(out, (0, 3, 1, 2, 4)).reshape(B, N, D)
        mu = jnp.mean(out, axis=-1, keepdims=True)
        var = jnp.mean(jnp.square(out - mu), axis=-1, keepdims=True)
        out = (out - mu) * jax.lax.rsqrt(var + LN_EPS) * ln_gamma + ln_beta
        return bit_linear(out, wo)

    def _L0_ffn_ref(hidden_states, gate_w, shared_gate, shared_up, shared_down, r_gate, r_up, r_down):
        import jax, jax.numpy as jnp
        import numpy as np
        B, S, H, F, E = (1, 256, 128, 256, 8)

        def _swiglu(x, wg, wu, wd):
            return jax.nn.silu(x @ wg.T) * (x @ wu.T) @ wd.T
        b, s, h = hidden_states.shape
        x = hidden_states.reshape(-1, h)
        shared_out = _swiglu(x, shared_gate, shared_up, shared_down)
        logits = x @ gate_w.T
        top_id = jnp.argmax(logits, axis=-1)
        score = jax.nn.sigmoid(jnp.max(logits, axis=-1))
        xs = x * score[:, None]

        def body(acc, ws):
            wg, wu, wd, e = ws
            xe = jnp.where((top_id == e)[:, None], xs, 0.0)
            return (acc + _swiglu(xe, wg, wu, wd), None)
        acc0 = jnp.zeros_like(x)
        routed_out, _ = jax.lax.scan(body, acc0, (r_gate, r_up, r_down, jnp.arange(E)))
        return (shared_out + routed_out).reshape(b, s, h)
    x = _layernorm(x + _L0_attn_ref(x, L0_attn_W_Q, L0_attn_b_Q, L0_attn_W_K, L0_attn_b_K, L0_attn_W_V, L0_attn_b_V, L0_attn_sink_scalars, L0_attn_v_nulls, L0_attn_W_O, L0_attn_W_O_bias), axis=-1)
    x = _layernorm(x + _L0_xattn_ref(x, ctx_1024, L0_xattn_wq, L0_xattn_wk, L0_xattn_wv, L0_xattn_wo, L0_xattn_ln_gamma, L0_xattn_ln_beta), axis=-1)
    x = _layernorm(x + _L0_ffn_ref(x, L0_ffn_gate_w, L0_ffn_shared_gate, L0_ffn_shared_up, L0_ffn_shared_down, L0_ffn_r_gate, L0_ffn_r_up, L0_ffn_r_down), axis=-1)
    return x

_drawn_inputs = setup_inputs


def setup_inputs(seed=0):
    import zlib

    import numpy as np

    out = dict(_drawn_inputs(seed))
    spreads = {'L0_xattn_ln_gamma': (1.0, 0.2), 'L0_xattn_ln_beta': (0.0, 0.1)}
    factors = {'L0_attn_b_Q': 6.592,
     'L0_attn_b_K': 6.414,
     'L0_attn_sink_scalars': 8.0,
     'L0_attn_v_nulls': 24.619}
    for name, (base, spread) in spreads.items():
        noise = np.random.default_rng([zlib.crc32(name.encode()), seed]).standard_normal(out[name].shape)
        drawn = base * np.exp(spread * noise) if base else spread * noise
        out[name] = jnp.asarray(drawn.astype(out[name].dtype))
    for name, factor in factors.items():
        out[name] = (out[name] * factor).astype(out[name].dtype)
    return out
```

```python
from contextlib import ExitStack
import math

import numpy as np

import concourse.bass as bass
from concourse import mybir

F32 = mybir.dt.float32
F16 = mybir.dt.float16
BF16 = mybir.dt.bfloat16
ALU = mybir.AluOpType
ACT = mybir.ActivationFunctionType
AX = mybir.AxisListType

P = 128
D = 128
B = 8
T = 256
TH = T // P
BR = 4
NH = 16
DH = 8
KV = 8
S2 = 1601
NT = 13
LAST = S2 - (NT - 1) * P
E = 9
F = 256
FC = F // P
CAP = 2.0 ** 60
MAGIC = 1.5 * 2.0 ** 23
GATE = math.pi / math.sqrt(3.0)
KGAIN = 16.0
ZSCALE = DH ** -0.5 / KGAIN
CHUNKS = [(0, 401), (401, 400), (801, 400), (1201, 400)]
KROWS = 6 * DH
SROWS = KROWS + 3
NZ = 3 * NH
NX = KV * NT
NM = NH * TH * len(CHUNKS)
N_WEIGHTS = 26

PER = dict(
    x_in=16, ctx_in=32,
    xT_ps=1, xT_sb=1, kproj=1, vproj=1, qproj=4, qproj_read=4, v1_ready=1,
    ksq_sb=1, knorm_ps=1, knorm_sb=1, krs=1, kparts=1, kscr=16, kstack=12 * 16,
    qparts=1, qscr=16, qstack=12 * 16,
    z=NZ, zexp=NZ, zcap=NZ, zln=NZ, zmax=NZ, gated=NH, masking=NH, bn_steps=16, thr=BR * NH, masked=NH,
    av1=4, av1_sb=4, nat1=8, nat1_read=8, ctxT_ps=2, ctxT_sb=2, y1=1,
    ln1_var=1, ln1_rstd=1, x1=1,
    csq=1, cn_ms=1, cn_r=1, yq=1, yT_ps=2, yT_sb=2, kvn=4, kvn_read=4, khl=1, kT_ps=2, kT_sb=2,
    k2scr=16, k2stack=12 * 16,
    qn_ms=1, qn_r=1, xq=1, xqT_ps=1, xqT_sb=1, qn=1, q2parts=1, q2T_ps=1, q2T_sb=1,
    q2scr=16, q2stack=24 * 16,
    mx=NM, mx_read=NM, mparts=1, mT_ps=1, mT_sb=1, mscr=16, mstack=6 * 16,
    s=NX, sexp=NX, av2=NX // 4, o2_sb=2, nat2=2, nat2_read=2,
    on_var=1, on_rstd=1, on_ms=1, on_r=1, oq=1, oqT_ps=1, oqT_sb=1, y2=1,
    ln2_var=1, ln2_rstd=1, x2=1,
    x2T_ps=1, x2T_sb=1, logits=1, lmax=1, lexp=1, route=1, routeT_ps=1, routeT_sb=1,
    bc=E - 1, xe=E - 1, gu=E, silu=E, hT=E, down=E, ln3_var=1, ln3_rstd=1,
    out_ready=1, out_done=16, out_free=1,
    dve_prep=18, dve_nat=24, dve_ln1=6, dve_ctx=10, dve_q=14, dve_m=4, dve_o=27, dve_route=6, dve_ln3=6,
    act_root=8, dve_setup=39,
)


def at(name, b, k):
    return b * PER[name] + k


class Chain:

    def __init__(self, eng, sem, name, b):
        self.eng, self.sem, self.name, self.b, self.k = eng, sem[name], name, b, 0

    def __call__(self, ins, carrier=None):
        self.k += 1
        ins.then_inc(self.sem, 1)
        self.eng.wait_ge(self.sem, at(self.name, self.b, self.k))
        if carrier is not None:
            self.eng.sem_inc(carrier, 1)

    def end(self):
        assert self.k == PER[self.name], (self.name, self.k)


def build(nc, x, ctx_t, wqA, wqB, wkA, wkB, wv, bqA, bqB, bkA, bkB, bv, sinks, vnull, wo, wob,
          w2q, w2kv, w2o, gamma, beta, gate_w, ffn_g, ffn_u, ffn_d, rope_cos, rope_sin, ident, out):
    ctx = ExitStack()
    with ctx:
        def sb(name, shape, dt=F32):
            return ctx.enter_context(nc.sbuf_tensor(name, shape, dt))

        def bank(name):
            return ctx.enter_context(nc.psum_tensor(name, [P, 512], F32))

        sem = {n: ctx.enter_context(nc.semaphore("s_" + n)) for n in PER}
        weights_in = ctx.enter_context(nc.semaphore("weights_in"))
        pool_setup = ctx.enter_context(nc.semaphore("pool_setup"))
        abs_ready = ctx.enter_context(nc.semaphore("abs_ready"))
        abs_sums = ctx.enter_context(nc.semaphore("abs_sums"))
        ternary = ctx.enter_context(nc.semaphore("ternary"))
        ternary_T = ctx.enter_context(nc.semaphore("ternary_T"))
        setup_done = ctx.enter_context(nc.semaphore("setup_done"))

        identF, identB, identH = sb("identF", [P, P]), sb("identB", [P, P], BF16), sb("identH", [P, P], F16)
        WQA, WQB = sb("WQA", [P, BR * P]), sb("WQB", [P, BR * P])
        WKA, WKB, WV = sb("WKA", [P, P]), sb("WKB", [P, P]), sb("WV", [P, P])
        BQA, BQB = sb("BQA", [P, BR]), sb("BQB", [P, BR])
        BKA, BKB, BV = sb("BKA", [P, 1]), sb("BKB", [P, 1]), sb("BV", [P, P])
        COS, SIN = sb("COS", [P, T]), sb("SIN", [P, T])
        SINKS = sb("SINKS", [P, BR * NH])
        SINKD = sb("SINKD", [P, BR * NH])
        SV = sb("SV", [P, BR * NH, DH])
        PR2_ = sb("PR2", [P, 8 * 512])
        WO = sb("WO", [P, BR, P])
        WOB = PR2_[:, 0:BR * P].rearrange("p (n d) -> p n d", n=BR)
        BMEAN = sb("BMEAN", [P, P])
        W2 = PR2_[:, BR * P:(BR + 3) * P].rearrange("p (n d) -> p n d", n=3)
        W2N = sb("W2N", [P, 3, P], BF16)
        W2T = sb("W2T", [P, 3, P], BF16)
        ABS = sb("ABS", [P, 4])
        WSC, WINV = sb("WSC", [P, 4]), sb("WINV", [P, 4])
        QC = sb("QC", [P, 1])
        GAM, BET = sb("GAM", [P, P]), sb("BET", [P, P])
        GW = sb("GW", [P, 8])
        FG, FU, FD = sb("FG", [P, E, F]), sb("FU", [P, E, F]), sb("FD", [P, E, FC, P])
        ONES = sb("ONES", [P, P])
        HEADS = sb("HEADS", [P, P])
        SEL = sb("SEL", [8, 8, P])
        IOTA8 = sb("IOTA8", [P, TH, 8])
        EPS_LN, EPS_RMS, ONE1 = sb("EPS_LN", [P, 1]), sb("EPS_RMS", [P, 1]), sb("ONE1", [P, 1])

        XIN, CIN = sb("XIN", [P, TH, D]), sb("CIN", [P, NT, D])
        XT, KR, TB, KSQ, KRS = (sb("XT", [P, T]), sb("KR", [P, T]), sb("TB", [P, 2, T]),
                                sb("KSQ", [P, T]), sb("KRS", [P, T]))
        KHL = sb("KHL", [P, 2, T], F16)
        PR2 = PR2_[:].rearrange("p (n t) -> p n t", n=8)
        QR = PR2_[:, 0:TH * BR * P].rearrange("p (h n t) -> p h n t", h=TH, n=BR)
        QRES = PR2_[:, TH * BR * P:2 * TH * BR * P].rearrange("p (h n t) -> p h n t", h=TH, n=BR)
        QABC = PR2_[:, 2 * TH * BR * P:4 * TH * BR * P].bitcast(BF16)[:, 0:3 * TH * BR * P].rearrange(
            "p (i h n t) -> p i h n t", i=3, h=TH, n=BR)
        V1 = sb("V1", [P, TH, NH, DH + 1])
        KS1 = sb("KS1", [P, NH // 2, T], F16)
        QS1 = sb("QS1", [P, NH // 2, TH * BR * P], BF16)
        PRB = sb("PRB", [P, 8, 3, BR, P])
        O1 = sb("O1", [P, 2, 512])
        CTX, CTXT = sb("CTX", [P, TH, BR, P]), O1
        DEN = sb("DEN", [P, 2, 4, 4])
        XB = sb("XB", [P, TH, D])
        RES, _, LST = sb("RES", [P, TH, D]), None, sb("LST", [P, 4, TH])
        X1, X2 = sb("X1", [P, TH, D]), sb("X2", [P, TH, D])
        CQB, CST = sb("CQB", [P, NT, D], BF16), sb("CST", [P, 8, NT])
        CSQ = sb("CSQ", [P, NT, D])
        K32 = CSQ[:].rearrange("p n d -> p (n d)")[:, 0:NT * 64].rearrange("p (n d) -> p n d", d=64)
        KHN = CSQ[:].rearrange("p n d -> p (n d)")[:, NT * 64:].bitcast(F16).rearrange(
            "p (n i d) -> p n i d", i=2, d=64)
        KT2 = sb("KT2", [P, NT * P], F16)
        YT = KT2[:].bitcast(BF16)
        V2 = sb("V2", [P, NT, KV, DH + 1])
        KS2 = sb("KS2", [P, KV // 2, NT * P], F16)
        QST, OST = sb("QST", [P, 8, TH]), sb("OST", [P, 8, TH])
        QSQ = sb("QSQ", [P, TH, D])
        OSQ = QSQ
        QQB, QQT = sb("QQB", [P, TH, D], BF16), sb("QQT", [P, T], BF16)
        OQB, OQT = sb("OQB", [P, TH, D], BF16), sb("OQT", [P, T], BF16)
        Q32 = sb("Q32", [P, TH, D])
        QP = sb("QP", [P, TH, 3, D], BF16)
        QT2 = sb("QT2", [P, 3, T], BF16)
        QS2 = sb("QS2", [P, KV // 2, 2, T], BF16)
        MC, MX = sb("MC", [P, TH, NH, 4]), sb("MX", [P, TH, NH])
        MP, MT = sb("MP", [P, TH, 3, NH], BF16), sb("MT", [48, T], BF16)
        O2 = sb("O2", [P, 512])
        ON = sb("ON", [P, TH, NH, DH])
        X2T = sb("X2T", [P, T])
        LG, LM = sb("LG", [P, 2, TH, 8]), sb("LM", [P, 4, TH])
        CR, CRT = sb("CR", [P, TH, 8]), sb("CRT", [8, T])
        XE, SG, HT = sb("XE", [P, 2, T]), sb("SG", [P, 2, FC * T]), sb("HT", [P, 2, FC * T])
        LST3 = sb("LST3", [P, 4, TH])
        OUT = sb("OUT", [P, TH, D])
        BN, BA = sb("BN", [P, TH, 6]), sb("BA", [P, TH, 2])

        k_scr = nc.dram_tensor("k_scr", (2, P, T), F16).ap()
        q_scr = nc.dram_tensor("q_scr", (3, P, TH * BR * P), BF16).ap()
        k2_scr = nc.dram_tensor("k2_scr", (P, NT * P), F16).ap()
        q2_scr = nc.dram_tensor("q2_scr", (3, P, T), BF16).ap()
        m_scr = nc.dram_tensor("m_scr", (3 * NH, T), BF16).ap()

        Z = [bank(f"Z{i}") for i in range(3)]
        S = [bank(f"S{i}") for i in range(2)]
        M = bank("M")
        ACC = bank("ACC")
        MISC = bank("MISC")

        block = ctx.enter_context(nc.Block())

        def ts(v):
            return slice(v * P, (v + 1) * P)

        def bcast(ap, n):
            return ap.unsqueeze(2).to_broadcast([P, ap.shape[1], n])

        @block.sync
        def _(sp):
            once = [(identF[:], ident), (WQA[:], wqA), (WQB[:], wqB), (WKA[:], wkA), (WKB[:], wkB),
                    (WV[:], wv), (BQA[:], bqA), (BQB[:], bqB), (BKA[:], bkA), (BKB[:], bkB),
                    (BV[:], bv.partition_broadcast(P)), (COS[:], rope_cos), (SIN[:], rope_sin),
                    (SINKS[:], sinks.partition_broadcast(P)),
                    (SV[:].rearrange("p h d -> p (h d)"), vnull.partition_broadcast(P)),
                    (WO[:], wo), (PR2_[:, 0:BR * P], wob.partition_broadcast(P)),
                    (W2[:, 0, :], w2q), (W2[:, 1, :], w2kv), (W2[:, 2, :], w2o),
                    (GAM[:], gamma.partition_broadcast(P)), (BET[:], beta.partition_broadcast(P)),
                    (GW[:], gate_w), (FG[:], ffn_g), (FU[:], ffn_u), (FD[:], ffn_d)]
            assert len(once) == N_WEIGHTS
            for dst, src in once:
                sp.dma_start(dst, src).then_inc(weights_in, 16)
            sp.wait_ge(setup_done, 1)
            sp.sem_inc(sem["out_free"], 1)
            with sp.Fori(0, B) as b:
                sp.dma_start(XIN[:], x[b].rearrange("(h p) d -> p h d", p=P)).then_inc(sem["x_in"], 16)
                sp.dma_start(CIN[:, 0:NT - 1, :], ctx_t[b, 0:(NT - 1) * P, :].rearrange(
                    "(i p) d -> p i d", p=P)).then_inc(sem["ctx_in"], 16)
                sp.dma_start(CIN[0:LAST, NT - 1, :], ctx_t[b, (NT - 1) * P:S2, :]).then_inc(
                    sem["ctx_in"], 16)
                sp.wait_ge(sem["kparts"], at("kparts", b, 1))
                sp.dma_start(k_scr.rearrange("n p t -> p n t"), KHL[:]).then_inc(sem["kscr"], 16)
                sp.wait_ge(sem["kscr"], at("kscr", b, 16))
                for r in range(2):
                    for i in range(6):
                        sp.dma_start(KS1[64 * r + 8 * i:64 * r + 8 * i + 8, :, :],
                                     k_scr[i // 3].rearrange("(n r d) t -> r d n t", r=2, d=DH)[r]
                                     ).then_inc(sem["kstack"], 16)
                sp.wait_ge(sem["qparts"], at("qparts", b, 1))
                sp.dma_start(q_scr.rearrange("n p t -> p n t"),
                             QABC[:].rearrange("p n h b t -> p n (h b t)")).then_inc(sem["qscr"], 16)
                sp.wait_ge(sem["qscr"], at("qscr", b, 16))
                for r in range(2):
                    for i in range(6):
                        sp.dma_start(QS1[64 * r + 8 * i:64 * r + 8 * i + 8, :, :],
                                     q_scr[i % 3].rearrange("(n r d) t -> r d n t", r=2, d=DH)[r]
                                     ).then_inc(sem["qstack"], 16)
                sp.wait_ge(sem["kT_sb"], at("kT_sb", b, 2))
                sp.dma_start(k2_scr, KT2[:]).then_inc(sem["k2scr"], 16)
                sp.wait_ge(sem["k2scr"], at("k2scr", b, 16))
                for r in range(2):
                    for i in range(6):
                        half = k2_scr[64 * (i // 3):64 * (i // 3) + 64, :]
                        sp.dma_start(KS2[64 * r + 8 * i:64 * r + 8 * i + 8, :, :],
                                     half.rearrange("(n r d) t -> r d n t", r=2, d=DH)[r]
                                     ).then_inc(sem["k2stack"], 16)
                sp.wait_ge(sem["q2T_sb"], at("q2T_sb", b, 1))
                sp.dma_start(q2_scr.rearrange("n p t -> p n t"), QT2[:]).then_inc(sem["q2scr"], 16)
                sp.wait_ge(sem["q2scr"], at("q2scr", b, 16))
                for r in range(2):
                    for i in range(6):
                        for g in range(2):
                            sp.dma_start(QS2[64 * r + 8 * i:64 * r + 8 * i + 8, :, g, :],
                                         q2_scr[i % 3].rearrange("(n r g d) t -> r g d n t", r=2, g=2,
                                                                 d=DH)[r, g]
                                         ).then_inc(sem["q2stack"], 16)
                sp.wait_ge(sem["mT_sb"], at("mT_sb", b, 1))
                sp.dma_start(m_scr, MT[:]).then_inc(sem["mscr"], 16)
                sp.wait_ge(sem["mscr"], at("mscr", b, 16))
                for r in range(2):
                    for i in range(3):
                        row = 64 * r + KROWS + i
                        sp.dma_start(QS2[row:row + 1, :, :, :],
                                     m_scr[NH * i:NH * (i + 1), :].rearrange(
                                         "(n r g) t -> r n g t", r=2, g=2)[r:r + 1]
                                     ).then_inc(sem["mstack"], 16)
                sp.wait_ge(sem["out_ready"], at("out_ready", b, 1))
                sp.dma_start(out[b].rearrange("(h p) d -> p h d", p=P), OUT[:]).then_inc(
                    sem["out_done"], 16)
                sp.wait_ge(sem["out_done"], at("out_done", b, 16))
                sp.sem_inc(sem["out_free"], 1)
            sp.wait_ge(sem["out_done"], at("out_done", B - 1, 16))

        @block.gpsimd
        def _(pool):
            pool.memset(ONES[:], 1.0).then_inc(pool_setup, 1)
            pool.memset(HEADS[:], 1.0).then_inc(pool_setup, 1)
            pool.memset(SEL[:], 0.0).then_inc(pool_setup, 1)
            pool.wait_ge(pool_setup, 3)
            hv = HEADS[:].rearrange("p (h d) -> p h d", d=DH)
            pool.affine_select(out=hv, in_=hv, compare_op=ALU.is_ge, fill=0.0, base=0,
                               pattern=[[-DH, NH], [0, DH]], channel_multiplier=1).then_inc(pool_setup, 1)
            pool.wait_ge(pool_setup, 4)
            pool.affine_select(out=hv, in_=hv, compare_op=ALU.is_ge, fill=0.0, base=DH - 1,
                               pattern=[[DH, NH], [0, DH]], channel_multiplier=-1).then_inc(pool_setup, 1)
            pool.affine_select(out=SEL[:], in_=SEL[:], compare_op=ALU.not_equal, fill=1.0, base=0,
                               pattern=[[-1, 8], [0, P]], channel_multiplier=1).then_inc(pool_setup, 1)
            pool.iota(IOTA8[:], pattern=[[0, TH], [-1, 8]], base=8, channel_multiplier=0,
                      allow_small_or_imprecise_dtypes=True).then_inc(pool_setup, 1)
            with pool.Fori(0, B) as b:
                pool.wait_ge(sem["ctx_in"], at("ctx_in", b, 32))
                pool.tensor_tensor(CSQ[:], CIN[:], CIN[:], ALU.mult).then_inc(sem["csq"], 1)
                for h in range(NH):
                    pool.wait_ge(sem["thr"], at("thr", b, BR * (h + 1)))
                    pool.sem_inc(sem["masking"], 1)
                    for j in (0, 2):
                        v = PRB[:, h % 8, j, :, :]
                        i = pool.affine_select(out=v, in_=v, compare_op=ALU.is_ge, fill=0.0, base=0,
                                               pattern=[[0, BR], [1, P]], channel_multiplier=-1)
                    i.then_inc(sem["masked"], 1)

        @block.scalar
        def _(act):
            def rsqrt(b, k, dst, src, scale, bias, ready, done):
                act.wait_ge(sem[ready], at(ready, b, 1))
                act.activation(dst, src, ACT.Ln, bias=bias, scale=scale).then_inc(sem["act_root"], 1)
                act.wait_ge(sem["act_root"], at("act_root", b, k))
                act.activation(dst, dst, ACT.Exp, scale=-0.5).then_inc(sem[done], 1)

            act.wait_ge(setup_done, 1)
            with act.Fori(0, B) as b:
                act.preload_act_table_set("natural_log_exp_and_others")
                act.wait_ge(sem["xT_ps"], at("xT_ps", b, 1))
                act.activation(XT[:], MISC[:, 0:T], ACT.Copy).then_inc(sem["xT_sb"], 1)
                act.wait_ge(sem["knorm_sb"], at("knorm_sb", b, 1))
                act.activation(KRS[:], KSQ[:], ACT.Ln).then_inc(sem["act_root"], 1)
                act.wait_ge(sem["act_root"], at("act_root", b, 1))
                act.activation(KRS[:], KRS[:], ACT.Exp, scale=-0.5).then_inc(sem["krs"], 1)

                rsqrt(b, 2, CST[:, 2, :], CST[:, 1, :], 1.0 / D, EPS_RMS[:], "cn_ms", "cn_r")
                for name, dst, dt in (("yT", YT, BF16), ("kT", KT2, F16)):
                    for c, (t0, t1) in enumerate(((0, 8), (8, NT))):
                        act.wait_ge(sem[name + "_ps"], at(name + "_ps", b, c + 1))
                        act.activation(dst[:, t0 * P:t1 * P],
                                       (MISC, S[1])[c][:].bitcast(dt)[:, 0:(t1 - t0) * P],
                                       ACT.Copy).then_inc(sem[name + "_sb"], 1)

                def z_tile(u):
                    return PRB[:, (u // 3) % 8, u % 3, :, :].rearrange("p b t -> p (b t)")

                def z_exp(u):
                    act.wait_ge(sem["z"], at("z", b, u + 1))
                    act.activation(z_tile(u), Z[u % 3][:], ACT.Exp, scale=ZSCALE).then_inc(sem["zexp"], 1)

                def z_ln(u):
                    act.wait_ge(sem["zcap"], at("zcap", b, u + 1))
                    act.activation(z_tile(u), z_tile(u), ACT.Ln, bias=ONE1[:]).then_inc(sem["zln"], 1)

                for half in range(2):
                    first = half * NZ // 2
                    for u in range(first, first + NZ // 2):
                        z_exp(u)
                        if u > first:
                            z_ln(u - 1)
                    z_ln(first + NZ // 2 - 1)
                    for h in range(8 * half, 8 * half + 8):
                        act.wait_ge(sem["zmax"], at("zmax", b, 3 * h + 3))
                        v = PRB[:, h % 8, :, :, :].rearrange("p j b t -> p (j b t)")
                        act.activation(v, v, ACT.Silu, scale=GATE).then_inc(sem["gated"], 1)
                    act.preload_act_table_set("natural_log_exp_and_others")
                    for g in range(2 * half, 2 * half + 2):
                        act.wait_ge(sem["av1"], at("av1", b, g + 1))
                        if g:
                            act.wait_ge(sem["nat1"], at("nat1", b, 2 * g))
                        act.activation(O1[:, 0, :], ACC[:], ACT.Copy)
                        act.activation(O1[:, 1, :], M[:], ACT.Copy).then_inc(sem["av1_sb"], 1)
                for t in range(TH):
                    act.wait_ge(sem["ctxT_ps"], at("ctxT_ps", b, t + 1))
                    act.activation(CTXT[:, t, :], (MISC, S[1])[t][:], ACT.Copy).then_inc(sem["ctxT_sb"], 1)
                rsqrt(b, 3, LST[:, 3, :], LST[:, 2, :], 1.0, EPS_LN[:], "ln1_var", "ln1_rstd")

                rsqrt(b, 4, QST[:, 2, :], QST[:, 1, :], 1.0 / D, EPS_RMS[:], "qn_ms", "qn_r")
                act.wait_ge(sem["xqT_ps"], at("xqT_ps", b, 1))
                act.activation(QQT[:], MISC[:].bitcast(BF16)[:, 0:T], ACT.Copy).then_inc(sem["xqT_sb"], 1)
                act.wait_ge(sem["q2T_ps"], at("q2T_ps", b, 1))
                act.activation(QT2[:].rearrange("p n t -> p (n t)"), MISC[:].bitcast(BF16)[:, 0:3 * T],
                               ACT.Copy).then_inc(sem["q2T_sb"], 1)
                act.wait_ge(sem["mT_ps"], at("mT_ps", b, 1))
                act.activation(MT[:], MISC[0:3 * NH, :].bitcast(BF16)[:, 0:T], ACT.Copy).then_inc(sem["mT_sb"], 1)
                for u in range(NX):
                    n = P if (u % (NX // 2)) // 4 < NT - 1 else LAST
                    act.wait_ge(sem["s"], at("s", b, u + 1))
                    if u >= 8:
                        act.wait_ge(sem["av2"], at("av2", b, u // 4 - 1))
                    act.activation(PR2[0:n, u % 8, :], S[u % 2][0:n, :], ACT.Exp).then_inc(sem["sexp"], 1)
                    if u in (NX // 2 + 3, NX - 1):
                        act.wait_ge(sem["av2"], at("av2", b, NT if u < NX - 1 else 2 * NT))
                        if u == NX - 1:
                            act.wait_ge(sem["nat2"], at("nat2", b, 1))
                        act.activation(O2[:], ACC[:], ACT.Copy).then_inc(sem["o2_sb"], 1)
                rsqrt(b, 5, OST[:, 2, :], OST[:, 1, :], 1.0, EPS_LN[:], "on_var", "on_rstd")
                rsqrt(b, 6, OST[:, 4, :], OST[:, 3, :], 1.0 / D, EPS_RMS[:], "on_ms", "on_r")
                act.wait_ge(sem["oqT_ps"], at("oqT_ps", b, 1))
                act.activation(OQT[:], MISC[:].bitcast(BF16)[:, 0:T], ACT.Copy).then_inc(sem["oqT_sb"], 1)
                rsqrt(b, 7, LST[:, 3, :], LST[:, 2, :], 1.0, EPS_LN[:], "ln2_var", "ln2_rstd")

                act.wait_ge(sem["x2T_ps"], at("x2T_ps", b, 1))
                act.activation(X2T[:], MISC[:, 0:T], ACT.Copy).then_inc(sem["x2T_sb"], 1)
                act.wait_ge(sem["lmax"], at("lmax", b, 1))
                act.activation(LM[:, 1, :], LM[:, 0, :], ACT.Exp, scale=-1.0).then_inc(sem["lexp"], 1)
                act.wait_ge(sem["routeT_ps"], at("routeT_ps", b, 1))
                act.activation(CRT[:], MISC[0:8, 0:T], ACT.Copy).then_inc(sem["routeT_sb"], 1)
                for e in range(E):
                    act.wait_ge(sem["gu"], at("gu", b, e + 1))
                    if e >= 2:
                        act.wait_ge(sem["hT"], at("hT", b, e - 1))
                    act.activation(SG[:, e % 2, :], Z[e % 2][:], ACT.Silu).then_inc(sem["silu"], 1)
                rsqrt(b, 8, LST3[:, 3, :], LST3[:, 2, :], 1.0, EPS_LN[:], "ln3_var", "ln3_rstd")

        @block.tensor
        def _(pe):
            def transposes(dst, parts, idn):
                for i, src in enumerate(parts):
                    n = src.shape[1]
                    last = pe.transpose(dst[0:n, ts(i)], src, idn)
                return last

            pe.wait_ge(pool_setup, 7)
            pe.wait_ge(abs_ready, 4)
            pe.matmul(MISC[:, 0:4], ONES[:], ABS[:], start=True, stop=True).then_inc(abs_sums, 1)
            pe.wait_ge(ternary, 1)
            transposes(MISC[:].bitcast(BF16), [W2N[:, i, :] for i in range(3)], identB[:]).then_inc(ternary_T, 1)
            pe.wait_ge(setup_done, 1)

            with pe.Fori(0, B) as b:
                pe.wait_ge(sem["x_in"], at("x_in", b, 16))
                transposes(MISC, [XIN[:, t, :] for t in range(TH)], identF[:]).then_inc(sem["xT_ps"], 1)
                pe.wait_ge(sem["xT_sb"], at("xT_sb", b, 1))
                pe.matmul(MISC[:, 0:T], WKA[:], XT[:], start=True, stop=True)
                pe.matmul(MISC[:, T:2 * T], WKB[:], XT[:], start=True, stop=True).then_inc(sem["kproj"], 1)
                for t in range(TH):
                    last = pe.matmul(ACC[:, ts(t)], XT[:, ts(t)], WV[:], start=True, stop=True)
                last.then_inc(sem["vproj"], 1)
                for br in range(BR):
                    if br >= 2:
                        pe.wait_ge(sem["qproj_read"], at("qproj_read", b, br - 1))
                    pe.matmul(Z[br % 2][:, 0:T], WQA[:, ts(br)], XT[:], start=True, stop=True)
                    pe.matmul(Z[br % 2][:, T:2 * T], WQB[:, ts(br)], XT[:], start=True,
                              stop=True).then_inc(sem["qproj"], 1)
                pe.wait_ge(sem["ksq_sb"], at("ksq_sb", b, 1))
                pe.matmul(MISC[:, 0:T], HEADS[:], KSQ[:], start=True, stop=True).then_inc(sem["knorm_ps"], 1)

                pe.wait_ge(sem["yq"], at("yq", b, 1))
                pe.wait_ge(sem["knorm_sb"], at("knorm_sb", b, 1))
                transposes(MISC[:].bitcast(BF16), [CQB[:, i, :] for i in range(8)], identB[:]
                           ).then_inc(sem["yT_ps"], 1)
                transposes(S[1][:].bitcast(BF16), [CQB[:, i, :] for i in range(8, NT)], identB[:]
                           ).then_inc(sem["yT_ps"], 1)
                for c in range(4):
                    dst = (MISC, S[1])[c % 2]
                    if c == 0:
                        pe.wait_ge(sem["yT_sb"], at("yT_sb", b, 2))
                    if c >= 2:
                        pe.wait_ge(sem["kvn_read"], at("kvn_read", b, c - 1))
                    for i in range(4 * c, min(4 * c + 4, NT)):
                        last = pe.matmul(dst[:, ts(i - 4 * c)], YT[:, ts(i)], W2T[:, 1, :],
                                         start=True, stop=True)
                    last.then_inc(sem["kvn"], 1)
                pe.wait_ge(sem["khl"], at("khl", b, 1))
                pe.wait_ge(sem["kvn_read"], at("kvn_read", b, 4))
                transposes(MISC[:].bitcast(F16), [KHN[:, i, :, :].rearrange("p n d -> p (n d)") for i in range(8)],
                           identH[:]).then_inc(sem["kT_ps"], 1)
                transposes(S[1][:].bitcast(F16), [KHN[:, i, :, :].rearrange("p n d -> p (n d)")
                                                  for i in range(8, NT)], identH[:]).then_inc(sem["kT_ps"], 1)

                pe.wait_ge(sem["kstack"], at("kstack", b, PER["kstack"]))
                pe.wait_ge(sem["qstack"], at("qstack", b, PER["qstack"]))
                pe.wait_ge(sem["qproj_read"], at("qproj_read", b, 4))
                pe.wait_ge(sem["v1_ready"], at("v1_ready", b, 1))
                for half in range(2):
                    for u in range(half * NZ // 2, (half + 1) * NZ // 2):
                        h, j = u // 3, u % 3
                        n, r = h // 2, 64 * (h % 2)
                        keys, queries = (0, 0, 1)[j], (0, 1, 1)[j]
                        if u >= 3:
                            pe.wait_ge(sem["zmax"], at("zmax", b, u - 2))
                        pe.matmul(Z[u % 3][:], KS1[r:r + KROWS, n, ts(keys)],
                                  QS1[r:r + KROWS, n, queries * 512:(queries + 1) * 512],
                                  start=True, stop=True).then_inc(sem["z"], 1)
                    for g in range(2 * half, 2 * half + 2):
                        pe.wait_ge(sem["masked"], at("masked", b, 4 * g + 4))
                        if g:
                            pe.wait_ge(sem["av1_sb"], at("av1_sb", b, g))
                        for j in range(3):
                            for h in range(4 * g, 4 * g + 4):
                                c = 32 * (h % 4)
                                last = pe.matmul((ACC, M, M)[j][c:c + DH + 1, :], V1[:, (0, 0, 1)[j], h, :],
                                                 PRB[:, h % 8, j, :, :].rearrange("p b t -> p (b t)"),
                                                 start=j < 2, stop=j != 1)
                        last.then_inc(sem["av1"], 1)
                        pe.wait_ge(sem["av1_sb"], at("av1_sb", b, g + 1))
                        for t in range(TH):
                            if g:
                                pe.wait_ge(sem["nat1_read"], at("nat1_read", b, 2 * g - 1 + t))
                            transposes((MISC, S[1])[t], [O1[:, t, ts(i)] for i in range(BR)], identF[:]
                                       ).then_inc(sem["nat1"], 1)
                for t in range(TH):
                    pe.wait_ge(sem["nat1_read"], at("nat1_read", b, 7 + t))
                    transposes((MISC, S[1])[t], [CTX[:, t, i, :] for i in range(BR)], identF[:]
                               ).then_inc(sem["ctxT_ps"], 1)
                for t in range(TH):
                    pe.wait_ge(sem["ctxT_sb"], at("ctxT_sb", b, t + 1))
                    for i in range(BR):
                        last = pe.matmul(ACC[:, ts(t)], CTXT[:, t, ts(i)], WO[:, i, :],
                                         start=i == 0, stop=i == BR - 1)
                last.then_inc(sem["y1"], 1)

                pe.wait_ge(sem["xq"], at("xq", b, 1))
                transposes(MISC[:].bitcast(BF16), [QQB[:, t, :] for t in range(TH)], identB[:]
                           ).then_inc(sem["xqT_ps"], 1)
                pe.wait_ge(sem["xqT_sb"], at("xqT_sb", b, 1))
                for t in range(TH):
                    last = pe.matmul(S[1][:, ts(t)], QQT[:, ts(t)], W2T[:, 0, :], start=True, stop=True)
                last.then_inc(sem["qn"], 1)
                pe.wait_ge(sem["q2parts"], at("q2parts", b, 1))
                transposes(MISC[:].bitcast(BF16), [QP[:, t, i, :] for i in range(3) for t in range(TH)],
                           identB[:]).then_inc(sem["q2T_ps"], 1)

                pe.wait_ge(sem["k2stack"], at("k2stack", b, PER["k2stack"]))
                pe.wait_ge(sem["q2stack"], at("q2stack", b, PER["q2stack"]))
                for u in range(NM):
                    h, t, c = u // 8, (u // 4) % 2, u % 4
                    n, r, g = h // 4, 64 * ((h // 2) % 2), h % 2
                    first, cols = CHUNKS[c]
                    if u >= 2:
                        pe.wait_ge(sem["mx_read"], at("mx_read", b, u - 1))
                    pe.matmul((M, MISC)[u % 2][:, 0:cols], QS2[r:r + KROWS, n, g, ts(t)],
                              KS2[r:r + KROWS, n, first:first + cols], start=True, stop=True
                              ).then_inc(sem["mx"], 1)
                pe.wait_ge(setup_done, 1)
                pe.wait_ge(sem["mparts"], at("mparts", b, 1))
                transposes(MISC[:].bitcast(BF16), [MP[:, t, :, :].rearrange("p n h -> p (n h)") for t in range(TH)],
                           identB[:]).then_inc(sem["mT_ps"], 1)

                pe.wait_ge(sem["mstack"], at("mstack", b, PER["mstack"]))

                def values(g4):
                    q, i = g4 // NT, g4 % NT
                    n = P if i < NT - 1 else LAST
                    if g4 == NT:
                        pe.wait_ge(sem["o2_sb"], at("o2_sb", b, 1))
                    pe.wait_ge(sem["sexp"], at("sexp", b, 4 * g4 + 4))
                    for c in range(4):
                        last = pe.matmul(ACC[32 * c:32 * c + DH + 1, :], V2[0:n, i, 4 * q + c, :],
                                         PR2[0:n, (4 * g4 + c) % 8, :], start=i == 0, stop=i == NT - 1)
                    last.then_inc(sem["av2"], 1)
                    if i == NT - 1:
                        pe.wait_ge(sem["o2_sb"], at("o2_sb", b, q + 1))
                        if q:
                            pe.wait_ge(sem["nat2_read"], at("nat2_read", b, q))
                        transposes(MISC, [O2[:, ts(k)] for k in range(4)], identF[:]).then_inc(sem["nat2"], 1)

                for g4 in range(2 * NT):
                    q, i = g4 // NT, g4 % NT
                    n = P if i < NT - 1 else LAST
                    for c in range(4):
                        u, kv = 4 * g4 + c, 4 * q + c
                        r = 64 * (kv % 2)
                        if u >= 2:
                            pe.wait_ge(sem["sexp"], at("sexp", b, u - 1))
                        pe.matmul(S[u % 2][0:n, :], KS2[r:r + SROWS, kv // 2, i * P:i * P + n],
                                  QS2[r:r + SROWS, kv // 2, :, :].rearrange("p g t -> p (g t)"),
                                  start=True, stop=True).then_inc(sem["s"], 1)
                    if g4:
                        values(g4 - 1)
                values(2 * NT - 1)

                pe.wait_ge(sem["oq"], at("oq", b, 1))
                transposes(MISC[:].bitcast(BF16), [OQB[:, t, :] for t in range(TH)], identB[:]
                           ).then_inc(sem["oqT_ps"], 1)
                pe.wait_ge(sem["oqT_sb"], at("oqT_sb", b, 1))
                for t in range(TH):
                    last = pe.matmul(S[1][:, ts(t)], OQT[:, ts(t)], W2T[:, 2, :], start=True, stop=True)
                last.then_inc(sem["y2"], 1)

                pe.wait_ge(sem["x2"], at("x2", b, 1))
                transposes(MISC, [X2[:, t, :] for t in range(TH)], identF[:]).then_inc(sem["x2T_ps"], 1)
                pe.wait_ge(sem["x2T_sb"], at("x2T_sb", b, 1))
                for t in range(TH):
                    last = pe.matmul(S[1][:, 8 * t:8 * t + 8], X2T[:, ts(t)], GW[:], start=True, stop=True)
                last.then_inc(sem["logits"], 1)

                def gate_up(e, rhs):
                    if e >= 2:
                        pe.wait_ge(sem["silu"], at("silu", b, e - 1))
                    if e >= 1:
                        pe.wait_ge(sem["hT"], at("hT", b, e))
                    for w, dst in ((FG, Z[e % 2]), (FU, Z[2])):
                        for c in range(FC):
                            last = pe.matmul(dst[:, c * T:(c + 1) * T], w[:, e, ts(c)], rhs,
                                             start=True, stop=True)
                    last.then_inc(sem["gu"], 1)

                def down(e):
                    pe.wait_ge(sem["hT"], at("hT", b, e + 1))
                    for t in range(TH):
                        for c in range(FC):
                            last = pe.matmul(S[0][:, ts(t)], HT[:, e % 2, c * T + t * P:c * T + (t + 1) * P],
                                             FD[:, e, c, :], start=(e == 0 and t == 0 and c == 0),
                                             stop=(e == E - 1 and c == FC - 1), skip_group_check=True)
                    last.then_inc(sem["down"], 1)

                gate_up(0, X2T[:])
                pe.wait_ge(sem["route"], at("route", b, 1))
                for t in range(TH):
                    last = pe.transpose(MISC[0:8, ts(t)], CR[:, t, :], identF[:])
                last.then_inc(sem["routeT_ps"], 1)
                pe.wait_ge(sem["routeT_sb"], at("routeT_sb", b, 1))
                for e in range(1, E + 1):
                    if e < E:
                        if e >= 2:
                            pe.wait_ge(sem["xe"], at("xe", b, e - 1))
                        pe.matmul(MISC[:, 0:T], SEL[:, e - 1, :], CRT[:], start=True, stop=True
                                  ).then_inc(sem["bc"], 1)
                    down(e - 1)
                    if e < E:
                        pe.wait_ge(sem["xe"], at("xe", b, e))
                        gate_up(e, XE[:, e % 2, :])

        @block.vector
        def _(dve):
            dve.wait_ge(weights_in, 16 * N_WEIGHTS)
            dve.wait_ge(pool_setup, 7)
            setup = Chain(dve, sem, "dve_setup", 0)
            for dst, value in ((ABS, 0.0), (EPS_LN, 1e-5), (EPS_RMS, 1e-6), (ONE1, 1.0),
                               (V1, 0.0), (V2, 0.0), (KS2, 1.0), (CIN, 0.0)):
                setup(dve.memset(dst[:], value))
            setup(dve.tensor_copy(identB[:], identF[:]))
            setup(dve.tensor_copy(identH[:], identF[:]))
            for v in (V1, V2):
                setup(dve.memset(v[:, :, :, DH:DH + 1], 1.0))
            for v in (*Z, *S, M, ACC, MISC):
                setup(dve.memset(v[:], 0.0))
            for col, rows, i in ((0, slice(0, P), 0), (1, slice(0, 64), 1), (2, slice(64, P), 1),
                                 (3, slice(0, P), 2)):
                dve.tensor_reduce(out=ABS[rows, col:col + 1], in_=W2[rows, i, :], axis=AX.X,
                                  op=ALU.add, apply_absolute_value=True).then_inc(abs_ready, 1)
            dve.wait_ge(abs_sums, 1)
            for col, n in ((0, P * D), (1, 64 * D), (2, 64 * D), (3, P * D)):
                setup(dve.tensor_scalar(WSC[:, col:col + 1], MISC[:, col:col + 1], 1.0 / n, 1e-5,
                                        ALU.mult, ALU.max))
            setup(dve.reciprocal(WINV[:], WSC[:]))
            for rows, i, col in ((slice(0, P), 0, 0), (slice(0, 64), 1, 1), (slice(64, P), 1, 2),
                                 (slice(0, P), 2, 3)):
                setup(dve.tensor_scalar(W2[rows, i, :], W2[rows, i, :], WINV[rows, col:col + 1], MAGIC,
                                        ALU.mult, ALU.add))
            setup(dve.tensor_scalar(W2, W2, MAGIC, None, ALU.subtract))
            dve.tensor_scalar(W2N[:], W2, -1.0, 1.0, ALU.max, ALU.min).then_inc(ternary, 1)
            setup(dve.tensor_tensor(QC[:], WSC[:, 0:1], WSC[:, 1:2], ALU.mult))
            setup(dve.tensor_scalar(QC[:], QC[:], DH ** -0.5, None, ALU.mult))
            setup(dve.tensor_scalar(SINKS[:], SINKS[:], GATE, None, ALU.mult))
            setup(dve.tensor_scalar(SINKD[:], SINKS[:], GATE * 1e-6, None, ALU.add))
            setup(dve.tensor_tensor(SV[:], SV[:], bcast(SINKS[:], DH), ALU.mult))
            setup(dve.tensor_tensor(BMEAN[:], WOB[:, 0, :], WOB[:, 1, :], ALU.add))
            setup(dve.tensor_tensor(BMEAN[:], BMEAN[:], WOB[:, 2, :], ALU.add))
            setup(dve.tensor_tensor(BMEAN[:], BMEAN[:], WOB[:, 3, :], ALU.add))
            setup(dve.tensor_scalar(BMEAN[:], BMEAN[:], 1.0 / BR, None, ALU.mult))
            dve.wait_ge(ternary_T, 1)
            dve.tensor_copy(W2T[:].rearrange("p n d -> p (n d)"), MISC[:].bitcast(BF16)[:, 0:3 * P]
                            ).then_inc(setup_done, 1)
            setup.end()

            def layer_norm(b, link, src, stats, dst, var_ready, rstd_ready, done):
                for t in range(TH):
                    link(dve.bn_stats(BN[:, t, :], src[:, t, :]), carrier=sem["bn_steps"])
                for t in range(TH):
                    link(dve.bn_aggr(BA[:, t, :], BN[:, t, :]), carrier=sem["bn_steps"])
                dve.tensor_copy(stats[:, 2, :], BA[:, :, 1]).then_inc(sem[var_ready], 1)
                dve.wait_ge(sem[rstd_ready], at(rstd_ready, b, 1))
                for t in range(TH):
                    last = dve.tensor_scalar(dst[:, t, :], src[:, t, :], BA[:, t, 0:1], stats[:, 3, t:t + 1],
                                             ALU.subtract, ALU.mult)
                    if t < TH - 1:
                        link(last)
                last.then_inc(sem[done], 1)

            def mean_square(link, src, stats, ready):
                link(dve.tensor_reduce(out=stats[:, 0, :], in_=src[:], axis=AX.X, op=ALU.max,
                                       apply_absolute_value=True))
                link(dve.tensor_tensor(QSQ[:], src[:], src[:], ALU.mult))
                dve.tensor_reduce(out=stats[:, 1, :], in_=QSQ[:], axis=AX.X, op=ALU.add).then_inc(sem[ready], 1)

            def quant_scales(link, stats, root):
                link(dve.tensor_tensor(stats[:, 5, :], stats[:, 0, :], stats[:, root, :], ALU.mult))
                link(dve.tensor_scalar(stats[:, 5, :], stats[:, 5, :], 1e-5, None, ALU.max))
                link(dve.reciprocal(stats[:, 6, :], stats[:, 5, :]))
                link(dve.tensor_tensor(stats[:, 6, :], stats[:, 6, :], stats[:, root, :], ALU.mult))
                link(dve.tensor_scalar(stats[:, 6, :], stats[:, 6, :], 127.0, None, ALU.mult))
                link(dve.tensor_scalar(stats[:, 7, :], stats[:, 5, :], 1.0 / 127.0, None, ALU.mult))

            with dve.Fori(0, B) as b:
                link = Chain(dve, sem, "dve_prep", b)
                dve.wait_ge(sem["x_in"], at("x_in", b, 16))
                for t in range(TH):
                    last = dve.tensor_tensor(XB[:, t, :], XIN[:, t, :], BMEAN[:], ALU.add)
                    link(last)

                def rope(psum, bias_a, bias_b, dst, done):
                    link(dve.scalar_tensor_tensor(out=TB[:, 0, :], in0=psum[:, 0:T], scalar=bias_a, in1=COS[:],
                                                  op0=ALU.add, op1=ALU.mult))
                    link(dve.scalar_tensor_tensor(out=TB[:, 1, :], in0=psum[:, T:2 * T], scalar=bias_b,
                                                  in1=SIN[:], op0=ALU.add, op1=ALU.mult))
                    ins = dve.tensor_tensor(dst, TB[:, 0, :] if dst.ndim == 2 else
                                            TB[:, 0, :].rearrange("p (h t) -> p h t", h=TH),
                                            TB[:, 1, :] if dst.ndim == 2 else
                                            TB[:, 1, :].rearrange("p (h t) -> p h t", h=TH), ALU.add)
                    if done:
                        ins.then_inc(sem[done], 1)
                    else:
                        link(ins)

                dve.wait_ge(sem["kproj"], at("kproj", b, 1))
                rope(MISC, BKA[:], BKB[:], KR[:], None)
                dve.tensor_tensor(KSQ[:], KR[:], KR[:], ALU.mult).then_inc(sem["ksq_sb"], 1)
                dve.wait_ge(sem["vproj"], at("vproj", b, 1))
                for t in range(TH):
                    last = dve.tensor_tensor(V1[:, t, :, 0:DH],
                                             ACC[:, ts(t)].rearrange("p (h d) -> p h d", d=DH),
                                             BV[:].rearrange("p (h d) -> p h d", d=DH), ALU.add)
                last.then_inc(sem["v1_ready"], 1)
                for br in range(BR):
                    dve.wait_ge(sem["qproj"], at("qproj", b, br + 1))
                    rope(Z[br % 2], BQA[:, br:br + 1], BQB[:, br:br + 1], QR[:, :, br, :], "qproj_read")
                    dve.wait_ge(sem["qproj_read"], at("qproj_read", b, br + 1))
                dve.wait_ge(sem["knorm_ps"], at("knorm_ps", b, 1))
                dve.tensor_scalar(KSQ[:], MISC[:, 0:T], 1e-6, None, ALU.max).then_inc(sem["knorm_sb"], 1)
                dve.wait_ge(sem["krs"], at("krs", b, 1))
                link(dve.scalar_tensor_tensor(out=TB[:, 0, :], in0=KR[:], scalar=KGAIN, in1=KRS[:],
                                              op0=ALU.mult, op1=ALU.mult))
                link(dve.tensor_copy(KHL[:, 0, :], TB[:, 0, :]))
                dve.tensor_tensor(KHL[:, 1, :], TB[:, 0, :], KHL[:, 0, :], ALU.subtract).then_inc(sem["kparts"], 1)
                link(dve.tensor_copy(QABC[:, 0], QR[:]))
                link(dve.tensor_tensor(QRES[:], QR[:], QABC[:, 0], ALU.subtract))
                link(dve.tensor_copy(QABC[:, 1], QRES[:]))
                dve.tensor_tensor(QABC[:, 2], QRES[:], QABC[:, 1], ALU.subtract).then_inc(sem["qparts"], 1)
                link.end()

                link = Chain(dve, sem, "dve_ctx", b)
                dve.wait_ge(sem["ctx_in"], at("ctx_in", b, 32))
                link(dve.tensor_reduce(out=CST[:, 0, :], in_=CIN[:], axis=AX.X, op=ALU.max,
                                       apply_absolute_value=True))
                dve.wait_ge(sem["csq"], at("csq", b, 1))
                dve.tensor_reduce(out=CST[:, 1, :], in_=CSQ[:], axis=AX.X, op=ALU.add).then_inc(sem["cn_ms"], 1)
                dve.wait_ge(sem["cn_r"], at("cn_r", b, 1))
                quant_scales(link, CST, 2)
                link(dve.tensor_scalar(CST[:, 4, :], CST[:, 7, :], WSC[:, 2:3], None, ALU.mult))
                link(dve.tensor_tensor(CIN[:], CIN[:], bcast(CST[:, 6, :], D), ALU.mult))
                dve.tensor_scalar(CQB[:], CIN[:], MAGIC, MAGIC, ALU.add, ALU.subtract).then_inc(sem["yq"], 1)
                for c in range(4):
                    i0, i1 = 4 * c, min(4 * c + 4, NT)
                    n = i1 - i0
                    src = (MISC, S[1])[c % 2][:, 0:n * P].rearrange("p (n d) -> p n d", d=P)
                    dve.wait_ge(sem["kvn"], at("kvn", b, c + 1))
                    dve.tensor_tensor(K32[:, i0:i1, :], src[:, :, 0:64], bcast(CST[:, 7, i0:i1], 64), ALU.mult)
                    dve.tensor_tensor(V2[:, i0:i1, :, 0:DH],
                                      src[:, :, 64:P].rearrange("p n (h d) -> p n h d", d=DH),
                                      CST[:, 4, i0:i1].unsqueeze(2).unsqueeze(3).to_broadcast(
                                          [P, n, KV, DH]), ALU.mult).then_inc(sem["kvn_read"], 1)
                dve.wait_ge(sem["kvn_read"], at("kvn_read", b, 4))
                link(dve.tensor_copy(KHN[:, :, 0, :], K32[:]))
                dve.tensor_tensor(KHN[:, :, 1, :], K32[:], KHN[:, :, 0, :], ALU.subtract).then_inc(sem["khl"], 1)
                link.end()

                def z_tile(u):
                    return PRB[:, (u // 3) % 8, u % 3, :, :].rearrange("p b t -> p (b t)")

                def z_cap(u):
                    dve.wait_ge(sem["zexp"], at("zexp", b, u + 1))
                    dve.tensor_scalar(z_tile(u), z_tile(u), CAP, None, ALU.min).then_inc(sem["zcap"], 1)

                def z_max(u):
                    dve.wait_ge(sem["zln"], at("zln", b, u + 1))
                    dve.scalar_tensor_tensor(out=z_tile(u), in0=Z[u % 3][:], scalar=ZSCALE, in1=z_tile(u),
                                             op0=ALU.mult, op1=ALU.max).then_inc(sem["zmax"], 1)

                link = Chain(dve, sem, "dve_nat", b)
                for half in range(2):
                    first = half * NZ // 2
                    for u in range(first, first + NZ // 2):
                        z_cap(u)
                        if u > first:
                            z_max(u - 1)
                    z_max(first + NZ // 2 - 1)
                    for h in range(8 * half, 8 * half + 8):
                        dve.wait_ge(sem["gated"], at("gated", b, h + 1))
                        for br in range(BR):
                            v = PRB[:, h % 8, :, br, :]
                            dve.scalar_tensor_tensor(out=v, in0=v, scalar=SINKS[:, NH * br + h:NH * br + h + 1],
                                                     in1=v, op0=ALU.is_ge, op1=ALU.mult).then_inc(sem["thr"], 1)
                    for g in range(2 * half, 2 * half + 2):
                        for t in range(TH):
                            dve.wait_ge(sem["nat1"], at("nat1", b, 2 * g + t + 1))
                            src = (MISC, S[1])[t][:].rearrange("p (n h c) -> p n h c", n=BR, c=32)
                            sink = SINKD[:].rearrange("p (n h) -> p n h", n=BR)[:, :, 4 * g:4 * g + 4]
                            null = SV[:].rearrange("p (n h) d -> p n h d", n=BR)[:, :, 4 * g:4 * g + 4, :]
                            dst = CTX[:, t, :, :].rearrange("p n (h d) -> p n h d", d=DH)[:, :, 4 * g:4 * g + 4, :]
                            link(dve.tensor_tensor(DEN[:, t], src[:, :, :, DH], sink, ALU.add))
                            link(dve.reciprocal(DEN[:, t], DEN[:, t]))
                            link(dve.tensor_tensor(dst, src[:, :, :, 0:DH], null, ALU.add))
                            dve.tensor_tensor(dst, dst, DEN[:, t].unsqueeze(3).to_broadcast([P, BR, 4, DH]),
                                              ALU.mult).then_inc(sem["nat1_read"], 1)
                link.end()
                link = Chain(dve, sem, "dve_ln1", b)
                dve.wait_ge(sem["y1"], at("y1", b, 1))
                link(dve.scalar_tensor_tensor(out=RES[:].rearrange("p h d -> p (h d)"), in0=ACC[:, 0:T],
                                              scalar=1.0 / BR, in1=XB[:].rearrange("p h d -> p (h d)"),
                                              op0=ALU.mult, op1=ALU.add))
                layer_norm(b, link, RES, LST, X1, "ln1_var", "ln1_rstd", "x1")
                dve.wait_ge(sem["x1"], at("x1", b, 1))
                link.end()

                link = Chain(dve, sem, "dve_q", b)
                mean_square(link, X1, QST, "qn_ms")
                dve.wait_ge(sem["qn_r"], at("qn_r", b, 1))
                quant_scales(link, QST, 2)
                link(dve.tensor_scalar(QST[:, 7, :], QST[:, 7, :], QC[:], None, ALU.mult))
                link(dve.tensor_tensor(QSQ[:], X1[:], bcast(QST[:, 6, :], D), ALU.mult))
                dve.tensor_scalar(QQB[:], QSQ[:], MAGIC, MAGIC, ALU.add, ALU.subtract).then_inc(sem["xq"], 1)
                dve.wait_ge(sem["qn"], at("qn", b, 1))
                link(dve.tensor_tensor(Q32[:], S[1][:, 0:T].rearrange("p (h d) -> p h d", d=D),
                                       bcast(QST[:, 7, :], D), ALU.mult))
                link(dve.tensor_copy(QP[:, :, 0, :], Q32[:]))
                link(dve.tensor_tensor(Q32[:], Q32[:], QP[:, :, 0, :], ALU.subtract))
                link(dve.tensor_copy(QP[:, :, 1, :], Q32[:]))
                dve.tensor_tensor(QP[:, :, 2, :], Q32[:], QP[:, :, 1, :], ALU.subtract).then_inc(sem["q2parts"], 1)
                link.end()

                link = Chain(dve, sem, "dve_m", b)
                for u in range(NM):
                    h, t, c = u // 8, (u // 4) % 2, u % 4
                    dve.wait_ge(sem["mx"], at("mx", b, u + 1))
                    dve.tensor_reduce(out=MC[:, t, h, c:c + 1], in_=(M, MISC)[u % 2][:, 0:CHUNKS[c][1]],
                                      axis=AX.X, op=ALU.max).then_inc(sem["mx_read"], 1)
                dve.wait_ge(sem["mx_read"], at("mx_read", b, NM))
                link(dve.tensor_reduce(out=MX[:], in_=MC[:], axis=AX.X, op=ALU.max, negate=True))
                link(dve.tensor_copy(MP[:, :, 0, :], MX[:]))
                link(dve.tensor_tensor(MX[:], MX[:], MP[:, :, 0, :], ALU.subtract))
                link(dve.tensor_copy(MP[:, :, 1, :], MX[:]))
                dve.tensor_tensor(MP[:, :, 2, :], MX[:], MP[:, :, 1, :], ALU.subtract).then_inc(sem["mparts"], 1)
                link.end()

                link = Chain(dve, sem, "dve_o", b)
                for q in range(2):
                    dve.wait_ge(sem["nat2"], at("nat2", b, q + 1))
                    src = MISC[:].rearrange("p (g h k c) -> p g h k c", g=2, h=TH, c=32)
                    link(dve.reciprocal(DEN[:].rearrange("p a b c -> p (a b c)")[:, 0:16],
                                        MISC[:].rearrange("p (k c) -> p k c", c=32)[:, :, DH]))
                    for g in range(2):
                        den = DEN[:].rearrange("p a b c -> p (a b c)")[:, 8 * g:8 * g + 8].rearrange(
                            "p (h k) -> p h k", h=TH)
                        last = dve.tensor_tensor(ON[:, :, 8 * q + g:8 * q + g + 7:2, :], src[:, g, :, :, 0:DH],
                                                 den.unsqueeze(3).to_broadcast([P, TH, 4, DH]), ALU.mult)
                        if g:
                            last.then_inc(sem["nat2_read"], 1)
                    dve.wait_ge(sem["nat2_read"], at("nat2_read", b, q + 1))
                on = ON[:].rearrange("p h n d -> p h (n d)")
                for t in range(TH):
                    link(dve.bn_stats(BN[:, t, :], on[:, t, :]), carrier=sem["bn_steps"])
                for t in range(TH):
                    link(dve.bn_aggr(BA[:, t, :], BN[:, t, :]), carrier=sem["bn_steps"])
                dve.tensor_copy(OST[:, 1, :], BA[:, :, 1]).then_inc(sem["on_var"], 1)
                dve.wait_ge(sem["on_rstd"], at("on_rstd", b, 1))
                for t in range(TH):
                    link(dve.tensor_scalar(on[:, t, :], on[:, t, :], BA[:, t, 0:1], OST[:, 2, t:t + 1],
                                           ALU.subtract, ALU.mult))
                link(dve.tensor_tensor(on, on, GAM[:].unsqueeze(1).to_broadcast([P, TH, D]), ALU.mult))
                link(dve.tensor_tensor(on, on, BET[:].unsqueeze(1).to_broadcast([P, TH, D]), ALU.add))
                link(dve.tensor_reduce(out=OST[:, 0, :], in_=on, axis=AX.X, op=ALU.max,
                                       apply_absolute_value=True))
                link(dve.tensor_tensor(OSQ[:], on, on, ALU.mult))
                dve.tensor_reduce(out=OST[:, 3, :], in_=OSQ[:], axis=AX.X, op=ALU.add).then_inc(sem["on_ms"], 1)
                dve.wait_ge(sem["on_r"], at("on_r", b, 1))
                quant_scales(link, OST, 4)
                link(dve.tensor_scalar(OST[:, 7, :], OST[:, 7, :], WSC[:, 3:4], None, ALU.mult))
                link(dve.tensor_tensor(OSQ[:], on, bcast(OST[:, 6, :], D), ALU.mult))
                dve.tensor_scalar(OQB[:], OSQ[:], MAGIC, MAGIC, ALU.add, ALU.subtract).then_inc(sem["oq"], 1)
                dve.wait_ge(sem["y2"], at("y2", b, 1))
                link(dve.tensor_tensor(RES[:], S[1][:, 0:T].rearrange("p (h d) -> p h d", d=D),
                                       bcast(OST[:, 7, :], D), ALU.mult))
                link(dve.tensor_tensor(RES[:], RES[:], X1[:], ALU.add))
                layer_norm(b, link, RES, LST, X2, "ln2_var", "ln2_rstd", "x2")
                link.end()

                link = Chain(dve, sem, "dve_route", b)
                dve.wait_ge(sem["logits"], at("logits", b, 1))
                lg = S[1][:, 0:8 * TH].rearrange("p (h e) -> p h e", e=8)
                dve.tensor_reduce(out=LM[:, 0, :], in_=lg, axis=AX.X, op=ALU.max).then_inc(sem["lmax"], 1)
                dve.wait_ge(sem["lmax"], at("lmax", b, 1))
                link(dve.tensor_tensor(LG[:, 0], lg, bcast(LM[:, 0, :], 8), ALU.is_equal))
                link(dve.tensor_tensor(LG[:, 0], LG[:, 0], IOTA8[:], ALU.mult))
                link(dve.tensor_reduce(out=LM[:, 2, :], in_=LG[:, 0], axis=AX.X, op=ALU.max))
                link(dve.tensor_tensor(LG[:, 1], IOTA8[:], bcast(LM[:, 2, :], 8), ALU.is_equal))
                dve.wait_ge(sem["lexp"], at("lexp", b, 1))
                link(dve.tensor_scalar(LM[:, 3, :], LM[:, 1, :], 1.0, None, ALU.add))
                link(dve.reciprocal(LM[:, 3, :], LM[:, 3, :]))
                dve.tensor_tensor(CR[:], LG[:, 1], bcast(LM[:, 3, :], 8), ALU.mult).then_inc(sem["route"], 1)
                link.end()

                def hidden(e):
                    dve.wait_ge(sem["silu"], at("silu", b, e + 1))
                    if e >= 2:
                        dve.wait_ge(sem["down"], at("down", b, e - 1))
                    dve.tensor_tensor(HT[:, e % 2, :], Z[2][:], SG[:, e % 2, :], ALU.mult).then_inc(sem["hT"], 1)

                hidden(0)
                for e in range(1, E):
                    dve.wait_ge(sem["bc"], at("bc", b, e))
                    if e >= 3:
                        dve.wait_ge(sem["gu"], at("gu", b, e - 1))
                    dve.tensor_tensor(XE[:, e % 2, :], MISC[:, 0:T], X2T[:], ALU.mult).then_inc(sem["xe"], 1)
                    hidden(e)
                link = Chain(dve, sem, "dve_ln3", b)
                dve.wait_ge(sem["down"], at("down", b, E))
                link(dve.tensor_tensor(RES[:].rearrange("p h d -> p (h d)"), S[0][:, 0:T],
                                       X2[:].rearrange("p h d -> p (h d)"), ALU.add))
                dve.wait_ge(sem["out_free"], at("out_free", b, 1))
                layer_norm(b, link, RES, LST3, OUT, "ln3_var", "ln3_rstd", "out_ready")
                link.end()


def _layout(inputs):
    f = {k: np.ascontiguousarray(np.asarray(v)) for k, v in inputs.items()}
    perm_a = np.concatenate([np.arange(0, DH, 2), np.arange(1, DH, 2)])
    perm_b = np.concatenate([np.arange(1, DH, 2), np.arange(0, DH, 2)])

    def cols(w, perm):
        return w.reshape(w.shape[:-1] + (-1, DH))[..., perm].reshape(w.shape)

    wq, bq, wk, bk = (f["L0_attn_" + n] for n in ("W_Q", "b_Q", "W_K", "b_K"))
    inv_freq = (1.0 / 10000.0 ** (np.arange(0, DH, 2, dtype=np.float32) / DH)).astype(np.float32)
    angle = (np.arange(T, dtype=np.float32)[:, None] * inv_freq[None, :]).astype(np.float32)
    cos, sin = np.cos(angle).T, np.sin(angle).T
    rope_cos = np.tile(np.concatenate([cos, cos]), (NH, 1)).astype(np.float32)
    rope_sin = np.tile(np.concatenate([-sin, sin]), (NH, 1)).astype(np.float32)

    def experts(shared, routed):
        return np.concatenate([shared[None], routed])

    g, u = (experts(f["L0_ffn_shared_" + n], f["L0_ffn_r_" + n]) for n in ("gate", "up"))
    dn = experts(f["L0_ffn_shared_down"], f["L0_ffn_r_down"])
    return dict(
        x=f["x"], ctx_t=f["ctx_1024"],
        wqA=cols(wq, perm_a), wqB=cols(wq, perm_b), wkA=cols(wk, perm_a), wkB=cols(wk, perm_b),
        wv=f["L0_attn_W_V"],
        bqA=cols(bq, perm_a).reshape(BR, P).T, bqB=cols(bq, perm_b).reshape(BR, P).T,
        bkA=cols(bk, perm_a).reshape(P, 1), bkB=cols(bk, perm_b).reshape(P, 1),
        bv=f["L0_attn_b_V"], sinks=f["L0_attn_sink_scalars"], vnull=f["L0_attn_v_nulls"].reshape(-1),
        wo=f["L0_attn_W_O"].transpose(1, 0, 2), wob=f["L0_attn_W_O_bias"].reshape(-1),
        w2q=f["L0_xattn_wq"], w2kv=np.concatenate([f["L0_xattn_wk"], f["L0_xattn_wv"]]),
        w2o=f["L0_xattn_wo"], gamma=f["L0_xattn_ln_gamma"], beta=f["L0_xattn_ln_beta"],
        gate_w=f["L0_ffn_gate_w"].T,
        ffn_g=g.transpose(2, 0, 1), ffn_u=u.transpose(2, 0, 1),
        ffn_d=dn.reshape(E, D, FC, P).transpose(3, 0, 2, 1),
        rope_cos=rope_cos, rope_sin=rope_sin, ident=np.eye(P, dtype=np.float32),
    )


def kernel(**inputs):
    import concourse.bacc as _bacc
    from concourse.bass_utils import run_bass_kernel_spmd as _run

    nc = _bacc.Bacc("TRN2", target_bir_lowering=False, num_devices=1, dynamic_dma_scratch_size=1024)
    arrays, args = {}, {}
    for name, a in _layout(inputs).items():
        a = np.ascontiguousarray(a)
        arrays["in_" + name] = a
        args[name] = nc.dram_tensor("in_" + name, a.shape, mybir.dt.from_np(a.dtype), kind="ExternalInput").ap()
    args["out"] = nc.dram_tensor("out_0", (B, T, D), F32, kind="ExternalOutput").ap()
    build(nc, **args)
    r = _run(nc, [arrays], core_ids=[0])
    return r.results[0]["out_0"]
```

```python
from contextlib import ExitStack
import math

import numpy as np

import concourse.bass as bass
from concourse import mybir

F32 = mybir.dt.float32
F16 = mybir.dt.float16
BF16 = mybir.dt.bfloat16
ALU = mybir.AluOpType
ACT = mybir.ActivationFunctionType
AX = mybir.AxisListType

P = 128
D = 128
B = 8
T = 256
TH = T // P
BR = 4
NH = 16
DH = 8
KV = 8
S2 = 1601
NT = 13
LAST = S2 - (NT - 1) * P
E = 9
F = 256
FC = F // P
CAP = 2.0 ** 60
POOL_HEADS = 12
LOWEST = -3.0e38
MAGIC = 1.5 * 2.0 ** 23
GATE = math.pi / math.sqrt(3.0)
KGAIN = 16.0
ZSCALE = DH ** -0.5 / KGAIN
MCOLS = 401
CHUNKS = (0, 400, 800, 1200)
assert CHUNKS[-1] + MCOLS == S2
KROWS = 6 * DH
M_ROW = 32
KEY_ROWS = ((0, 3, 0), (1, 1, 24), (1, 2, 35))
QUERY_ROWS = ((slice(0, 3), 0), (slice(0, 1), 24), (slice(1, 3), 35))
PREP_AT = {u: k for k, u in enumerate((0, 2, 4, 10, 16, 22, 28, 32, 36, 44, 46, 50, 54, 60, 64, 72, 76))}
PREP_STEPS = len(PREP_AT)
FIRST_HALF = 13
EXPERT_EVERY = 12
FFN_STEPS = EXPERT_EVERY * 8 + 20
EXPERT_AT = dict(weight=0, inputs=2, gate=4, up=6, silu=7, hidden=9, down0=11, down1=13)
NZ = 3 * NH
NX = KV * NT
NM = NH * TH * len(CHUNKS)
N_WEIGHTS = 27

PER = dict(
    x_in=16, ctx_in=32,
    xT_ps=1, xT_sb=1, kproj=1, vproj=1, qproj=4, qproj_read=4, v1_ready=1,
    ksq_sb=1, knorm_ps=1, knorm_sb=1, krs=1, kparts=1, kscr=16, kstack=4 * 16,
    qparts=1, qscr=16, qstack=4 * 16,
    z=NZ, zexp=NZ, zcap=NZ, zln=NZ, zmax=NZ, gated=NH, masking=NH + POOL_HEADS, bn_steps=16, thr=BR * NH - POOL_HEADS, thr_pool=2 * POOL_HEADS, masked=NH,
    av1=4, av1_sb=4, nat1=8, nat1_read=8, ctxT_ps=2, ctxT_sb=2, y1=1,
    ln1_var=1, ln1_rstd=1, x1=1,
    csq=1, cn_ms=1, cn_r=1, yq=1, yT_ps=2, yT_sb=2, kvn=4, kvn_read=4, khl=1, kT_ps=2, kT_sb=2,
    k2scr=16, k2stack=6 * 16,
    qn_ms=1, qn_r=1, xq=1, xqT_ps=1, xqT_sb=1, qn=1, q2parts=1, q2T_ps=1, q2T_sb=1,
    q2scr=16, q2stack=6 * 16,
    mx=NM, mx_copy=NM // 2, mx_read=NM // 2, mparts=1, mT_ps=1, mT_sb=1, mscr=16, mstack=2 * 16,
    s=NX, sexp=NX, av2=NX // 4, o2_sb=2, nat2=2, nat2_read=2,
    on_var=1, on_rstd=1, on_ms=1, on_r=1, oq=1, oqT_ps=1, oqT_sb=1, y2=1,
    ln2_var=1, ln2_rstd=1, x2=1,
    x2T_ps=1, x2T_sb=1, logits=1, lmax=1, lexp=1, route=1, lg_sb=1, v2_ready=1, mzero=2, mx_head=NH,
    bc=E - 1, xe=E - 1, g=E, up=E, silu=E, hT=E, down=E, ln3_var=1, ln3_rstd=1,
    out_ready=1, out_done=16, out_free=1,
    dve_prep=18, dve_nat=24, dve_ln1=6, dve_ctx=10, dve_q=14, dve_m=3, dve_o=27, dve_route=6, dve_ln3=6,
    act_root=5, prep_root=2, ffn_root=1, dve_setup=44,
)


def at(name, b, k):
    return b * PER[name] + k


def expert(k, stage):
    e, rest = divmod(k - EXPERT_AT[stage], EXPERT_EVERY)
    return e if rest == 0 and 0 <= e < E else None


class Chain:

    def __init__(self, eng, sem, name, b):
        self.eng, self.sem, self.name, self.b, self.k = eng, sem[name], name, b, 0

    def __call__(self, ins, carrier=None):
        self.k += 1
        ins.then_inc(self.sem, 1)
        self.eng.wait_ge(self.sem, at(self.name, self.b, self.k))
        if carrier is not None:
            self.eng.sem_inc(carrier, 1)

    def end(self):
        assert self.k == PER[self.name], (self.name, self.k)


def build(nc, x, ctx_t, wqA, wqB, wkA, wkB, wv, bqA, bqB, bkA, bkB, bv, sinks, vnull, wo, wob,
          w2q, w2kv, w2o, gamma, beta, gate_w, ffn_g, ffn_u, ffn_d, rope_cos, rope_sin, heads, ident, out):
    ctx = ExitStack()
    with ctx:
        def sb(name, shape, dt=F32):
            return ctx.enter_context(nc.sbuf_tensor(name, shape, dt))

        def bank(name):
            return ctx.enter_context(nc.psum_tensor(name, [P, 512], F32))

        sem = {n: ctx.enter_context(nc.semaphore("s_" + n)) for n in PER}
        weights_in = ctx.enter_context(nc.semaphore("weights_in"))
        pool_setup = ctx.enter_context(nc.semaphore("pool_setup"))
        abs_ready = ctx.enter_context(nc.semaphore("abs_ready"))
        abs_sums = ctx.enter_context(nc.semaphore("abs_sums"))
        ternary = ctx.enter_context(nc.semaphore("ternary"))
        ternary_T = ctx.enter_context(nc.semaphore("ternary_T"))
        setup_done = ctx.enter_context(nc.semaphore("setup_done"))

        identF, identB, identH = sb("identF", [P, P]), sb("identB", [P, P], BF16), sb("identH", [P, P], F16)
        WQA, WQB = sb("WQA", [P, BR * P]), sb("WQB", [P, BR * P])
        WKA, WKB, WV = sb("WKA", [P, P]), sb("WKB", [P, P]), sb("WV", [P, P])
        BQA, BQB = sb("BQA", [P, BR]), sb("BQB", [P, BR])
        BKA, BKB, BV = sb("BKA", [P, 1]), sb("BKB", [P, 1]), sb("BV", [P, P])
        COS, SIN = sb("COS", [P, T]), sb("SIN", [P, T])
        SINKS = sb("SINKS", [P, BR * NH])
        SINKD = sb("SINKD", [P, BR * NH])
        SV = sb("SV", [P, BR * NH, DH])
        PR2_ = sb("PR2", [P, 8 * 512])
        WO = sb("WO", [P, BR, P])
        WOB = PR2_[:, 0:BR * P].rearrange("p (n d) -> p n d", n=BR)
        BMEAN = sb("BMEAN", [P, P])
        W2 = PR2_[:, BR * P:(BR + 3) * P].rearrange("p (n d) -> p n d", n=3)
        W2N = sb("W2N", [P, 3, P], BF16)
        W2T = sb("W2T", [P, 3, P], BF16)
        ABS = sb("ABS", [P, 4])
        WSC, WINV = sb("WSC", [P, 4]), sb("WINV", [P, 4])
        QC = sb("QC", [P, 1])
        GAM, BET = sb("GAM", [P, P]), sb("BET", [P, P])
        GW = sb("GW", [P, 8])
        FG, FU, FD = sb("FG", [P, E, F]), sb("FU", [P, E, F]), sb("FD", [P, E, FC, P])
        ONES = sb("ONES", [P, P])
        HEADS = sb("HEADS", [P, P])
        IOTA8 = sb("IOTA8", [P, TH, 8])
        EPS_LN, EPS_RMS, ONE1 = sb("EPS_LN", [P, 1]), sb("EPS_RMS", [P, 1]), sb("ONE1", [P, 1])

        XIN, CIN = sb("XIN", [P, TH, D]), sb("CIN", [P, NT, D])
        XT, KR, TB, KSQ, KRS = (sb("XT", [P, T]), sb("KR", [P, T]), sb("TB", [P, 2, T]),
                                sb("KSQ", [P, T]), sb("KRS", [P, T]))
        KHL = sb("KHL", [P, 2, T], F16)
        PR2 = PR2_[:].rearrange("p (n t) -> p n t", n=8)
        CTX = PR2_[:, 0:1024].rearrange("p (h n t) -> p h n t", h=TH, n=BR)
        O1 = PR2_[:, 1024:2048].rearrange("p (h t) -> p h t", h=TH)
        CTXT = O1
        XE = PR2_[:, 0:512].rearrange("p (s t) -> p s t", s=2)
        SG = PR2_[:, 512:1536].rearrange("p (s t) -> p s t", s=2)
        HT = PR2_[:, 1536:2560].rearrange("p (s t) -> p s t", s=2)
        PRB_ = sb("PRB", [P, 8 * 3 * BR * P])
        PRB = PRB_[:].rearrange("p (h j b t) -> p h j b t", h=8, j=3, b=BR)
        QR = PRB_[:, 0:TH * BR * P].rearrange("p (h n t) -> p h n t", h=TH, n=BR)
        QRES = PRB_[:, TH * BR * P:2 * TH * BR * P].rearrange("p (h n t) -> p h n t", h=TH, n=BR)
        QABC = PRB_[:, 2 * TH * BR * P:4 * TH * BR * P].bitcast(BF16)[:, 0:3 * TH * BR * P].rearrange(
            "p (i h n t) -> p i h n t", i=3, h=TH, n=BR)
        V1 = sb("V1", [P, TH, NH, DH + 1])
        KS1 = sb("KS1", [P, NH, T], F16)
        QS1 = sb("QS1", [P, NH // 2, TH * BR * P], BF16)
        KEEP = sb("KEEP", [P, 3, P])
        DEN = sb("DEN", [P, 2, 4, 4])
        XB = sb("XB", [P, TH, D])
        RES, LST = sb("RES", [P, TH, D]), sb("LST", [P, 4, TH])
        X1, X2 = sb("X1", [P, TH, D]), sb("X2", [P, TH, D])
        CQB, CST = sb("CQB", [P, NT, D], BF16), sb("CST", [P, 8, NT])
        CSQ = sb("CSQ", [P, NT, D])
        K32 = CSQ[:].rearrange("p n d -> p (n d)")[:, 0:NT * 64].rearrange("p (n d) -> p n d", d=64)
        KHN = CSQ[:].rearrange("p n d -> p (n d)")[:, NT * 64:].bitcast(F16).rearrange(
            "p (n i d) -> p n i d", i=2, d=64)
        KT2 = sb("KT2", [P, NT * P], F16)
        YT = KT2[:].bitcast(BF16)
        V2N, V2 = sb("V2N", [P, NT, KV, DH]), sb("V2", [P, NT, KV, DH + 1])
        KS2 = sb("KS2", [P, KV, NT * P], F16)
        QST, OST = sb("QST", [P, 8, TH]), sb("OST", [P, 8, TH])
        QSQ = sb("QSQ", [P, TH, D])
        OSQ = QSQ
        QQB, QQT = sb("QQB", [P, TH, D], BF16), sb("QQT", [P, T], BF16)
        OQB, OQT = sb("OQB", [P, TH, D], BF16), sb("OQT", [P, T], BF16)
        Q32 = sb("Q32", [P, TH, D])
        QP = sb("QP", [P, TH, 3, D], BF16)
        QT2 = sb("QT2", [P, 3, T], BF16)
        QS2 = sb("QS2", [P, KV // 2, 2, T], BF16)
        MX = sb("MX", [P, TH, NH])
        MP, MT = sb("MP", [P, TH, 3, NH], BF16), sb("MT", [48, T], BF16)
        O2 = sb("O2", [P, 512])
        ON = sb("ON", [P, TH, NH, DH])
        X2T = sb("X2T", [P, T])
        LG, LM = sb("LG", [P, 2, TH, 8]), sb("LM", [P, 4, TH])
        CR = sb("CR", [P, TH, 8])
        LST3 = sb("LST3", [P, 4, TH])
        OUT = sb("OUT", [P, TH, D])
        BN, BA = sb("BN", [P, TH, 6]), sb("BA", [P, TH, 2])

        k_scr = nc.dram_tensor("k_scr", (2, P, T), F16).ap()
        q_scr = nc.dram_tensor("q_scr", (3, P, TH * BR * P), BF16).ap()
        k2_scr = nc.dram_tensor("k2_scr", (P, NT * P), F16).ap()
        q2_scr = nc.dram_tensor("q2_scr", (3, P, T), BF16).ap()
        m_scr = nc.dram_tensor("m_scr", (3 * NH, T), BF16).ap()

        Z = [bank(f"Z{i}") for i in range(3)]
        S = [bank(f"S{i}") for i in range(2)]
        ZR = (*Z, S[0])
        M = bank("M")
        ACC = bank("ACC")
        MISC = bank("MISC")

        SR = (*S, M)
        MR = (M, MISC, ACC, Z[1])
        MCOPY = PRB_[:, 0:4 * MCOLS].rearrange("p (s c) -> p s c", s=4)
        MSCAN = PRB_[:, 4 * MCOLS:20 * MCOLS].rearrange("p (s c) -> p s c", s=16)

        block = ctx.enter_context(nc.Block())

        def ts(v):
            return slice(v * P, (v + 1) * P)

        def bcast(ap, n):
            return ap.unsqueeze(2).to_broadcast([P, ap.shape[1], n])

        @block.sync
        def _(sp):
            once = [(identF[:], ident), (WQA[:], wqA), (WQB[:], wqB), (WKA[:], wkA), (WKB[:], wkB),
                    (WV[:], wv), (BQA[:], bqA), (BQB[:], bqB), (BKA[:], bkA), (BKB[:], bkB),
                    (BV[:], bv.partition_broadcast(P)), (HEADS[:], heads), (COS[:], rope_cos), (SIN[:], rope_sin),
                    (SINKS[:], sinks.partition_broadcast(P)),
                    (SV[:].rearrange("p h d -> p (h d)"), vnull.partition_broadcast(P)),
                    (WO[:], wo), (PR2_[:, 0:BR * P], wob.partition_broadcast(P)),
                    (W2[:, 0, :], w2q), (W2[:, 1, :], w2kv), (W2[:, 2, :], w2o),
                    (GAM[:], gamma.partition_broadcast(P)), (BET[:], beta.partition_broadcast(P)),
                    (GW[:], gate_w), (FG[:], ffn_g), (FU[:], ffn_u), (FD[:], ffn_d)]
            assert len(once) == N_WEIGHTS
            for dst, src in once:
                sp.dma_start(dst, src).then_inc(weights_in, 16)
            sp.wait_ge(setup_done, 1)

            def load(b):
                sp.dma_start(XIN[:], x[b].rearrange("(h p) d -> p h d", p=P)).then_inc(sem["x_in"], 16)
                sp.dma_start(CIN[:, 0:NT - 1, :], ctx_t[b, 0:(NT - 1) * P, :].rearrange(
                    "(i p) d -> p i d", p=P)).then_inc(sem["ctx_in"], 16)
                sp.dma_start(CIN[0:LAST, NT - 1, :], ctx_t[b, (NT - 1) * P:S2, :]).then_inc(
                    sem["ctx_in"], 16)

            def thrice(rows, r, n):
                own = rows.rearrange("(r d n) t -> r d (n t)", r=2, n=n)[r]
                return own.unsqueeze(0).to_broadcast([3] + list(own.shape))

            def parts_of(scratch, r, parts):
                return scratch.rearrange("i (r d n) t -> r i d (n t)", r=2, d=DH)[r][parts]

            def stack_stage1(b):
                sp.wait_ge(sem["kparts"], at("kparts", b, 1))
                sp.dma_start(k_scr.rearrange("n p t -> p n t"), KHL[:]).then_inc(sem["kscr"], 16)
                sp.wait_ge(sem["kscr"], at("kscr", b, 16))
                for r in range(2):
                    for part in range(2):
                        row = 64 * r + 24 * part
                        sp.dma_start(KS1[row:row + 24, 8 * r:8 * r + 8, :], thrice(k_scr[part], r, 8)
                                     ).then_inc(sem["kstack"], 16)
                sp.wait_ge(sem["qparts"], at("qparts", b, 1))
                sp.dma_start(q_scr.rearrange("n p t -> p n t"),
                             QABC[:].rearrange("p n h b t -> p n (h b t)")).then_inc(sem["qscr"], 16)
                sp.wait_ge(sem["qscr"], at("qscr", b, 16))
                for r in range(2):
                    for row in (64 * r, 64 * r + 24):
                        sp.dma_start(QS1[row:row + 24, :, :], parts_of(q_scr, r, slice(0, 3))
                                     ).then_inc(sem["qstack"], 16)
                sp.wait_ge(sem["kT_sb"], at("kT_sb", b, 2))
                sp.dma_start(k2_scr, KT2[:]).then_inc(sem["k2scr"], 16)
                sp.wait_ge(sem["k2scr"], at("k2scr", b, 16))

            def stack_stage2(b, first):
                if not first:
                    sp.wait_ge(sem["s"], at("s", b - 1, NX))
                for r in range(2):
                    for part, n, row in KEY_ROWS:
                        sp.dma_start(KS2[64 * r + row:64 * r + row + 8 * n, 4 * r:4 * r + 4, :],
                                     thrice(k2_scr[64 * part:64 * part + 64, :], r, 4)[0:n]
                                     ).then_inc(sem["k2stack"], 16)

            def stack_queries2(b):
                sp.wait_ge(sem["q2T_sb"], at("q2T_sb", b, 1))
                sp.dma_start(q2_scr.rearrange("n p t -> p n t"), QT2[:]).then_inc(sem["q2scr"], 16)
                sp.wait_ge(sem["q2scr"], at("q2scr", b, 16))
                for r in range(2):
                    for parts, row in QUERY_ROWS:
                        n = 8 * (parts.stop - parts.start)
                        sp.dma_start(QS2[64 * r + row:64 * r + row + n, :, :, :], parts_of(q2_scr, r, parts)
                                     ).then_inc(sem["q2stack"], 16)
                sp.wait_ge(sem["mT_sb"], at("mT_sb", b, 1))
                sp.dma_start(m_scr, MT[:]).then_inc(sem["mscr"], 16)
                sp.wait_ge(sem["mscr"], at("mscr", b, 16))
                for r in range(2):
                    row = 64 * r + M_ROW
                    sp.dma_start(QS2[row:row + 3, :, :, :], m_scr.rearrange(
                        "(i r n g) t -> r i n g t", i=3, r=2, g=2)[r]).then_inc(sem["mstack"], 16)

            def store(b):
                sp.wait_ge(sem["out_ready"], at("out_ready", b, 1))
                sp.dma_start(out[b].rearrange("(h p) d -> p h d", p=P), OUT[:]).then_inc(
                    sem["out_done"], 16)

            def row(b, first=False, last=False):
                stack_stage2(b, first)
                if not last:
                    load(b + 1)
                stack_queries2(b)
                if not first:
                    store(b - 1)
                if not last:
                    stack_stage1(b + 1)
                if not first:
                    sp.wait_ge(sem["out_done"], at("out_done", b - 1, 16))
                    sp.sem_inc(sem["out_free"], 1)

            load(0)
            sp.sem_inc(sem["out_free"], 1)
            stack_stage1(0)
            row(0, first=True)
            with sp.Fori(1, B - 1) as b:
                row(b)
            row(B - 1, last=True)
            store(B - 1)
            sp.wait_ge(sem["out_done"], at("out_done", B - 1, 16))

        @block.gpsimd
        def _(pool):
            pool.memset(ONES[:], 1.0).then_inc(pool_setup, 1)
            pool.iota(IOTA8[:], pattern=[[0, TH], [-1, 8]], base=8, channel_multiplier=0,
                      allow_small_or_imprecise_dtypes=True).then_inc(pool_setup, 1)

            def square_context(b):
                pool.wait_ge(sem["ctx_in"], at("ctx_in", b, 32))
                pool.tensor_tensor(CSQ[:], CIN[:], CIN[:], ALU.mult).then_inc(sem["csq"], 1)

            def mask(b):
                for h in range(NH):
                    if h < POOL_HEADS:
                        pool.wait_ge(sem["gated"], at("gated", b, h + 1))
                        pool.sem_inc(sem["masking"], 1)
                        v = PRB[:, h % 8, :, BR - 1, :]
                        sink = SINKS[:, NH * (BR - 1) + h:NH * (BR - 1) + h + 1]
                        pool.tensor_scalar(KEEP[:], v, sink, None, ALU.is_ge).then_inc(sem["thr_pool"], 1)
                        pool.wait_ge(sem["thr_pool"], at("thr_pool", b, 2 * h + 1))
                        pool.tensor_tensor(v, v, KEEP[:], ALU.mult).then_inc(sem["thr_pool"], 1)
                        pool.wait_ge(sem["thr_pool"], at("thr_pool", b, 2 * h + 2))
                    pool.wait_ge(sem["thr"], at("thr", b, (BR - 1) * (h + 1) + max(0, h + 1 - POOL_HEADS)))
                    pool.sem_inc(sem["masking"], 1)
                    for j in (0, 2):
                        v = PRB[:, h % 8, j, :, :]
                        i = pool.affine_select(out=v, in_=v, compare_op=ALU.is_ge, fill=0.0, base=0,
                                               pattern=[[0, BR], [1, P]], channel_multiplier=-1)
                    i.then_inc(sem["masked"], 1)

            square_context(0)
            mask(0)
            with pool.Fori(1, B) as b:
                square_context(b)
                mask(b)

        @block.scalar
        def _(act):
            def rsqrt(b, k, dst, src, scale, bias, ready, done, root="act_root"):
                act.wait_ge(sem[ready], at(ready, b, 1))
                act.activation(dst, src, ACT.Ln, bias=bias, scale=scale).then_inc(sem[root], 1)
                act.wait_ge(sem[root], at(root, b, k))
                act.activation(dst, dst, ACT.Exp, scale=-0.5).then_inc(sem[done], 1)

            def prepare(b, k):
                if k == 1:
                    act.wait_ge(sem["xT_ps"], at("xT_ps", b, 1))
                    act.activation(XT[:], Z[0][:, 0:T], ACT.Copy).then_inc(sem["xT_sb"], 1)
                elif k == 3:
                    rsqrt(b, 1, CST[:, 2, :], CST[:, 1, :], 1.0 / D, EPS_RMS[:], "cn_ms", "cn_r", "prep_root")
                elif k == 6:
                    act.wait_ge(sem["knorm_sb"], at("knorm_sb", b, 1))
                    act.activation(KRS[:], KSQ[:], ACT.Ln).then_inc(sem["prep_root"], 1)
                    act.wait_ge(sem["prep_root"], at("prep_root", b, 2))
                    act.activation(KRS[:], KRS[:], ACT.Exp, scale=-0.5).then_inc(sem["krs"], 1)
                elif k in (10, 16):
                    name, dst, dt = ("yT", YT, BF16) if k == 10 else ("kT", KT2, F16)
                    for c, (t0, t1) in enumerate(((0, 8), (8, NT))):
                        act.wait_ge(sem[name + "_ps"], at(name + "_ps", b, c + 1))
                        act.activation(dst[:, t0 * P:t1 * P], (Z[2], Z[0])[c][:].bitcast(dt)[:, 0:(t1 - t0) * P],
                                       ACT.Copy).then_inc(sem[name + "_sb"], 1)

            def attention1(b, first):
                act.preload_act_table_set("natural_log_exp_and_others")
                act.wait_ge(sem["kvn_read"], at("kvn_read", b, 4))
                if not first:
                    act.wait_ge(sem["av2"], at("av2", b - 1, 2 * NT))
                act.activation(V2[:, :, :, 0:DH], V2N[:], ACT.Copy).then_inc(sem["v2_ready"], 1)

                def z_tile(u):
                    return PRB[:, (u // 3) % 8, u % 3, :, :].rearrange("p b t -> p (b t)")

                def z_exp(u):
                    act.wait_ge(sem["z"], at("z", b, u + 1))
                    act.activation(z_tile(u), ZR[u % 4][:], ACT.Exp, scale=ZSCALE).then_inc(sem["zexp"], 1)

                def z_ln(u):
                    act.wait_ge(sem["zcap"], at("zcap", b, u + 1))
                    act.activation(z_tile(u), z_tile(u), ACT.Ln, bias=ONE1[:]).then_inc(sem["zln"], 1)

                def outputs(g):
                    act.wait_ge(sem["av1"], at("av1", b, g + 1))
                    if g:
                        act.wait_ge(sem["nat1"], at("nat1", b, 2 * g))
                    act.activation(O1[:, 0, :], ACC[:], ACT.Copy)
                    act.activation(O1[:, 1, :], M[:], ACT.Copy).then_inc(sem["av1_sb"], 1)

                for g in range(NH // 4):
                    for u in range(12 * g, 12 * g + 12):
                        z_exp(u)
                        if u > 12 * g:
                            z_ln(u - 1)
                    z_ln(12 * g + 11)
                    for h in range(4 * g, 4 * g + 4):
                        act.wait_ge(sem["zmax"], at("zmax", b, 3 * h + 3))
                        v = PRB[:, h % 8, :, :, :].rearrange("p j b t -> p (j b t)")
                        act.activation(v, v, ACT.Silu, scale=GATE).then_inc(sem["gated"], 1)
                    act.preload_act_table_set("natural_log_exp_and_others")
                    if g:
                        outputs(g - 1)
                outputs(NH // 4 - 1)
                for t in range(TH):
                    act.wait_ge(sem["ctxT_ps"], at("ctxT_ps", b, t + 1))
                    act.activation(CTXT[:, t, :], (MISC, S[1])[t][:], ACT.Copy).then_inc(sem["ctxT_sb"], 1)
                rsqrt(b, 1, LST[:, 3, :], LST[:, 2, :], 1.0, EPS_LN[:], "ln1_var", "ln1_rstd")

            def queries2(b):
                rsqrt(b, 2, QST[:, 2, :], QST[:, 1, :], 1.0 / D, EPS_RMS[:], "qn_ms", "qn_r")
                act.wait_ge(sem["xqT_ps"], at("xqT_ps", b, 1))
                act.activation(QQT[:], MISC[:].bitcast(BF16)[:, 0:T], ACT.Copy).then_inc(sem["xqT_sb"], 1)
                act.wait_ge(sem["q2T_ps"], at("q2T_ps", b, 1))
                act.activation(QT2[:].rearrange("p n t -> p (n t)"), MISC[:].bitcast(BF16)[:, 0:3 * T],
                               ACT.Copy).then_inc(sem["q2T_sb"], 1)

            def ffn(b, k):
                if k == 1:
                    act.wait_ge(sem["x2T_ps"], at("x2T_ps", b, 1))
                    act.activation(X2T[:], S[1][:, 0:T], ACT.Copy).then_inc(sem["x2T_sb"], 1)
                elif k == 5:
                    act.wait_ge(sem["lmax"], at("lmax", b, 1))
                    act.activation(LM[:, 1, :], LM[:, 0, :], ACT.Exp, scale=-1.0).then_inc(sem["lexp"], 1)
                elif expert(k, "silu") is not None:
                    e = expert(k, "silu")
                    act.wait_ge(sem["g"], at("g", b, e + 1))
                    if e >= 2:
                        act.wait_ge(sem["hT"], at("hT", b, e - 1))
                    act.activation(SG[:, e % 2, :], Z[0][:], ACT.Silu).then_inc(sem["silu"], 1)
                elif k == FFN_STEPS - 1:
                    act.preload_act_table_set("natural_log_exp_and_others")
                    rsqrt(b, 1, LST3[:, 3, :], LST3[:, 2, :], 1.0, EPS_LN[:], "ln3_var", "ln3_rstd", "ffn_root")

            def maxima(b, with_ffn):
                for u in range(NM):
                    if with_ffn and u < FFN_STEPS:
                        ffn(b - 1, u)
                    if u % 2:
                        act.wait_ge(sem["mx"], at("mx", b, u + 1))
                        if u >= 8:
                            act.wait_ge(sem["mx_read"], at("mx_read", b, (u - 7) // 2 + 1))
                        act.activation(MCOPY[:, u // 2 % 4, :], MR[u % 4][:, 0:MCOLS], ACT.Copy
                                       ).then_inc(sem["mx_copy"], 1)

            def softmax2(b, nxt):
                act.wait_ge(sem["mT_ps"], at("mT_ps", b, 1))
                act.activation(MT[:], MISC[0:3 * NH, :].bitcast(BF16)[:, 0:T], ACT.Copy).then_inc(sem["mT_sb"], 1)
                for u in range(NX):
                    if nxt and u in PREP_AT:
                        prepare(b + 1, PREP_AT[u])
                    n = P if (u % (NX // 2)) // 4 < NT - 1 else LAST
                    act.wait_ge(sem["s"], at("s", b, u + 1))
                    if u >= 8:
                        act.wait_ge(sem["av2"], at("av2", b, u // 4 - 1))
                    act.activation(PR2[0:n, u % 8, :], SR[u % 3][0:n, :], ACT.Exp).then_inc(sem["sexp"], 1)
                    if u in (NX // 2 + 3, NX - 1):
                        act.wait_ge(sem["av2"], at("av2", b, NT if u < NX - 1 else 2 * NT))
                        if u == NX - 1:
                            act.wait_ge(sem["nat2"], at("nat2", b, 1))
                        act.activation(O2[:], ACC[:], ACT.Copy).then_inc(sem["o2_sb"], 1)
                rsqrt(b, 3, OST[:, 2, :], OST[:, 1, :], 1.0, EPS_LN[:], "on_var", "on_rstd")
                rsqrt(b, 4, OST[:, 4, :], OST[:, 3, :], 1.0 / D, EPS_RMS[:], "on_ms", "on_r")
                act.wait_ge(sem["oqT_ps"], at("oqT_ps", b, 1))
                act.activation(OQT[:], MISC[:].bitcast(BF16)[:, 0:T], ACT.Copy).then_inc(sem["oqT_sb"], 1)
                rsqrt(b, 5, LST[:, 3, :], LST[:, 2, :], 1.0, EPS_LN[:], "ln2_var", "ln2_rstd")

            def row(b, first=False, last=False):
                attention1(b, first)
                queries2(b)
                maxima(b, with_ffn=not first)
                softmax2(b, nxt=not last)

            act.wait_ge(setup_done, 1)
            act.preload_act_table_set("natural_log_exp_and_others")
            for k in range(PREP_STEPS):
                prepare(0, k)
            row(0, first=True)
            with act.Fori(1, B - 1) as b:
                row(b)
            row(B - 1, last=True)
            for k in range(FFN_STEPS):
                ffn(B - 1, k)

        @block.tensor
        def _(pe):
            def transposes(dst, parts, idn):
                for i, src in enumerate(parts):
                    n = src.shape[1]
                    last = pe.transpose(dst[0:n, ts(i)], src, idn)
                return last

            pe.wait_ge(pool_setup, 2)
            pe.wait_ge(abs_ready, 4)
            pe.matmul(MISC[:, 0:4], ONES[:], ABS[:], start=True, stop=True).then_inc(abs_sums, 1)
            pe.wait_ge(ternary, 1)
            transposes(MISC[:].bitcast(BF16), [W2N[:, i, :] for i in range(3)], identB[:]).then_inc(ternary_T, 1)
            pe.wait_ge(setup_done, 1)

            def prepare(b, k):
                def queries(br):
                    if br >= 2:
                        pe.wait_ge(sem["qproj_read"], at("qproj_read", b, br - 1))
                    pe.matmul(Z[br % 2][:, 0:T], WQA[:, ts(br)], XT[:], start=True, stop=True)
                    pe.matmul(Z[br % 2][:, T:2 * T], WQB[:, ts(br)], XT[:], start=True,
                              stop=True).then_inc(sem["qproj"], 1)

                def context_projections(c):
                    dst = Z[1 + c % 2]
                    for i in range(4 * c, min(4 * c + 4, NT)):
                        last = pe.matmul(dst[:, ts(i - 4 * c)], YT[:, ts(i)], W2T[:, 1, :],
                                         start=True, stop=True)
                    last.then_inc(sem["kvn"], 1)

                if k == 0:
                    pe.wait_ge(sem["x_in"], at("x_in", b, 16))
                    transposes(Z[0], [XIN[:, t, :] for t in range(TH)], identF[:]).then_inc(sem["xT_ps"], 1)
                elif k == 2:
                    pe.wait_ge(sem["xT_sb"], at("xT_sb", b, 1))
                    pe.matmul(Z[1][:, 0:T], WKA[:], XT[:], start=True, stop=True)
                    pe.matmul(Z[1][:, T:2 * T], WKB[:], XT[:], start=True, stop=True).then_inc(sem["kproj"], 1)
                    for t in range(TH):
                        last = pe.matmul(Z[2][:, ts(t)], XT[:, ts(t)], WV[:], start=True, stop=True)
                    last.then_inc(sem["vproj"], 1)
                    queries(0)
                elif k == 4:
                    pe.wait_ge(sem["ksq_sb"], at("ksq_sb", b, 1))
                    pe.wait_ge(sem["v1_ready"], at("v1_ready", b, 1))
                    pe.matmul(Z[2][:, 0:T], HEADS[:], KSQ[:], start=True, stop=True).then_inc(sem["knorm_ps"], 1)
                    queries(1)
                elif k in (5, 6):
                    queries(k - 3)
                elif k == 9:
                    pe.wait_ge(sem["yq"], at("yq", b, 1))
                    pe.wait_ge(sem["knorm_sb"], at("knorm_sb", b, 1))
                    pe.wait_ge(sem["qproj_read"], at("qproj_read", b, 4))
                    transposes(Z[2][:].bitcast(BF16), [CQB[:, i, :] for i in range(8)], identB[:]
                               ).then_inc(sem["yT_ps"], 1)
                    transposes(Z[0][:].bitcast(BF16), [CQB[:, i, :] for i in range(8, NT)], identB[:]
                               ).then_inc(sem["yT_ps"], 1)
                elif k == 11:
                    pe.wait_ge(sem["yT_sb"], at("yT_sb", b, 2))
                    context_projections(0)
                    context_projections(1)
                elif k == 13:
                    for c in (2, 3):
                        pe.wait_ge(sem["kvn_read"], at("kvn_read", b, c - 1))
                        context_projections(c)
                elif k == 15:
                    pe.wait_ge(sem["khl"], at("khl", b, 1))
                    pe.wait_ge(sem["kvn_read"], at("kvn_read", b, 4))
                    for bank_, tiles in ((Z[2], range(8)), (Z[0], range(8, NT))):
                        transposes(bank_[:].bitcast(F16), [KHN[:, i, :, :].rearrange("p n d -> p (n d)")
                                                           for i in tiles], identH[:]).then_inc(sem["kT_ps"], 1)

            def attention1(b):
                pe.wait_ge(sem["kstack"], at("kstack", b, PER["kstack"]))
                pe.wait_ge(sem["qstack"], at("qstack", b, PER["qstack"]))
                pe.wait_ge(sem["kT_sb"], at("kT_sb", b, 2))

                def scores(u):
                    h, j = u // 3, u % 3
                    keys, queries = (0, 0, 1)[j], (0, 1, 1)[j]
                    if u >= 4:
                        pe.wait_ge(sem["zmax"], at("zmax", b, u - 3))
                    pe.matmul(ZR[u % 4][:], KS1[:, 8 * (h % 2) + h // 2, ts(keys)], QS1[:, h // 2, queries * 512:(queries + 1) * 512],
                              start=True, stop=True).then_inc(sem["z"], 1)

                def values(g):
                    pe.wait_ge(sem["masked"], at("masked", b, 4 * g + 4))
                    if g:
                        pe.wait_ge(sem["av1_sb"], at("av1_sb", b, g))
                    for j in range(3):
                        for h in range(4 * g, 4 * g + 4):
                            c = 32 * (h % 4)
                            last = pe.matmul((ACC, M, M)[j][c:c + DH + 1, :], V1[:, (0, 0, 1)[j], h, :],
                                             PRB[:, h % 8, j, :, :].rearrange("p b t -> p (b t)"),
                                             start=j < 2, stop=j != 1)
                    last.then_inc(sem["av1"], 1)
                    pe.wait_ge(sem["av1_sb"], at("av1_sb", b, g + 1))
                    for t in range(TH):
                        if g:
                            pe.wait_ge(sem["nat1_read"], at("nat1_read", b, 2 * g - 1 + t))
                        transposes((MISC, S[1])[t], [O1[:, t, ts(i)] for i in range(BR)], identF[:]
                                   ).then_inc(sem["nat1"], 1)

                for g in range(NH // 4):
                    for u in range(12 * g, 12 * g + 12):
                        scores(u)
                    if g:
                        values(g - 1)
                values(NH // 4 - 1)
                for t in range(TH):
                    pe.wait_ge(sem["nat1_read"], at("nat1_read", b, 7 + t))
                    transposes((MISC, S[1])[t], [CTX[:, t, i, :] for i in range(BR)], identF[:]
                               ).then_inc(sem["ctxT_ps"], 1)
                for t in range(TH):
                    pe.wait_ge(sem["ctxT_sb"], at("ctxT_sb", b, t + 1))
                    for i in range(BR):
                        last = pe.matmul(ACC[:, ts(t)], CTXT[:, t, ts(i)], WO[:, i, :],
                                         start=i == 0, stop=i == BR - 1)
                last.then_inc(sem["y1"], 1)

            def queries2(b):
                pe.wait_ge(sem["xq"], at("xq", b, 1))
                transposes(MISC[:].bitcast(BF16), [QQB[:, t, :] for t in range(TH)], identB[:]
                           ).then_inc(sem["xqT_ps"], 1)
                pe.wait_ge(sem["xqT_sb"], at("xqT_sb", b, 1))
                for t in range(TH):
                    last = pe.matmul(S[1][:, ts(t)], QQT[:, ts(t)], W2T[:, 0, :], start=True, stop=True)
                last.then_inc(sem["qn"], 1)
                pe.wait_ge(sem["q2parts"], at("q2parts", b, 1))
                transposes(MISC[:].bitcast(BF16), [QP[:, t, i, :] for i in range(3) for t in range(TH)],
                           identB[:]).then_inc(sem["q2T_ps"], 1)

            def ffn(b, k):
                if k == 0:
                    pe.wait_ge(sem["x2"], at("x2", b, 1))
                    transposes(S[1], [X2[:, t, :] for t in range(TH)], identF[:]).then_inc(sem["x2T_ps"], 1)
                elif k == 2:
                    pe.wait_ge(sem["x2T_sb"], at("x2T_sb", b, 1))
                    for t in range(TH):
                        last = pe.matmul(S[1][:, 8 * t:8 * t + 8], X2T[:, ts(t)], GW[:], start=True, stop=True)
                    last.then_inc(sem["logits"], 1)
                e = expert(k, "weight")
                if e:
                    if e >= 2:
                        pe.wait_ge(sem["xe"], at("xe", b, e - 1))
                    else:
                        pe.wait_ge(sem["route"], at("route", b, 1))
                    for t in range(TH):
                        last = pe.matmul(S[1][:, ts(t)], CR[:, t, e - 1:e].to_broadcast([P, P]), identF[:],
                                         start=True, stop=True)
                    last.then_inc(sem["bc"], 1)
                for name, w in (("gate", FG), ("up", FU)):
                    e = expert(k, name)
                    if e is not None:
                        dst = Z[0] if w is FG else Z[2]
                        if e:
                            pe.wait_ge(sem["xe"], at("xe", b, e))
                        if e and w is FG:
                            pe.wait_ge(sem["silu"], at("silu", b, e))
                        if e and w is FU:
                            pe.wait_ge(sem["hT"], at("hT", b, e))
                        for c in range(FC):
                            last = pe.matmul(dst[:, c * T:(c + 1) * T], w[:, e, ts(c)],
                                             XE[:, e % 2, :] if e else X2T[:], start=True, stop=True)
                        last.then_inc(sem["g" if w is FG else "up"], 1)
                for t in range(TH):
                    e = expert(k, f"down{t}")
                    if e is not None:
                        pe.wait_ge(sem["hT"], at("hT", b, e + 1))
                        for c in range(FC):
                            last = pe.matmul(S[0][:, ts(t)], HT[:, e % 2, c * T + t * P:c * T + (t + 1) * P],
                                             FD[:, e, c, :], start=(e == 0 and t == 0 and c == 0),
                                             stop=(e == E - 1 and c == FC - 1), skip_group_check=True)
                        if t:
                            last.then_inc(sem["down"], 1)

            def maxima(b, with_ffn):
                pe.wait_ge(sem["k2stack"], at("k2stack", b, PER["k2stack"]))
                pe.wait_ge(sem["q2stack"], at("q2stack", b, PER["q2stack"]))
                pe.wait_ge(sem["mzero"], at("mzero", b, 2))
                for u in range(NM):
                    if with_ffn and u < FFN_STEPS:
                        ffn(b - 1, u)
                    h, t, c = u // 8, (u // 4) % 2, u % 4
                    if u >= 4:
                        name = "mx_copy" if u % 2 else "mx_read"
                        pe.wait_ge(sem[name], at(name, b, (u - 4) // 2 + 1))
                    pe.matmul(MR[u % 4][:, 0:MCOLS], QS2[:, h // 4, h % 2, ts(t)],
                              KS2[:, 4 * (h // 2 % 2) + h // 4, CHUNKS[c]:CHUNKS[c] + MCOLS], start=True, stop=True
                              ).then_inc(sem["mx"], 1)
                pe.wait_ge(setup_done, 1)
                pe.wait_ge(sem["mparts"], at("mparts", b, 1))
                transposes(MISC[:].bitcast(BF16), [MP[:, t, :, :].rearrange("p n h -> p (n h)") for t in range(TH)],
                           identB[:]).then_inc(sem["mT_ps"], 1)

            def softmax2(b, nxt):
                pe.wait_ge(sem["mstack"], at("mstack", b, PER["mstack"]))
                pe.wait_ge(sem["v2_ready"], at("v2_ready", b, 1))

                def values(g4):
                    q, i = g4 // NT, g4 % NT
                    n = P if i < NT - 1 else LAST
                    if g4 == NT:
                        pe.wait_ge(sem["o2_sb"], at("o2_sb", b, 1))
                    pe.wait_ge(sem["sexp"], at("sexp", b, 4 * g4 + 4))
                    for c in range(4):
                        last = pe.matmul(ACC[32 * c:32 * c + DH + 1, :], V2[0:n, i, 4 * q + c, :],
                                         PR2[0:n, (4 * g4 + c) % 8, :], start=i == 0, stop=i == NT - 1)
                    last.then_inc(sem["av2"], 1)
                    if i == NT - 1:
                        pe.wait_ge(sem["o2_sb"], at("o2_sb", b, q + 1))
                        if q:
                            pe.wait_ge(sem["nat2_read"], at("nat2_read", b, q))
                        transposes(MISC, [O2[:, ts(k)] for k in range(4)], identF[:]).then_inc(sem["nat2"], 1)

                for g4 in range(2 * NT):
                    q, i = g4 // NT, g4 % NT
                    n = P if i < NT - 1 else LAST
                    for c in range(4):
                        u, kv = 4 * g4 + c, 4 * q + c
                        if nxt and u in PREP_AT:
                            prepare(b + 1, PREP_AT[u])
                        if u >= 3:
                            pe.wait_ge(sem["sexp"], at("sexp", b, u - 2))
                        pe.matmul(SR[u % 3][0:n, :], KS2[:, 4 * (kv % 2) + kv // 2, i * P:i * P + n],
                                  QS2[:, kv // 2, :, :].rearrange("p g t -> p (g t)"),
                                  start=True, stop=True).then_inc(sem["s"], 1)
                    if g4:
                        values(g4 - 1)
                values(2 * NT - 1)

                pe.wait_ge(sem["oq"], at("oq", b, 1))
                transposes(MISC[:].bitcast(BF16), [OQB[:, t, :] for t in range(TH)], identB[:]
                           ).then_inc(sem["oqT_ps"], 1)
                pe.wait_ge(sem["oqT_sb"], at("oqT_sb", b, 1))
                for t in range(TH):
                    last = pe.matmul(S[1][:, ts(t)], OQT[:, ts(t)], W2T[:, 2, :], start=True, stop=True)
                last.then_inc(sem["y2"], 1)

            def row(b, first=False, last=False):
                attention1(b)
                queries2(b)
                maxima(b, with_ffn=not first)
                softmax2(b, nxt=not last)

            for k in range(PREP_STEPS):
                prepare(0, k)
            row(0, first=True)
            with pe.Fori(1, B - 1) as b:
                row(b)
            row(B - 1, last=True)
            for k in range(FFN_STEPS):
                ffn(B - 1, k)

        @block.vector
        def _(dve):
            dve.wait_ge(weights_in, 16 * N_WEIGHTS)
            dve.wait_ge(pool_setup, 2)
            setup = Chain(dve, sem, "dve_setup", 0)
            for dst, value in ((ABS, 0.0), (EPS_LN, 1e-5), (EPS_RMS, 1e-6), (ONE1, 1.0),
                               (V1, 0.0), (V2, 0.0), (KS1, 0.0), (QS1, 0.0), (KS2, 0.0), (QS2, 0.0),
                               (CIN, 0.0)):
                setup(dve.memset(dst[:], value))
            for r in range(2):
                setup(dve.memset(KS2[64 * r + M_ROW:64 * r + M_ROW + 3, 4 * r:4 * r + 4, :], 1.0))
            setup(dve.tensor_copy(identB[:], identF[:]))
            setup(dve.tensor_copy(identH[:], identF[:]))
            for v in (V1, V2):
                setup(dve.memset(v[:, :, :, DH:DH + 1], 1.0))
            for v in (*Z, *S, M, ACC, MISC):
                setup(dve.memset(v[:], 0.0))
            for col, rows, i in ((0, slice(0, P), 0), (1, slice(0, 64), 1), (2, slice(64, P), 1),
                                 (3, slice(0, P), 2)):
                dve.tensor_reduce(out=ABS[rows, col:col + 1], in_=W2[rows, i, :], axis=AX.X,
                                  op=ALU.add, apply_absolute_value=True).then_inc(abs_ready, 1)
            dve.wait_ge(abs_sums, 1)
            for col, n in ((0, P * D), (1, 64 * D), (2, 64 * D), (3, P * D)):
                setup(dve.tensor_scalar(WSC[:, col:col + 1], MISC[:, col:col + 1], 1.0 / n, 1e-5,
                                        ALU.mult, ALU.max))
            setup(dve.reciprocal(WINV[:], WSC[:]))
            for rows, i, col in ((slice(0, P), 0, 0), (slice(0, 64), 1, 1), (slice(64, P), 1, 2),
                                 (slice(0, P), 2, 3)):
                setup(dve.tensor_scalar(W2[rows, i, :], W2[rows, i, :], WINV[rows, col:col + 1], MAGIC,
                                        ALU.mult, ALU.add))
            setup(dve.tensor_scalar(W2, W2, MAGIC, None, ALU.subtract))
            dve.tensor_scalar(W2N[:], W2, -1.0, 1.0, ALU.max, ALU.min).then_inc(ternary, 1)
            setup(dve.tensor_tensor(QC[:], WSC[:, 0:1], WSC[:, 1:2], ALU.mult))
            setup(dve.tensor_scalar(QC[:], QC[:], DH ** -0.5, None, ALU.mult))
            setup(dve.tensor_scalar(SINKS[:], SINKS[:], GATE, None, ALU.mult))
            setup(dve.tensor_scalar(SINKD[:], SINKS[:], GATE * 1e-6, None, ALU.add))
            setup(dve.tensor_tensor(SV[:], SV[:], bcast(SINKS[:], DH), ALU.mult))
            setup(dve.tensor_tensor(BMEAN[:], WOB[:, 0, :], WOB[:, 1, :], ALU.add))
            setup(dve.tensor_tensor(BMEAN[:], BMEAN[:], WOB[:, 2, :], ALU.add))
            setup(dve.tensor_tensor(BMEAN[:], BMEAN[:], WOB[:, 3, :], ALU.add))
            setup(dve.tensor_scalar(BMEAN[:], BMEAN[:], 1.0 / BR, None, ALU.mult))
            dve.wait_ge(ternary_T, 1)
            dve.tensor_copy(W2T[:].rearrange("p n d -> p (n d)"), MISC[:].bitcast(BF16)[:, 0:3 * P]
                            ).then_inc(setup_done, 1)
            setup.end()

            def layer_norm(b, link, src, stats, dst, var_ready, rstd_ready, done):
                for t in range(TH):
                    link(dve.bn_stats(BN[:, t, :], src[:, t, :]), carrier=sem["bn_steps"])
                for t in range(TH):
                    link(dve.bn_aggr(BA[:, t, :], BN[:, t, :]), carrier=sem["bn_steps"])
                dve.tensor_copy(stats[:, 2, :], BA[:, :, 1]).then_inc(sem[var_ready], 1)
                dve.wait_ge(sem[rstd_ready], at(rstd_ready, b, 1))
                for t in range(TH):
                    last = dve.tensor_scalar(dst[:, t, :], src[:, t, :], BA[:, t, 0:1], stats[:, 3, t:t + 1],
                                             ALU.subtract, ALU.mult)
                    if t < TH - 1:
                        link(last)
                last.then_inc(sem[done], 1)

            def mean_square(link, src, stats, ready):
                link(dve.tensor_reduce(out=stats[:, 0, :], in_=src[:], axis=AX.X, op=ALU.max,
                                       apply_absolute_value=True))
                link(dve.tensor_tensor(QSQ[:], src[:], src[:], ALU.mult))
                dve.tensor_reduce(out=stats[:, 1, :], in_=QSQ[:], axis=AX.X, op=ALU.add).then_inc(sem[ready], 1)

            def quant_scales(link, stats, root):
                link(dve.tensor_tensor(stats[:, 5, :], stats[:, 0, :], stats[:, root, :], ALU.mult))
                link(dve.tensor_scalar(stats[:, 5, :], stats[:, 5, :], 1e-5, None, ALU.max))
                link(dve.reciprocal(stats[:, 6, :], stats[:, 5, :]))
                link(dve.tensor_tensor(stats[:, 6, :], stats[:, 6, :], stats[:, root, :], ALU.mult))
                link(dve.tensor_scalar(stats[:, 6, :], stats[:, 6, :], 127.0, None, ALU.mult))
                link(dve.tensor_scalar(stats[:, 7, :], stats[:, 5, :], 1.0 / 127.0, None, ALU.mult))

            link = {}

            def rope(psum, bias_a, bias_b, dst, done):
                chain = link["prep"]
                chain(dve.scalar_tensor_tensor(out=TB[:, 0, :], in0=psum[:, 0:T], scalar=bias_a, in1=COS[:],
                                               op0=ALU.add, op1=ALU.mult))
                chain(dve.scalar_tensor_tensor(out=TB[:, 1, :], in0=psum[:, T:2 * T], scalar=bias_b,
                                               in1=SIN[:], op0=ALU.add, op1=ALU.mult))
                cos_part, sin_part = TB[:, 0, :], TB[:, 1, :]
                if len(dst.shape) == 3:
                    cos_part, sin_part = (v.rearrange("p (h t) -> p h t", h=TH) for v in (cos_part, sin_part))
                ins = dve.tensor_tensor(dst, cos_part, sin_part, ALU.add)
                if done:
                    ins.then_inc(sem[done], 1)
                else:
                    chain(ins)

            def queries(b, br):
                dve.wait_ge(sem["qproj"], at("qproj", b, br + 1))
                rope(Z[br % 2], BQA[:, br:br + 1], BQB[:, br:br + 1], QR[:, :, br, :], "qproj_read")
                dve.wait_ge(sem["qproj_read"], at("qproj_read", b, br + 1))

            def context_projections(b, c):
                i0, i1 = 4 * c, min(4 * c + 4, NT)
                n = i1 - i0
                src = Z[1 + c % 2][:, 0:n * P].rearrange("p (n d) -> p n d", d=P)
                dve.wait_ge(sem["kvn"], at("kvn", b, c + 1))
                dve.tensor_tensor(K32[:, i0:i1, :], src[:, :, 0:64], bcast(CST[:, 7, i0:i1], 64), ALU.mult)
                dve.tensor_tensor(V2N[:, i0:i1, :, :],
                                  src[:, :, 64:P].rearrange("p n (h d) -> p n h d", d=DH),
                                  CST[:, 4, i0:i1].unsqueeze(2).unsqueeze(3).to_broadcast(
                                      [P, n, KV, DH]), ALU.mult).then_inc(sem["kvn_read"], 1)

            def prepare(b, k):
                if k == 0:
                    link["prep"] = Chain(dve, sem, "dve_prep", b)
                    link["ctx"] = Chain(dve, sem, "dve_ctx", b)
                    dve.wait_ge(sem["ctx_in"], at("ctx_in", b, 32))
                    link["ctx"](dve.tensor_reduce(out=CST[:, 0, :], in_=CIN[:], axis=AX.X, op=ALU.max,
                                                  apply_absolute_value=True))
                elif k == 2:
                    dve.wait_ge(sem["csq"], at("csq", b, 1))
                    dve.tensor_reduce(out=CST[:, 1, :], in_=CSQ[:], axis=AX.X, op=ALU.add).then_inc(sem["cn_ms"], 1)
                    dve.wait_ge(sem["x_in"], at("x_in", b, 16))
                    for t in range(TH):
                        link["prep"](dve.tensor_tensor(XB[:, t, :], XIN[:, t, :], BMEAN[:], ALU.add))
                elif k == 3:
                    dve.wait_ge(sem["kproj"], at("kproj", b, 1))
                    rope(Z[1], BKA[:], BKB[:], KR[:], None)
                    dve.tensor_tensor(KSQ[:], KR[:], KR[:], ALU.mult).then_inc(sem["ksq_sb"], 1)
                    dve.wait_ge(sem["vproj"], at("vproj", b, 1))
                    for t in range(TH):
                        last = dve.tensor_tensor(V1[:, t, :, 0:DH],
                                                 Z[2][:, ts(t)].rearrange("p (h d) -> p h d", d=DH),
                                                 BV[:].rearrange("p (h d) -> p h d", d=DH), ALU.add)
                    last.then_inc(sem["v1_ready"], 1)
                elif k == 4:
                    dve.wait_ge(sem["cn_r"], at("cn_r", b, 1))
                    quant_scales(link["ctx"], CST, 2)
                    link["ctx"](dve.tensor_scalar(CST[:, 4, :], CST[:, 7, :], WSC[:, 2:3], None, ALU.mult))
                    queries(b, 0)
                elif k == 5:
                    dve.wait_ge(sem["knorm_ps"], at("knorm_ps", b, 1))
                    dve.tensor_scalar(KSQ[:], Z[2][:, 0:T], 1e-6, None, ALU.max).then_inc(sem["knorm_sb"], 1)
                    queries(b, 1)
                elif k == 6:
                    queries(b, 2)
                    link["ctx"](dve.tensor_tensor(CIN[:], CIN[:], bcast(CST[:, 6, :], D), ALU.mult))
                elif k == 7:
                    dve.wait_ge(sem["krs"], at("krs", b, 1))
                    link["prep"](dve.scalar_tensor_tensor(out=TB[:, 0, :], in0=KR[:], scalar=KGAIN, in1=KRS[:],
                                                          op0=ALU.mult, op1=ALU.mult))
                    link["prep"](dve.tensor_copy(KHL[:, 0, :], TB[:, 0, :]))
                    dve.tensor_tensor(KHL[:, 1, :], TB[:, 0, :], KHL[:, 0, :], ALU.subtract).then_inc(sem["kparts"], 1)
                    dve.wait_ge(sem["kparts"], at("kparts", b, 1))
                    queries(b, 3)
                elif k == 8:
                    dve.tensor_scalar(CQB[:], CIN[:], MAGIC, MAGIC, ALU.add, ALU.subtract).then_inc(sem["yq"], 1)
                    link["prep"](dve.tensor_copy(QABC[:, 0], QR[:]))
                    link["prep"](dve.tensor_tensor(QRES[:], QR[:], QABC[:, 0], ALU.subtract))
                elif k == 9:
                    link["prep"](dve.tensor_copy(QABC[:, 1], QRES[:]))
                    dve.tensor_tensor(QABC[:, 2], QRES[:], QABC[:, 1], ALU.subtract).then_inc(sem["qparts"], 1)
                    link["prep"].end()
                elif k == 12:
                    context_projections(b, 0)
                    context_projections(b, 1)
                elif k == 14:
                    context_projections(b, 2)
                    context_projections(b, 3)
                    dve.wait_ge(sem["kvn_read"], at("kvn_read", b, 4))
                    link["ctx"](dve.tensor_copy(KHN[:, :, 0, :], K32[:]))
                    dve.tensor_tensor(KHN[:, :, 1, :], K32[:], KHN[:, :, 0, :], ALU.subtract).then_inc(sem["khl"], 1)
                    link["ctx"].end()

            def attention1(b):
                def z_tile(u):
                    return PRB[:, (u // 3) % 8, u % 3, :, :].rearrange("p b t -> p (b t)")

                def z_cap(u):
                    dve.wait_ge(sem["zexp"], at("zexp", b, u + 1))
                    dve.tensor_scalar(z_tile(u), z_tile(u), CAP, None, ALU.min).then_inc(sem["zcap"], 1)

                def z_max(u):
                    dve.wait_ge(sem["zln"], at("zln", b, u + 1))
                    dve.scalar_tensor_tensor(out=z_tile(u), in0=ZR[u % 4][:], scalar=ZSCALE, in1=z_tile(u),
                                             op0=ALU.mult, op1=ALU.max).then_inc(sem["zmax"], 1)

                def threshold(h, br):
                    dve.wait_ge(sem["gated"], at("gated", b, h + 1))
                    v = PRB[:, h % 8, :, br, :]
                    dve.scalar_tensor_tensor(out=v, in0=v, scalar=SINKS[:, NH * br + h:NH * br + h + 1],
                                             in1=v, op0=ALU.is_ge, op1=ALU.mult).then_inc(sem["thr"], 1)

                nat = Chain(dve, sem, "dve_nat", b)

                def normalise(g, t):
                    dve.wait_ge(sem["nat1"], at("nat1", b, 2 * g + t + 1))
                    src = (MISC, S[1])[t][:].rearrange("p (n h c) -> p n h c", n=BR, c=32)
                    sink = SINKD[:].rearrange("p (n h) -> p n h", n=BR)[:, :, 4 * g:4 * g + 4]
                    null = SV[:].rearrange("p (n h) d -> p n h d", n=BR)[:, :, 4 * g:4 * g + 4, :]
                    dst = CTX[:, t, :, :].rearrange("p n (h d) -> p n h d", d=DH)[:, :, 4 * g:4 * g + 4, :]
                    nat(dve.tensor_tensor(DEN[:, t], src[:, :, :, DH], sink, ALU.add))
                    nat(dve.reciprocal(DEN[:, t], DEN[:, t]))
                    nat(dve.tensor_tensor(dst, src[:, :, :, 0:DH], null, ALU.add))
                    dve.tensor_tensor(dst, dst, DEN[:, t].unsqueeze(3).to_broadcast([P, BR, 4, DH]),
                                      ALU.mult).then_inc(sem["nat1_read"], 1)

                for g in range(NH // 4):
                    for i in range(12):
                        z_cap(12 * g + i)
                        if i > 1:
                            z_max(12 * g + i - 2)
                        if g:
                            threshold(4 * (g - 1) + i // 3, i % 3)
                    z_max(12 * g + 10)
                    z_max(12 * g + 11)
                    if g > 1:
                        for t in range(TH):
                            normalise(g - 2, t)
                for r in range(2):
                    dve.memset(QS2[64 * r + M_ROW:64 * r + M_ROW + 3, :, :, :], 0.0).then_inc(sem["mzero"], 1)
                g = NH // 4 - 1
                for h in range(4 * g, 4 * g + 4):
                    for br in range(BR):
                        threshold(h, br)
                for g in (NH // 4 - 2, NH // 4 - 1):
                    for t in range(TH):
                        normalise(g, t)
                nat.end()

            def output1(b):
                link = Chain(dve, sem, "dve_ln1", b)
                dve.wait_ge(sem["y1"], at("y1", b, 1))
                link(dve.scalar_tensor_tensor(out=RES[:].rearrange("p h d -> p (h d)"), in0=ACC[:, 0:T],
                                              scalar=1.0 / BR, in1=XB[:].rearrange("p h d -> p (h d)"),
                                              op0=ALU.mult, op1=ALU.add))
                layer_norm(b, link, RES, LST, X1, "ln1_var", "ln1_rstd", "x1")
                dve.wait_ge(sem["x1"], at("x1", b, 1))
                link.end()


            def queries2(b):
                link = Chain(dve, sem, "dve_q", b)
                mean_square(link, X1, QST, "qn_ms")
                dve.wait_ge(sem["qn_r"], at("qn_r", b, 1))
                quant_scales(link, QST, 2)
                link(dve.tensor_scalar(QST[:, 7, :], QST[:, 7, :], QC[:], None, ALU.mult))
                link(dve.tensor_tensor(QSQ[:], X1[:], bcast(QST[:, 6, :], D), ALU.mult))
                dve.tensor_scalar(QQB[:], QSQ[:], MAGIC, MAGIC, ALU.add, ALU.subtract).then_inc(sem["xq"], 1)
                dve.wait_ge(sem["qn"], at("qn", b, 1))
                link(dve.tensor_tensor(Q32[:], S[1][:, 0:T].rearrange("p (h d) -> p h d", d=D),
                                       bcast(QST[:, 7, :], D), ALU.mult))
                link(dve.tensor_copy(QP[:, :, 0, :], Q32[:]))
                link(dve.tensor_tensor(Q32[:], Q32[:], QP[:, :, 0, :], ALU.subtract))
                link(dve.tensor_copy(QP[:, :, 1, :], Q32[:]))
                dve.tensor_tensor(QP[:, :, 2, :], Q32[:], QP[:, :, 1, :], ALU.subtract).then_inc(sem["q2parts"], 1)
                link.end()


            def maxima(b, with_ffn):
                chain = Chain(dve, sem, "dve_m", b)

                def batch(k):
                    place = 8 * (k // 2 % 2) + 2 * (k // 4) + k % 2
                    slots = MSCAN[:, 4 * (k % 4):4 * (k % 4) + 4, MCOLS - 1:MCOLS].rearrange(
                        "p (t c) o -> p t (c o)", t=TH)
                    dve.tensor_reduce(out=MX[:, :, place:place + 1], in_=slots, axis=AX.X, op=ALU.max, negate=True
                                      ).then_inc(sem["mx_head"], 1)

                for u in range(NM):
                    if with_ffn and u < FFN_STEPS:
                        ffn(b - 1, u)
                    if u % 2:
                        h = u // 8
                        dve.wait_ge(sem["mx_copy"], at("mx_copy", b, u // 2 + 1))
                        dve.tensor_tensor_scan(out=MSCAN[:, u // 2 % 16, :], data0=MR[(u - 1) % 4][:, 0:MCOLS],
                                               data1=MCOPY[:, u // 2 % 4, :], initial=LOWEST,
                                               op0=ALU.max, op1=ALU.max).then_inc(sem["mx_read"], 1)
                        if h and u % 8 == 1:
                            dve.wait_ge(sem["mx_read"], at("mx_read", b, 4 * h))
                            batch(h - 1)
                dve.wait_ge(sem["mx_read"], at("mx_read", b, NM // 2))
                batch(NH - 1)
                dve.wait_ge(sem["mx_head"], at("mx_head", b, NH))
                link = chain
                link(dve.tensor_copy(MP[:, :, 0, :], MX[:]))
                link(dve.tensor_tensor(MX[:], MX[:], MP[:, :, 0, :], ALU.subtract))
                link(dve.tensor_copy(MP[:, :, 1, :], MX[:]))
                dve.tensor_tensor(MP[:, :, 2, :], MX[:], MP[:, :, 1, :], ALU.subtract).then_inc(sem["mparts"], 1)
                link.end()


            def softmax2(b, nxt):
                link = Chain(dve, sem, "dve_o", b)
                for q in range(2):
                    if nxt:
                        for k in range(*((0, FIRST_HALF), (FIRST_HALF, PREP_STEPS))[q]):
                            prepare(b + 1, k)
                    dve.wait_ge(sem["nat2"], at("nat2", b, q + 1))
                    src = MISC[:].rearrange("p (g h k c) -> p g h k c", g=2, h=TH, c=32)
                    link(dve.reciprocal(DEN[:].rearrange("p a b c -> p (a b c)")[:, 0:16],
                                        MISC[:].rearrange("p (k c) -> p k c", c=32)[:, :, DH]))
                    for g in range(2):
                        den = DEN[:].rearrange("p a b c -> p (a b c)")[:, 8 * g:8 * g + 8].rearrange(
                            "p (h k) -> p h k", h=TH)
                        last = dve.tensor_tensor(ON[:, :, 8 * q + g:8 * q + g + 7:2, :], src[:, g, :, :, 0:DH],
                                                 den.unsqueeze(3).to_broadcast([P, TH, 4, DH]), ALU.mult)
                        if g:
                            last.then_inc(sem["nat2_read"], 1)
                    dve.wait_ge(sem["nat2_read"], at("nat2_read", b, q + 1))
                on = ON[:].rearrange("p h n d -> p h (n d)")
                for t in range(TH):
                    link(dve.bn_stats(BN[:, t, :], on[:, t, :]), carrier=sem["bn_steps"])
                for t in range(TH):
                    link(dve.bn_aggr(BA[:, t, :], BN[:, t, :]), carrier=sem["bn_steps"])
                dve.tensor_copy(OST[:, 1, :], BA[:, :, 1]).then_inc(sem["on_var"], 1)
                dve.wait_ge(sem["on_rstd"], at("on_rstd", b, 1))
                for t in range(TH):
                    link(dve.tensor_scalar(on[:, t, :], on[:, t, :], BA[:, t, 0:1], OST[:, 2, t:t + 1],
                                           ALU.subtract, ALU.mult))
                link(dve.tensor_tensor(on, on, GAM[:].unsqueeze(1).to_broadcast([P, TH, D]), ALU.mult))
                link(dve.tensor_tensor(on, on, BET[:].unsqueeze(1).to_broadcast([P, TH, D]), ALU.add))
                link(dve.tensor_reduce(out=OST[:, 0, :], in_=on, axis=AX.X, op=ALU.max,
                                       apply_absolute_value=True))
                link(dve.tensor_tensor(OSQ[:], on, on, ALU.mult))
                dve.tensor_reduce(out=OST[:, 3, :], in_=OSQ[:], axis=AX.X, op=ALU.add).then_inc(sem["on_ms"], 1)
                dve.wait_ge(sem["on_r"], at("on_r", b, 1))
                quant_scales(link, OST, 4)
                link(dve.tensor_scalar(OST[:, 7, :], OST[:, 7, :], WSC[:, 3:4], None, ALU.mult))
                link(dve.tensor_tensor(OSQ[:], on, bcast(OST[:, 6, :], D), ALU.mult))
                dve.tensor_scalar(OQB[:], OSQ[:], MAGIC, MAGIC, ALU.add, ALU.subtract).then_inc(sem["oq"], 1)
                dve.wait_ge(sem["y2"], at("y2", b, 1))
                link(dve.tensor_tensor(RES[:], S[1][:, 0:T].rearrange("p (h d) -> p h d", d=D),
                                       bcast(OST[:, 7, :], D), ALU.mult))
                link(dve.tensor_tensor(RES[:], RES[:], X1[:], ALU.add))
                layer_norm(b, link, RES, LST, X2, "ln2_var", "ln2_rstd", "x2")
                link.end()


            def ffn(b, k):
                if k == 3:
                    link["route"] = Chain(dve, sem, "dve_route", b)
                    dve.wait_ge(sem["logits"], at("logits", b, 1))
                    dve.tensor_copy(LG[:, 1], S[1][:, 0:8 * TH].rearrange("p (h e) -> p h e", e=8)
                                    ).then_inc(sem["lg_sb"], 1)
                    dve.wait_ge(sem["lg_sb"], at("lg_sb", b, 1))
                    dve.tensor_reduce(out=LM[:, 0, :], in_=LG[:, 1], axis=AX.X, op=ALU.max).then_inc(sem["lmax"], 1)
                    dve.wait_ge(sem["lmax"], at("lmax", b, 1))
                    link["route"](dve.tensor_tensor(LG[:, 0], LG[:, 1], bcast(LM[:, 0, :], 8), ALU.is_equal))
                    link["route"](dve.tensor_tensor(LG[:, 0], LG[:, 0], IOTA8[:], ALU.mult))
                    link["route"](dve.tensor_reduce(out=LM[:, 2, :], in_=LG[:, 0], axis=AX.X, op=ALU.max))
                    link["route"](dve.tensor_tensor(LG[:, 0], IOTA8[:], bcast(LM[:, 2, :], 8), ALU.is_equal))
                elif k == 7:
                    dve.wait_ge(sem["lexp"], at("lexp", b, 1))
                    link["route"](dve.tensor_scalar(LM[:, 3, :], LM[:, 1, :], 1.0, None, ALU.add))
                    link["route"](dve.reciprocal(LM[:, 3, :], LM[:, 3, :]))
                    dve.tensor_tensor(CR[:], LG[:, 0], bcast(LM[:, 3, :], 8), ALU.mult).then_inc(sem["route"], 1)
                    link["route"].end()
                e = expert(k, "inputs")
                if e:
                    dve.wait_ge(sem["bc"], at("bc", b, e))
                    if e >= 3:
                        dve.wait_ge(sem["up"], at("up", b, e - 1))
                    dve.tensor_tensor(XE[:, e % 2, :], S[1][:, 0:T], X2T[:], ALU.mult).then_inc(sem["xe"], 1)
                e = expert(k, "hidden")
                if e is not None:
                    dve.wait_ge(sem["silu"], at("silu", b, e + 1))
                    dve.wait_ge(sem["up"], at("up", b, e + 1))
                    if e >= 2:
                        dve.wait_ge(sem["down"], at("down", b, e - 1))
                    dve.tensor_tensor(HT[:, e % 2, :], Z[2][:], SG[:, e % 2, :], ALU.mult).then_inc(sem["hT"], 1)
                if k == FFN_STEPS - 1:
                    chain = Chain(dve, sem, "dve_ln3", b)
                    dve.wait_ge(sem["down"], at("down", b, E))
                    chain(dve.tensor_tensor(RES[:].rearrange("p h d -> p (h d)"), S[0][:, 0:T],
                                            X2[:].rearrange("p h d -> p (h d)"), ALU.add))
                    dve.wait_ge(sem["out_free"], at("out_free", b, 1))
                    layer_norm(b, chain, RES, LST3, OUT, "ln3_var", "ln3_rstd", "out_ready")
                    chain.end()

            def row(b, first=False, last=False):
                attention1(b)
                output1(b)
                queries2(b)
                maxima(b, with_ffn=not first)
                softmax2(b, nxt=not last)

            for k in range(PREP_STEPS):
                prepare(0, k)
            row(0, first=True)
            with dve.Fori(1, B - 1) as b:
                row(b)
            row(B - 1, last=True)
            for k in range(FFN_STEPS):
                ffn(B - 1, k)


def _layout(inputs):
    f = {k: np.ascontiguousarray(np.asarray(v)) for k, v in inputs.items()}
    perm_a = np.concatenate([np.arange(0, DH, 2), np.arange(1, DH, 2)])
    perm_b = np.concatenate([np.arange(1, DH, 2), np.arange(0, DH, 2)])

    def cols(w, perm):
        w = w.reshape(w.shape[:-1] + (-1, NH // 2, 2, DH))[..., perm]
        return np.moveaxis(w, -3, -1).reshape(w.shape[:-4] + (-1,))

    def rows(w, group):
        return w.reshape(-1, 2, group, DH, D).transpose(1, 3, 0, 2, 4).reshape(w.shape)

    wq, bq, wk, bk = (f["L0_attn_" + n] for n in ("W_Q", "b_Q", "W_K", "b_K"))
    inv_freq = (1.0 / 10000.0 ** (np.arange(0, DH, 2, dtype=np.float32) / DH)).astype(np.float32)
    angle = (np.arange(T, dtype=np.float32)[:, None] * inv_freq[None, :]).astype(np.float32)
    cos, sin = np.cos(angle).T, np.sin(angle).T
    rope_cos = np.tile(np.repeat(np.concatenate([cos, cos]), NH // 2, axis=0), (2, 1)).astype(np.float32)
    rope_sin = np.tile(np.repeat(np.concatenate([-sin, sin]), NH // 2, axis=0), (2, 1)).astype(np.float32)
    r_of, n_of = np.arange(P) // 64, np.arange(P) % (NH // 2)
    heads = ((r_of[:, None] == r_of) & (n_of[:, None] == n_of)).astype(np.float32)

    def experts(shared, routed):
        return np.concatenate([shared[None], routed])

    g, u = (experts(f["L0_ffn_shared_" + n], f["L0_ffn_r_" + n]) for n in ("gate", "up"))
    dn = experts(f["L0_ffn_shared_down"], f["L0_ffn_r_down"])
    return dict(
        x=f["x"], ctx_t=f["ctx_1024"],
        wqA=cols(wq, perm_a), wqB=cols(wq, perm_b), wkA=cols(wk, perm_a), wkB=cols(wk, perm_b),
        wv=f["L0_attn_W_V"],
        bqA=cols(bq, perm_a).reshape(BR, P).T, bqB=cols(bq, perm_b).reshape(BR, P).T,
        bkA=cols(bk, perm_a).reshape(P, 1), bkB=cols(bk, perm_b).reshape(P, 1),
        bv=f["L0_attn_b_V"], sinks=f["L0_attn_sink_scalars"], vnull=f["L0_attn_v_nulls"].reshape(-1),
        wo=f["L0_attn_W_O"].transpose(1, 0, 2), wob=f["L0_attn_W_O_bias"].reshape(-1),
        w2q=rows(f["L0_xattn_wq"], 2), w2kv=np.concatenate([rows(f["L0_xattn_wk"], 1), f["L0_xattn_wv"]]),
        w2o=f["L0_xattn_wo"], gamma=f["L0_xattn_ln_gamma"], beta=f["L0_xattn_ln_beta"],
        gate_w=f["L0_ffn_gate_w"].T,
        ffn_g=g.transpose(2, 0, 1), ffn_u=u.transpose(2, 0, 1),
        ffn_d=dn.reshape(E, D, FC, P).transpose(3, 0, 2, 1),
        rope_cos=rope_cos, rope_sin=rope_sin, heads=heads, ident=np.eye(P, dtype=np.float32),
    )


def kernel(**inputs):
    import concourse.bacc as _bacc
    from concourse.bass_utils import run_bass_kernel_spmd as _run

    nc = _bacc.Bacc("TRN2", target_bir_lowering=False, num_devices=1, dynamic_dma_scratch_size=1024)
    arrays, args = {}, {}
    for name, a in _layout(inputs).items():
        a = np.ascontiguousarray(a)
        arrays["in_" + name] = a
        args[name] = nc.dram_tensor("in_" + name, a.shape, mybir.dt.from_np(a.dtype), kind="ExternalInput").ap()
    args["out"] = nc.dram_tensor("out_0", (B, T, D), F32, kind="ExternalOutput").ap()
    build(nc, **args)
    r = _run(nc, [arrays], core_ids=[0])
    return r.results[0]["out_0"]
```

```python
from contextlib import ExitStack
import math

import numpy as np

import concourse.bass as bass
from concourse import mybir

F32 = mybir.dt.float32
F16 = mybir.dt.float16
BF16 = mybir.dt.bfloat16
ALU = mybir.AluOpType
ACT = mybir.ActivationFunctionType
AX = mybir.AxisListType

P = 128
D = 128
B = 8
T = 256
TH = T // P
BR = 4
NH = 16
DH = 8
KV = 8
S2 = 1601
NT = 13
LAST = S2 - (NT - 1) * P
E = 9
F = 256
FC = F // P
CAP = 2.0 ** 60
POOL_BRANCHES = [0 if h >= NH - 4 else (2, 2, 1, 1)[h % 4] for h in range(NH)]
DVE_BRANCHES = [(h, br) for h in range(NH) for br in range(BR - POOL_BRANCHES[h])]
DVE_TO_TILE = 4 * BR - sum(POOL_BRANCHES[0:4])
NO_MISC = (44, 80)
LOWEST = -3.0e38
MAGIC = 1.5 * 2.0 ** 23
GATE = math.pi / math.sqrt(3.0)
KGAIN = 16.0
ZSCALE = DH ** -0.5 / KGAIN
MCOLS = 401
CHUNKS = (0, 400, 800, 1200)
assert CHUNKS[-1] + MCOLS == S2
M_ROW = 32
KEY_ROWS = ((0, 3, 0), (1, 1, 24), (1, 2, 35))
QUERY_ROWS = ((slice(0, 3), 0), (slice(0, 1), 24), (slice(1, 3), 35))
PREP_FIRST = 4
PREP_AT = {u: k + PREP_FIRST for k, u in enumerate((4, 5, 12, 14, 18, 20, 30, 32, 37, 39, 48, 52, 53))}
PREP_STEPS = PREP_FIRST + len(PREP_AT)
CTX_AT = {1: 0, 5: 1, 9: 2, 17: 3, 25: 4}
CTX_STEPS = len(CTX_AT)
TAIL_AT = {1: (0,), 3: (1,), 4: (2,), 6: (3,), 7: (4,), 8: (5,), 9: (6,), 10: (7, 8), 11: (9,)}
TAIL_STEPS = 10
EXPERT_EVERY = 12
FFN_STEPS = EXPERT_EVERY * 8 + 22
FFN_BESIDE = 36
FFN_FIRST = FFN_BESIDE + 13
MWIDE = 4 * ((FFN_STEPS - FFN_FIRST) // 4 + 1)
BESIDE = {h: (9 * j, 9 * j + 9) for j, h in enumerate(range(NH - 4, NH))}
ROUTE_AT = {15: 0, 16: 1, 17: 2, 18: 3, 19: 4, 20: 5}
EXPERT_AT = dict(weight=0, inputs=2, gate=6, up=8, silu=9, hidden=12, down0=15, down1=17)
NZ = 3 * NH
NX = KV * NT
NM = NH * TH * len(CHUNKS)
N_WEIGHTS = 27

PER = dict(
    x_in=16, ctx_in=32,
    xT_ps=1, xT_sb=1, kproj=1, vproj=1, qproj=4, qproj_read=4, v1_ready=1,
    ksq_sb=1, knorm_ps=1, knorm_sb=1, krs=1, kparts=1, kscr=16, kstack=4 * 16,
    qparts=1, qscr=16, qstack=4 * 16,
    z=NZ, zexp=NZ, zcap=NZ, zln=NZ, zmax=NZ, gated=NH, thr=len(DVE_BRANCHES),
    thr_pool=2 * sum(POOL_BRANCHES), masked=NH,
    masking=NH + sum(POOL_BRANCHES), bn_steps=16,
    av1=4, av1_sb=8, nat1=8, nat1_read=8, ctxT_ps=2, ctxT_sb=2, y1=1,
    ln1_var=1, ln1_rstd=1, x1=1,
    csq=1, cn_ms=1, cn_r=1, yq=1, yT_ps=2, yT_sb=2, kvn=4, kvn_read=4, khl=1, kT_ps=2, kT_sb=2,
    k2scr=16, k2stack=6 * 16,
    qn_ms=1, qn_r=1, xq=1, xqT_ps=1, xqT_sb=1, qn=1, q2parts=1, q2T_ps=1, q2T_sb=1,
    q2scr=16, q2stack=6 * 16,
    mx=NM, mx_copy=NM // 2, mx_read=NM // 2, mparts=1, mT_ps=1, mT_sb=1, mscr=16, mstack=2 * 16,
    s=NX, sexp=NX, av2=NX // 4, o2_sb=2, nat2=2, nat2_read=2,
    on_var=1, on_rstd=1, on_ms=1, on_r=1, oq=1, oqT_ps=1, oqT_sb=1, y2=1,
    ln2_var=1, ln2_rstd=1, x2=1,
    x2T_ps=1, x2T_sb=1, logits=1, lmax=1, lexp=1, route=1, lg_sb=1, v2_ready=1, mzero=2, mx_head=NH,
    bc=E - 1, xe=E - 1, g=E, up=E, silu=E, hT=E, down=E, ln3_var=1, ln3_rstd=1,
    out_ready=1, out_done=16, out_free=1,
    dve_prep=19, dve_nat=24, dve_ln1=6, dve_ctx=9, dve_q=14, dve_m=3, dve_o=27, dve_route=6, dve_ln3=6,
    act_root=5, key_root=1, ctx_root=1, ffn_root=1, dve_setup=44,
)


def at(name, b, k):
    return b * PER[name] + k


def expert(k, stage):
    e, rest = divmod(k - EXPERT_AT[stage], EXPERT_EVERY)
    return e if rest == 0 and 0 <= e < E else None


class Chain:

    def __init__(self, eng, sem, name, b):
        self.eng, self.sem, self.name, self.b, self.k = eng, sem[name], name, b, 0

    def __call__(self, ins, carrier=None):
        self.k += 1
        ins.then_inc(self.sem, 1)
        self.eng.wait_ge(self.sem, at(self.name, self.b, self.k))
        if carrier is not None:
            self.eng.sem_inc(carrier, 1)

    def end(self):
        assert self.k == PER[self.name], (self.name, self.k)


def build(nc, x, ctx_t, wqA, wqB, wkA, wkB, wv, bqA, bqB, bkA, bkB, bv, sinks, vnull, wo, wob,
          w2q, w2kv, w2o, gamma, beta, gate_w, ffn_g, ffn_u, ffn_d, rope_cos, rope_sin, heads, ident, out):
    ctx = ExitStack()
    with ctx:
        def sb(name, shape, dt=F32):
            return ctx.enter_context(nc.sbuf_tensor(name, shape, dt))

        def bank(name):
            return ctx.enter_context(nc.psum_tensor(name, [P, 512], F32))

        sem = {n: ctx.enter_context(nc.semaphore("s_" + n)) for n in PER}
        weights_in = ctx.enter_context(nc.semaphore("weights_in"))
        pool_setup = ctx.enter_context(nc.semaphore("pool_setup"))
        abs_ready = ctx.enter_context(nc.semaphore("abs_ready"))
        abs_sums = ctx.enter_context(nc.semaphore("abs_sums"))
        ternary = ctx.enter_context(nc.semaphore("ternary"))
        ternary_T = ctx.enter_context(nc.semaphore("ternary_T"))
        setup_done = ctx.enter_context(nc.semaphore("setup_done"))

        identF, identB, identH = sb("identF", [P, P]), sb("identB", [P, P], BF16), sb("identH", [P, P], F16)
        WQA, WQB = sb("WQA", [P, BR * P]), sb("WQB", [P, BR * P])
        WKA, WKB, WV = sb("WKA", [P, P]), sb("WKB", [P, P]), sb("WV", [P, P])
        BQA, BQB = sb("BQA", [P, BR]), sb("BQB", [P, BR])
        BKA, BKB, BV = sb("BKA", [P, 1]), sb("BKB", [P, 1]), sb("BV", [P, P])
        COS, SIN = sb("COS", [P, T]), sb("SIN", [P, T])
        SINKS = sb("SINKS", [P, BR * NH])
        SINKD = sb("SINKD", [P, BR * NH])
        SV = sb("SV", [P, BR * NH, DH])
        PR2_ = sb("PR2", [P, 8 * 512])
        WO = sb("WO", [P, BR, P])
        WOB = PR2_[:, 0:BR * P].rearrange("p (n d) -> p n d", n=BR)
        BMEAN = sb("BMEAN", [P, P])
        W2 = PR2_[:, BR * P:(BR + 3) * P].rearrange("p (n d) -> p n d", n=3)
        W2N = sb("W2N", [P, 3, P], BF16)
        W2T = sb("W2T", [P, 3, P], BF16)
        ABS = sb("ABS", [P, 4])
        WSC, WINV = sb("WSC", [P, 4]), sb("WINV", [P, 4])
        QC = sb("QC", [P, 1])
        GAM, BET = sb("GAM", [P, P]), sb("BET", [P, P])
        GW = sb("GW", [P, 8])
        FG, FU, FD = sb("FG", [P, E, F]), sb("FU", [P, E, F]), sb("FD", [P, E, FC, P])
        ONES = sb("ONES", [P, P])
        HEADS = sb("HEADS", [P, P])
        IOTA8 = sb("IOTA8", [P, TH, 8])
        EPS_LN, EPS_RMS, ONE1 = sb("EPS_LN", [P, 1]), sb("EPS_RMS", [P, 1]), sb("ONE1", [P, 1])

        XIN, CIN = sb("XIN", [P, TH, D]), sb("CIN", [P, NT, D])
        XT, KR, TB, KSQ, KRS = (sb("XT", [P, T]), sb("KR", [P, T]), sb("TB", [P, 2, T]),
                                sb("KSQ", [P, T]), sb("KRS", [P, T]))
        KHL = sb("KHL", [P, 2, T], F16)
        PR2 = PR2_[:].rearrange("p (n t) -> p n t", n=8)
        CTX = PR2_[:, 0:1024].rearrange("p (h n t) -> p h n t", h=TH, n=BR)
        O1 = PR2_[:, 1024:2048].rearrange("p (h t) -> p h t", h=TH)
        CTXT = O1
        SG = PR2_[:, 2048:3072].rearrange("p (s t) -> p s t", s=2)
        HT = PR2_[:, 3072:4096].rearrange("p (s t) -> p s t", s=2)
        XE = sb("XE", [P, 2, T])
        PRB_ = sb("PRB", [P, 8 * 3 * BR * P])
        PRB = PRB_[:].rearrange("p (h j b t) -> p h j b t", h=8, j=3, b=BR)
        QR = PRB_[:, 0:TH * BR * P].rearrange("p (h n t) -> p h n t", h=TH, n=BR)
        QRES = PRB_[:, TH * BR * P:2 * TH * BR * P].rearrange("p (h n t) -> p h n t", h=TH, n=BR)
        QABC = PRB_[:, 2 * TH * BR * P:4 * TH * BR * P].bitcast(BF16)[:, 0:3 * TH * BR * P].rearrange(
            "p (i h n t) -> p i h n t", i=3, h=TH, n=BR)
        V1 = sb("V1", [P, TH, NH, DH + 1])
        KS1 = sb("KS1", [P, NH, T], F16)
        QS1 = sb("QS1", [P, NH // 2, TH * BR * P], BF16)
        KEEP = sb("KEEP", [P, 3, P])
        DEN = sb("DEN", [P, 2, 4, 4])
        XB = sb("XB", [P, TH, D])
        RES, LST = sb("RES", [P, TH, D]), sb("LST", [P, 4, TH])
        X1, X2 = sb("X1", [P, TH, D]), sb("X2", [P, TH, D])
        CQB, CST = sb("CQB", [P, NT, D], BF16), sb("CST", [P, 8, NT])
        CSQ = sb("CSQ", [P, NT, D])
        K32 = CSQ[:].rearrange("p n d -> p (n d)")[:, 0:NT * 64].rearrange("p (n d) -> p n d", d=64)
        KHN = CSQ[:].rearrange("p n d -> p (n d)")[:, NT * 64:].bitcast(F16).rearrange(
            "p (n i d) -> p n i d", i=2, d=64)
        KT2 = sb("KT2", [P, NT * P], F16)
        YT = KT2[:].bitcast(BF16)
        V2N, V2 = sb("V2N", [P, NT, KV, DH]), sb("V2", [P, NT, KV, DH + 1])
        KS2 = sb("KS2", [P, KV, NT * P], F16)
        QST, OST = sb("QST", [P, 8, TH]), sb("OST", [P, 8, TH])
        QSQ = sb("QSQ", [P, TH, D])
        OSQ = QSQ
        QQB, QQT = sb("QQB", [P, TH, D], BF16), sb("QQT", [P, T], BF16)
        OQB, OQT = sb("OQB", [P, TH, D], BF16), sb("OQT", [P, T], BF16)
        Q32 = sb("Q32", [P, TH, D])
        QP = sb("QP", [P, TH, 3, D], BF16)
        QT2 = sb("QT2", [P, 3, T], BF16)
        QS2 = sb("QS2", [P, KV // 2, 2, T], BF16)
        MX = sb("MX", [P, TH, NH])
        MP, MT = sb("MP", [P, TH, 3, NH], BF16), sb("MT", [48, T], BF16)
        O2 = sb("O2", [P, 512])
        ON = sb("ON", [P, TH, NH, DH])
        X2T = sb("X2T", [P, T])
        LG, LM = sb("LG", [P, 2, TH, 8]), sb("LM", [P, 4, TH])
        CR = sb("CR", [P, TH, 8])
        LST3 = sb("LST3", [P, 4, TH])
        OUT = sb("OUT", [P, TH, D])
        BN, BA = sb("BN", [P, TH, 6]), sb("BA", [P, TH, 2])

        k_scr = nc.dram_tensor("k_scr", (2, P, T), F16).ap()
        q_scr = nc.dram_tensor("q_scr", (3, P, TH * BR * P), BF16).ap()
        k2_scr = nc.dram_tensor("k2_scr", (P, NT * P), F16).ap()
        q2_scr = nc.dram_tensor("q2_scr", (3, P, T), BF16).ap()
        m_scr = nc.dram_tensor("m_scr", (3 * NH, T), BF16).ap()

        Z = [bank(f"Z{i}") for i in range(3)]
        S = [bank(f"S{i}") for i in range(2)]
        ZR = (*Z, S[0])
        M = bank("M")
        ACC = bank("ACC")
        MISC = bank("MISC")

        SR = [(*S, M)[u % 3] if u in range(*NO_MISC) else (*S, M, MISC)[u % 4] for u in range(NX)]
        MR = [(M, MISC, ACC, S[1])[u % 4] if u < MWIDE else (M, MISC, ACC, S[1], *Z)[(u - MWIDE) % 7]
              for u in range(NM)]
        MCOPY = PRB_[:, 0:4 * MCOLS].rearrange("p (s c) -> p s c", s=4)
        MSCAN = PRB_[:, 4 * MCOLS:20 * MCOLS].rearrange("p (s c) -> p s c", s=16)

        KV_BANKS = (Z[2], Z[0], Z[1], Z[2])

        block = ctx.enter_context(nc.Block())

        def ts(v):
            return slice(v * P, (v + 1) * P)

        def bcast(ap, n):
            return ap.unsqueeze(2).to_broadcast([P, ap.shape[1], n])

        @block.sync
        def _(sp):
            once = [(identF[:], ident), (WQA[:], wqA), (WQB[:], wqB), (WKA[:], wkA), (WKB[:], wkB),
                    (WV[:], wv), (BQA[:], bqA), (BQB[:], bqB), (BKA[:], bkA), (BKB[:], bkB),
                    (BV[:], bv.partition_broadcast(P)), (HEADS[:], heads), (COS[:], rope_cos), (SIN[:], rope_sin),
                    (SINKS[:], sinks.partition_broadcast(P)),
                    (SV[:].rearrange("p h d -> p (h d)"), vnull.partition_broadcast(P)),
                    (WO[:], wo), (PR2_[:, 0:BR * P], wob.partition_broadcast(P)),
                    (W2[:, 0, :], w2q), (W2[:, 1, :], w2kv), (W2[:, 2, :], w2o),
                    (GAM[:], gamma.partition_broadcast(P)), (BET[:], beta.partition_broadcast(P)),
                    (GW[:], gate_w), (FG[:], ffn_g), (FU[:], ffn_u), (FD[:], ffn_d)]
            assert len(once) == N_WEIGHTS
            for dst, src in once:
                sp.dma_start(dst, src).then_inc(weights_in, 16)
            sp.wait_ge(setup_done, 1)

            def load(b):
                sp.dma_start(XIN[:], x[b].rearrange("(h p) d -> p h d", p=P)).then_inc(sem["x_in"], 16)
                sp.dma_start(CIN[:, 0:NT - 1, :], ctx_t[b, 0:(NT - 1) * P, :].rearrange(
                    "(i p) d -> p i d", p=P)).then_inc(sem["ctx_in"], 16)
                sp.dma_start(CIN[0:LAST, NT - 1, :], ctx_t[b, (NT - 1) * P:S2, :]).then_inc(
                    sem["ctx_in"], 16)

            def thrice(rows, r, n):
                own = rows.rearrange("(r d n) t -> r d (n t)", r=2, n=n)[r]
                return own.unsqueeze(0).to_broadcast([3] + list(own.shape))

            def parts_of(scratch, r, parts):
                return scratch.rearrange("i (r d n) t -> r i d (n t)", r=2, d=DH)[r][parts]

            def stack_stage1(b):
                sp.wait_ge(sem["kparts"], at("kparts", b, 1))
                sp.dma_start(k_scr.rearrange("n p t -> p n t"), KHL[:]).then_inc(sem["kscr"], 16)
                sp.wait_ge(sem["kscr"], at("kscr", b, 16))
                for r in range(2):
                    for part in range(2):
                        row = 64 * r + 24 * part
                        sp.dma_start(KS1[row:row + 24, 8 * r:8 * r + 8, :], thrice(k_scr[part], r, 8)
                                     ).then_inc(sem["kstack"], 16)
                sp.wait_ge(sem["qparts"], at("qparts", b, 1))
                sp.dma_start(q_scr.rearrange("n p t -> p n t"),
                             QABC[:].rearrange("p n h b t -> p n (h b t)")).then_inc(sem["qscr"], 16)
                sp.wait_ge(sem["qscr"], at("qscr", b, 16))
                for r in range(2):
                    for row in (64 * r, 64 * r + 24):
                        sp.dma_start(QS1[row:row + 24, :, :], parts_of(q_scr, r, slice(0, 3))
                                     ).then_inc(sem["qstack"], 16)
                sp.wait_ge(sem["kT_sb"], at("kT_sb", b, 2))
                sp.dma_start(k2_scr, KT2[:]).then_inc(sem["k2scr"], 16)
                sp.wait_ge(sem["k2scr"], at("k2scr", b, 16))

            def stack_stage2(b, first):
                if not first:
                    sp.wait_ge(sem["s"], at("s", b - 1, NX))
                for r in range(2):
                    for part, n, row in KEY_ROWS:
                        sp.dma_start(KS2[64 * r + row:64 * r + row + 8 * n, 4 * r:4 * r + 4, :],
                                     thrice(k2_scr[64 * part:64 * part + 64, :], r, 4)[0:n]
                                     ).then_inc(sem["k2stack"], 16)

            def stack_queries2(b):
                sp.wait_ge(sem["q2T_sb"], at("q2T_sb", b, 1))
                sp.dma_start(q2_scr.rearrange("n p t -> p n t"), QT2[:]).then_inc(sem["q2scr"], 16)
                sp.wait_ge(sem["q2scr"], at("q2scr", b, 16))
                for r in range(2):
                    for parts, row in QUERY_ROWS:
                        n = 8 * (parts.stop - parts.start)
                        sp.dma_start(QS2[64 * r + row:64 * r + row + n, :, :, :], parts_of(q2_scr, r, parts)
                                     ).then_inc(sem["q2stack"], 16)
                sp.wait_ge(sem["mT_sb"], at("mT_sb", b, 1))
                sp.dma_start(m_scr, MT[:]).then_inc(sem["mscr"], 16)
                sp.wait_ge(sem["mscr"], at("mscr", b, 16))
                for r in range(2):
                    row = 64 * r + M_ROW
                    sp.dma_start(QS2[row:row + 3, :, :, :], m_scr.rearrange(
                        "(i r n g) t -> r i n g t", i=3, r=2, g=2)[r]).then_inc(sem["mstack"], 16)

            def store(b):
                sp.wait_ge(sem["out_ready"], at("out_ready", b, 1))
                sp.dma_start(out[b].rearrange("(h p) d -> p h d", p=P), OUT[:]).then_inc(
                    sem["out_done"], 16)

            def row(b, first=False, last=False):
                stack_stage2(b, first)
                if not last:
                    load(b + 1)
                stack_queries2(b)
                if not first:
                    store(b - 1)
                if not last:
                    stack_stage1(b + 1)
                if not first:
                    sp.wait_ge(sem["out_done"], at("out_done", b - 1, 16))
                    sp.sem_inc(sem["out_free"], 1)

            load(0)
            sp.sem_inc(sem["out_free"], 1)
            stack_stage1(0)
            row(0, first=True)
            with sp.Fori(1, B - 1) as b:
                row(b)
            row(B - 1, last=True)
            store(B - 1)
            sp.wait_ge(sem["out_done"], at("out_done", B - 1, 16))

        @block.gpsimd
        def _(pool):
            pool.memset(ONES[:], 1.0).then_inc(pool_setup, 1)
            pool.iota(IOTA8[:], pattern=[[0, TH], [-1, 8]], base=8, channel_multiplier=0,
                      allow_small_or_imprecise_dtypes=True).then_inc(pool_setup, 1)

            def square_context(b):
                pool.wait_ge(sem["ctx_in"], at("ctx_in", b, 32))
                pool.tensor_tensor(CSQ[:], CIN[:], CIN[:], ALU.mult).then_inc(sem["csq"], 1)

            def mask(b):
                for h in range(NH):
                    for br in range(BR - POOL_BRANCHES[h], BR):
                        done = 2 * (sum(POOL_BRANCHES[:h]) + br - BR + POOL_BRANCHES[h])
                        pool.wait_ge(sem["gated"], at("gated", b, h + 1))
                        pool.sem_inc(sem["masking"], 1)
                        v = PRB[:, h % 8, :, br, :]
                        sink = SINKS[:, NH * br + h:NH * br + h + 1]
                        pool.tensor_scalar(KEEP[:], v, sink, None, ALU.is_ge).then_inc(sem["thr_pool"], 1)
                        pool.wait_ge(sem["thr_pool"], at("thr_pool", b, done + 1))
                        pool.tensor_tensor(v, v, KEEP[:], ALU.mult).then_inc(sem["thr_pool"], 1)
                        pool.wait_ge(sem["thr_pool"], at("thr_pool", b, done + 2))
                    pool.wait_ge(sem["thr"], at("thr", b, sum(BR - n for n in POOL_BRANCHES[:h + 1])))
                    pool.sem_inc(sem["masking"], 1)
                    for j in (0, 2):
                        v = PRB[:, h % 8, j, :, :]
                        i = pool.affine_select(out=v, in_=v, compare_op=ALU.is_ge, fill=0.0, base=0,
                                               pattern=[[0, BR], [1, P]], channel_multiplier=-1)
                    i.then_inc(sem["masked"], 1)

            square_context(0)
            mask(0)
            with pool.Fori(1, B) as b:
                square_context(b)
                mask(b)

        @block.scalar
        def _(act):
            def rsqrt(b, k, dst, src, scale, bias, ready, done, root="act_root"):
                act.wait_ge(sem[ready], at(ready, b, 1))
                act.activation(dst, src, ACT.Ln, bias=bias, scale=scale).then_inc(sem[root], 1)
                act.wait_ge(sem[root], at(root, b, k))
                act.activation(dst, dst, ACT.Exp, scale=-0.5).then_inc(sem[done], 1)

            def prepare(b, k):
                if k == 1:
                    act.wait_ge(sem["xT_ps"], at("xT_ps", b, 1))
                    act.activation(XT[:], Z[0][:, 0:T], ACT.Copy).then_inc(sem["xT_sb"], 1)
                elif k == 7:
                    act.wait_ge(sem["knorm_sb"], at("knorm_sb", b, 1))
                    act.activation(KRS[:], KSQ[:], ACT.Ln).then_inc(sem["key_root"], 1)
                    act.wait_ge(sem["key_root"], at("key_root", b, 1))
                    act.activation(KRS[:], KRS[:], ACT.Exp, scale=-0.5).then_inc(sem["krs"], 1)
                if k in (1, 15):
                    name, dst, dt, banks = ("yT", YT, BF16, (Z[1], Z[2])) if k == 1 else ("kT", KT2, F16, (Z[0], Z[1]))
                    for c, (t0, t1) in enumerate(((0, 8), (8, NT))):
                        act.wait_ge(sem[name + "_ps"], at(name + "_ps", b, c + 1))
                        act.activation(dst[:, t0 * P:t1 * P], banks[c][:].bitcast(dt)[:, 0:(t1 - t0) * P],
                                       ACT.Copy).then_inc(sem[name + "_sb"], 1)

            def quantise_context(b, k):
                if k == 1:
                    rsqrt(b, 1, CST[:, 2, :], CST[:, 1, :], 1.0 / D, EPS_RMS[:], "cn_ms", "cn_r", "ctx_root")

            def attention1(b, first):
                act.preload_act_table_set("natural_log_exp_and_others")
                act.wait_ge(sem["kvn_read"], at("kvn_read", b, 4))
                if not first:
                    act.wait_ge(sem["av2"], at("av2", b - 1, 2 * NT))
                act.activation(V2[:, :, :, 0:DH], V2N[:], ACT.Copy).then_inc(sem["v2_ready"], 1)

                def z_tile(u):
                    return PRB[:, (u // 3) % 8, u % 3, :, :].rearrange("p b t -> p (b t)")

                def z_exp(u):
                    act.wait_ge(sem["z"], at("z", b, u + 1))
                    act.activation(z_tile(u), ZR[u % 4][:], ACT.Exp, scale=ZSCALE).then_inc(sem["zexp"], 1)

                def z_ln(u):
                    act.wait_ge(sem["zcap"], at("zcap", b, u + 1))
                    act.activation(z_tile(u), z_tile(u), ACT.Ln, bias=ONE1[:]).then_inc(sem["zln"], 1)

                for g in range(NH // 4):
                    for u in range(12 * g, 12 * g + 12):
                        for k in TAIL_AT.get(u, ()) if not first else ():
                            tail(b - 1, k)
                        if not first and u in ROUTE_AT:
                            route(b - 1, ROUTE_AT[u])
                        z_exp(u)
                        if u > 12 * g:
                            z_ln(u - 1)
                    z_ln(12 * g + 11)
                    for h in range(4 * g, 4 * g + 4):
                        act.wait_ge(sem["zmax"], at("zmax", b, 3 * h + 3))
                        v = PRB[:, h % 8, :, :, :].rearrange("p j b t -> p (j b t)")
                        act.activation(v, v, ACT.Silu, scale=GATE).then_inc(sem["gated"], 1)
                        if h >= NH - 4 and not first:
                            for k in range(*BESIDE[h]):
                                ffn(b - 1, k)
                    act.preload_act_table_set("natural_log_exp_and_others")
                    if g:
                        act.wait_ge(sem["av1"], at("av1", b, g))
                for t in range(TH):
                    act.wait_ge(sem["ctxT_ps"], at("ctxT_ps", b, t + 1))
                    act.activation(CTXT[:, t, :], (MISC, S[1])[t][:], ACT.Copy).then_inc(sem["ctxT_sb"], 1)
                rsqrt(b, 1, LST[:, 3, :], LST[:, 2, :], 1.0, EPS_LN[:], "ln1_var", "ln1_rstd")

            def queries2(b):
                rsqrt(b, 2, QST[:, 2, :], QST[:, 1, :], 1.0 / D, EPS_RMS[:], "qn_ms", "qn_r")
                act.wait_ge(sem["xqT_ps"], at("xqT_ps", b, 1))
                act.activation(QQT[:], MISC[:].bitcast(BF16)[:, 0:T], ACT.Copy).then_inc(sem["xqT_sb"], 1)
                act.wait_ge(sem["q2T_ps"], at("q2T_ps", b, 1))
                act.activation(QT2[:].rearrange("p n t -> p (n t)"), MISC[:].bitcast(BF16)[:, 0:3 * T],
                               ACT.Copy).then_inc(sem["q2T_sb"], 1)

            def ffn(b, k):
                if expert(k, "silu") is not None:
                    e = expert(k, "silu")
                    act.wait_ge(sem["g"], at("g", b, e + 1))
                    if e >= 2:
                        act.wait_ge(sem["hT"], at("hT", b, e - 1))
                    act.activation(SG[:, e % 2, :], Z[0][:], ACT.Silu).then_inc(sem["silu"], 1)
                elif k == FFN_STEPS - 1:
                    act.preload_act_table_set("natural_log_exp_and_others")
                    rsqrt(b, 1, LST3[:, 3, :], LST3[:, 2, :], 1.0, EPS_LN[:], "ln3_var", "ln3_rstd", "ffn_root")

            def route(b, k):
                if k == 1:
                    act.wait_ge(sem["x2T_ps"], at("x2T_ps", b, 1))
                    act.activation(X2T[:], MISC[:, 0:T], ACT.Copy).then_inc(sem["x2T_sb"], 1)
                elif k == 4:
                    act.wait_ge(sem["lmax"], at("lmax", b, 1))
                    act.activation(LM[:, 1, :], LM[:, 0, :], ACT.Exp, scale=-1.0).then_inc(sem["lexp"], 1)

            def maxima(b, with_ffn, nxt):
                for k in range(FFN_BESIDE, FFN_FIRST) if with_ffn else ():
                    ffn(b - 1, k)
                for u in range(NM):
                    if nxt and u in CTX_AT:
                        quantise_context(b + 1, CTX_AT[u])
                    if with_ffn and u + FFN_FIRST < FFN_STEPS:
                        ffn(b - 1, u + FFN_FIRST)
                    if u % 2 == 0:
                        act.wait_ge(sem["mx"], at("mx", b, u + 1))
                        if u >= 8:
                            act.wait_ge(sem["mx_read"], at("mx_read", b, u // 2 - 3))
                        act.activation(MCOPY[:, u // 2 % 4, :], MR[u][:, 0:MCOLS], ACT.Copy
                                       ).then_inc(sem["mx_copy"], 1)

            def softmax2(b, nxt):
                act.wait_ge(sem["mT_ps"], at("mT_ps", b, 1))
                act.activation(MT[:], MISC[0:3 * NH, :].bitcast(BF16)[:, 0:T], ACT.Copy).then_inc(sem["mT_sb"], 1)
                for k in range(PREP_FIRST if nxt else 0):
                    prepare(b + 1, k)
                for u in range(NX):
                    if nxt and u in PREP_AT:
                        prepare(b + 1, PREP_AT[u])
                    n = P if (u % (NX // 2)) // 4 < NT - 1 else LAST
                    act.wait_ge(sem["s"], at("s", b, u + 1))
                    if u >= 8:
                        act.wait_ge(sem["av2"], at("av2", b, u // 4 - 1))
                    act.activation(PR2[0:n, u % 8, :], SR[u][0:n, :], ACT.Exp).then_inc(sem["sexp"], 1)
                    if u in (NX // 2 + 3, NX - 1):
                        act.wait_ge(sem["av2"], at("av2", b, NT if u < NX - 1 else 2 * NT))
                        if u == NX - 1:
                            act.wait_ge(sem["nat2"], at("nat2", b, 1))
                        act.activation(O2[:], ACC[:], ACT.Copy).then_inc(sem["o2_sb"], 1)

            def tail(b, k):
                if k == 1:
                    rsqrt(b, 3, OST[:, 2, :], OST[:, 1, :], 1.0, EPS_LN[:], "on_var", "on_rstd")
                elif k == 3:
                    rsqrt(b, 4, OST[:, 4, :], OST[:, 3, :], 1.0 / D, EPS_RMS[:], "on_ms", "on_r")
                elif k == 6:
                    act.wait_ge(sem["oqT_ps"], at("oqT_ps", b, 1))
                    act.activation(OQT[:], MISC[:].bitcast(BF16)[:, 0:T], ACT.Copy).then_inc(sem["oqT_sb"], 1)
                elif k == 9:
                    rsqrt(b, 5, LST[:, 3, :], LST[:, 2, :], 1.0, EPS_LN[:], "ln2_var", "ln2_rstd")

            def row(b, first=False, last=False):
                attention1(b, first)
                queries2(b)
                maxima(b, with_ffn=not first, nxt=not last)
                softmax2(b, nxt=not last)

            act.wait_ge(setup_done, 1)
            act.preload_act_table_set("natural_log_exp_and_others")
            for k in range(CTX_STEPS):
                quantise_context(0, k)
            for k in range(PREP_STEPS):
                prepare(0, k)
            row(0, first=True)
            with act.Fori(1, B - 1) as b:
                row(b)
            row(B - 1, last=True)
            for k in range(TAIL_STEPS):
                tail(B - 1, k)
            for k in range(len(ROUTE_AT)):
                route(B - 1, k)
            for k in range(FFN_STEPS):
                ffn(B - 1, k)

        @block.tensor
        def _(pe):
            def transposes(dst, parts, idn):
                for i, src in enumerate(parts):
                    n = src.shape[1]
                    last = pe.transpose(dst[0:n, ts(i)], src, idn)
                return last

            pe.wait_ge(pool_setup, 2)
            pe.wait_ge(abs_ready, 4)
            pe.matmul(MISC[:, 0:4], ONES[:], ABS[:], start=True, stop=True).then_inc(abs_sums, 1)
            pe.wait_ge(ternary, 1)
            transposes(MISC[:].bitcast(BF16), [W2N[:, i, :] for i in range(3)], identB[:]).then_inc(ternary_T, 1)
            pe.wait_ge(setup_done, 1)

            def prepare(b, k):
                def queries(br):
                    if br >= 2:
                        pe.wait_ge(sem["qproj_read"], at("qproj_read", b, br - 1))
                    pe.matmul(Z[br % 2][:, 0:T], WQA[:, ts(br)], XT[:], start=True, stop=True)
                    pe.matmul(Z[br % 2][:, T:2 * T], WQB[:, ts(br)], XT[:], start=True,
                              stop=True).then_inc(sem["qproj"], 1)

                def context_projections(c):
                    dst = KV_BANKS[c]
                    for i in range(4 * c, min(4 * c + 4, NT)):
                        last = pe.matmul(dst[:, ts(i - 4 * c)], YT[:, ts(i)], W2T[:, 1, :],
                                         start=True, stop=True)
                    last.then_inc(sem["kvn"], 1)

                if k == 0:
                    pe.wait_ge(sem["x_in"], at("x_in", b, 16))
                    transposes(Z[0], [XIN[:, t, :] for t in range(TH)], identF[:]).then_inc(sem["xT_ps"], 1)
                    pe.wait_ge(sem["yq"], at("yq", b, 1))
                    for bank_, tiles in ((Z[1], range(8)), (Z[2], range(8, NT))):
                        transposes(bank_[:].bitcast(BF16), [CQB[:, i, :] for i in tiles], identB[:]
                                   ).then_inc(sem["yT_ps"], 1)
                elif k == 2:
                    pe.wait_ge(sem["xT_sb"], at("xT_sb", b, 1))
                    pe.wait_ge(sem["yT_sb"], at("yT_sb", b, 2))
                    pe.matmul(Z[1][:, 0:T], WKA[:], XT[:], start=True, stop=True)
                    pe.matmul(Z[1][:, T:2 * T], WKB[:], XT[:], start=True, stop=True).then_inc(sem["kproj"], 1)
                    for t in range(TH):
                        last = pe.matmul(Z[2][:, ts(t)], XT[:, ts(t)], WV[:], start=True, stop=True)
                    last.then_inc(sem["vproj"], 1)
                    queries(0)
                elif k == 4:
                    pe.wait_ge(sem["ksq_sb"], at("ksq_sb", b, 1))
                    pe.wait_ge(sem["v1_ready"], at("v1_ready", b, 1))
                    pe.matmul(Z[2][:, 0:T], HEADS[:], KSQ[:], start=True, stop=True).then_inc(sem["knorm_ps"], 1)
                    queries(1)
                elif k == 6:
                    queries(2)
                elif k == 8:
                    queries(3)
                    pe.wait_ge(sem["knorm_sb"], at("knorm_sb", b, 1))
                    context_projections(0)
                elif k == 10:
                    pe.wait_ge(sem["qproj_read"], at("qproj_read", b, 4))
                    context_projections(1)
                    context_projections(2)
                elif k == 12:
                    pe.wait_ge(sem["kvn_read"], at("kvn_read", b, 1))
                    context_projections(3)
                elif k == 14:
                    pe.wait_ge(sem["khl"], at("khl", b, 1))
                    pe.wait_ge(sem["kvn_read"], at("kvn_read", b, 4))
                    for bank_, tiles in ((Z[0], range(8)), (Z[1], range(8, NT))):
                        transposes(bank_[:].bitcast(F16), [KHN[:, i, :, :].rearrange("p n d -> p (n d)")
                                                           for i in tiles], identH[:]).then_inc(sem["kT_ps"], 1)

            def attention1(b, first):
                pe.wait_ge(sem["kstack"], at("kstack", b, PER["kstack"]))
                pe.wait_ge(sem["qstack"], at("qstack", b, PER["qstack"]))
                pe.wait_ge(sem["kT_sb"], at("kT_sb", b, 2))

                def scores(u):
                    h, j = u // 3, u % 3
                    keys, queries = (0, 0, 1)[j], (0, 1, 1)[j]
                    if u >= 4:
                        pe.wait_ge(sem["zmax"], at("zmax", b, u - 3))
                    pe.matmul(ZR[u % 4][:], KS1[:, 8 * (h % 2) + h // 2, ts(keys)], QS1[:, h // 2, queries * 512:(queries + 1) * 512],
                              start=True, stop=True).then_inc(sem["z"], 1)

                def values(g):
                    pe.wait_ge(sem["masked"], at("masked", b, 4 * g + 4))
                    if g:
                        pe.wait_ge(sem["av1_sb"], at("av1_sb", b, 2 * g))
                    for j in range(3):
                        for h in range(4 * g, 4 * g + 4):
                            c = 32 * (h % 4)
                            last = pe.matmul((ACC, M, M)[j][c:c + DH + 1, :], V1[:, (0, 0, 1)[j], h, :],
                                             PRB[:, h % 8, j, :, :].rearrange("p b t -> p (b t)"),
                                             start=j < 2, stop=j != 1)
                    last.then_inc(sem["av1"], 1)
                    for t in range(TH):
                        pe.wait_ge(sem["av1_sb"], at("av1_sb", b, 2 * g + t + 1))
                        if g:
                            pe.wait_ge(sem["nat1_read"], at("nat1_read", b, 2 * g - 1 + t))
                        transposes((MISC, S[1])[t], [O1[:, t, ts(i)] for i in range(BR)], identF[:]
                                   ).then_inc(sem["nat1"], 1)

                for g in range(NH // 4):
                    for u in range(12 * g, 12 * g + 12):
                        for k in TAIL_AT.get(u, ()) if not first else ():
                            tail(b - 1, k)
                        if not first and u in ROUTE_AT:
                            route(b - 1, ROUTE_AT[u])
                        scores(u)
                    if g:
                        values(g - 1)
                for k in range(FFN_BESIDE if not first else 0):
                    ffn(b - 1, k)
                values(NH // 4 - 1)
                for t in range(TH):
                    pe.wait_ge(sem["nat1_read"], at("nat1_read", b, 7 + t))
                    transposes((MISC, S[1])[t], [CTX[:, t, i, :] for i in range(BR)], identF[:]
                               ).then_inc(sem["ctxT_ps"], 1)
                for t in range(TH):
                    pe.wait_ge(sem["ctxT_sb"], at("ctxT_sb", b, t + 1))
                    for i in range(BR):
                        last = pe.matmul(ACC[:, ts(t)], CTXT[:, t, ts(i)], WO[:, i, :],
                                         start=i == 0, stop=i == BR - 1)
                last.then_inc(sem["y1"], 1)

            def queries2(b):
                pe.wait_ge(sem["xq"], at("xq", b, 1))
                transposes(MISC[:].bitcast(BF16), [QQB[:, t, :] for t in range(TH)], identB[:]
                           ).then_inc(sem["xqT_ps"], 1)
                pe.wait_ge(sem["xqT_sb"], at("xqT_sb", b, 1))
                for t in range(TH):
                    last = pe.matmul(S[1][:, ts(t)], QQT[:, ts(t)], W2T[:, 0, :], start=True, stop=True)
                last.then_inc(sem["qn"], 1)
                pe.wait_ge(sem["q2parts"], at("q2parts", b, 1))
                transposes(MISC[:].bitcast(BF16), [QP[:, t, i, :] for i in range(3) for t in range(TH)],
                           identB[:]).then_inc(sem["q2T_ps"], 1)

            def ffn(b, k):
                e = expert(k, "weight")
                if e:
                    if e >= 2:
                        pe.wait_ge(sem["xe"], at("xe", b, e - 1))
                    else:
                        pe.wait_ge(sem["route"], at("route", b, 1))
                    for t in range(TH):
                        last = pe.matmul(Z[1][:, ts(t)], CR[:, t, e - 1:e].to_broadcast([P, P]), identF[:],
                                         start=True, stop=True)
                    last.then_inc(sem["bc"], 1)
                for name, w in (("gate", FG), ("up", FU)):
                    e = expert(k, name)
                    if e is not None:
                        dst = Z[0] if w is FG else Z[2]
                        if e:
                            pe.wait_ge(sem["xe"], at("xe", b, e))
                        if e and w is FG:
                            pe.wait_ge(sem["silu"], at("silu", b, e))
                        if e and w is FU:
                            pe.wait_ge(sem["hT"], at("hT", b, e))
                        for c in range(FC):
                            last = pe.matmul(dst[:, c * T:(c + 1) * T], w[:, e, ts(c)],
                                             XE[:, e % 2, :] if e else X2T[:], start=True, stop=True)
                        last.then_inc(sem["g" if w is FG else "up"], 1)
                for t in range(TH):
                    e = expert(k, f"down{t}")
                    if e is not None:
                        pe.wait_ge(sem["hT"], at("hT", b, e + 1))
                        for c in range(FC):
                            last = pe.matmul(S[0][:, ts(t)], HT[:, e % 2, c * T + t * P:c * T + (t + 1) * P],
                                             FD[:, e, c, :], start=(e == 0 and t == 0 and c == 0),
                                             stop=(e == E - 1 and c == FC - 1), skip_group_check=True)
                        if t:
                            last.then_inc(sem["down"], 1)

            def route(b, k):
                if k == 0:
                    pe.wait_ge(sem["x2"], at("x2", b, 1))
                    transposes(MISC, [X2[:, t, :] for t in range(TH)], identF[:]).then_inc(sem["x2T_ps"], 1)
                elif k == 2:
                    pe.wait_ge(sem["x2T_sb"], at("x2T_sb", b, 1))
                    for t in range(TH):
                        last = pe.matmul(MISC[:, 8 * t:8 * t + 8], X2T[:, ts(t)], GW[:], start=True, stop=True)
                    last.then_inc(sem["logits"], 1)

            def maxima(b, with_ffn, nxt):
                for k in range(FFN_BESIDE, FFN_FIRST) if with_ffn else ():
                    ffn(b - 1, k)
                pe.wait_ge(sem["k2stack"], at("k2stack", b, PER["k2stack"]))
                pe.wait_ge(sem["q2stack"], at("q2stack", b, PER["q2stack"]))
                pe.wait_ge(sem["mzero"], at("mzero", b, 2))
                for u in range(NM):
                    if with_ffn and u + FFN_FIRST < FFN_STEPS:
                        ffn(b - 1, u + FFN_FIRST)
                    h, t, c = u // 8, (u // 4) % 2, u % 4
                    before = [v for v in range(u) if MR[v] is MR[u]]
                    if before:
                        name = "mx_read" if before[-1] % 2 else "mx_copy"
                        pe.wait_ge(sem[name], at(name, b, before[-1] // 2 + 1))
                    pe.matmul(MR[u][:, 0:MCOLS], QS2[:, h // 4, h % 2, ts(t)],
                              KS2[:, 4 * (h // 2 % 2) + h // 4, CHUNKS[c]:CHUNKS[c] + MCOLS], start=True, stop=True
                              ).then_inc(sem["mx"], 1)
                pe.wait_ge(setup_done, 1)
                pe.wait_ge(sem["mparts"], at("mparts", b, 1))
                transposes(MISC[:].bitcast(BF16), [MP[:, t, :, :].rearrange("p n h -> p (n h)") for t in range(TH)],
                           identB[:]).then_inc(sem["mT_ps"], 1)

            def softmax2(b, nxt):
                for k in range(PREP_FIRST if nxt else 0):
                    prepare(b + 1, k)
                pe.wait_ge(sem["mstack"], at("mstack", b, PER["mstack"]))
                pe.wait_ge(sem["v2_ready"], at("v2_ready", b, 1))

                def values(g4):
                    q, i = g4 // NT, g4 % NT
                    n = P if i < NT - 1 else LAST
                    if g4 == NT:
                        pe.wait_ge(sem["o2_sb"], at("o2_sb", b, 1))
                    pe.wait_ge(sem["sexp"], at("sexp", b, 4 * g4 + 4))
                    for c in range(4):
                        last = pe.matmul(ACC[32 * c:32 * c + DH + 1, :], V2[0:n, i, 4 * q + c, :],
                                         PR2[0:n, (4 * g4 + c) % 8, :], start=i == 0, stop=i == NT - 1)
                    last.then_inc(sem["av2"], 1)
                    if i == NT - 1:
                        pe.wait_ge(sem["o2_sb"], at("o2_sb", b, q + 1))
                        if q:
                            pe.wait_ge(sem["nat2_read"], at("nat2_read", b, q))
                        transposes(MISC, [O2[:, ts(k)] for k in range(4)], identF[:]).then_inc(sem["nat2"], 1)

                for g4 in range(2 * NT):
                    q, i = g4 // NT, g4 % NT
                    n = P if i < NT - 1 else LAST
                    for c in range(4):
                        u, kv = 4 * g4 + c, 4 * q + c
                        if nxt and u in PREP_AT:
                            prepare(b + 1, PREP_AT[u])
                        before = [v for v in range(u) if SR[v] is SR[u]]
                        if before:
                            pe.wait_ge(sem["sexp"], at("sexp", b, before[-1] + 1))
                        if u == NO_MISC[1]:
                            pe.wait_ge(sem["nat2_read"], at("nat2_read", b, 1))
                        pe.matmul(SR[u][0:n, :], KS2[:, 4 * (kv % 2) + kv // 2, i * P:i * P + n],
                                  QS2[:, kv // 2, :, :].rearrange("p g t -> p (g t)"),
                                  start=True, stop=True).then_inc(sem["s"], 1)
                    if g4:
                        values(g4 - 1)
                values(2 * NT - 1)

            def tail(b, k):
                if k == 5:
                    pe.wait_ge(sem["oq"], at("oq", b, 1))
                    transposes(MISC[:].bitcast(BF16), [OQB[:, t, :] for t in range(TH)], identB[:]
                               ).then_inc(sem["oqT_ps"], 1)
                elif k == 7:
                    pe.wait_ge(sem["oqT_sb"], at("oqT_sb", b, 1))
                    for t in range(TH):
                        last = pe.matmul(S[1][:, ts(t)], OQT[:, ts(t)], W2T[:, 2, :], start=True, stop=True)
                    last.then_inc(sem["y2"], 1)

            def row(b, first=False, last=False):
                attention1(b, first)
                queries2(b)
                maxima(b, with_ffn=not first, nxt=not last)
                softmax2(b, nxt=not last)

            for k in range(PREP_STEPS):
                prepare(0, k)
            row(0, first=True)
            with pe.Fori(1, B - 1) as b:
                row(b)
            row(B - 1, last=True)
            for k in range(TAIL_STEPS):
                tail(B - 1, k)
            for k in range(len(ROUTE_AT)):
                route(B - 1, k)
            for k in range(FFN_STEPS):
                ffn(B - 1, k)

        @block.vector
        def _(dve):
            dve.wait_ge(weights_in, 16 * N_WEIGHTS)
            dve.wait_ge(pool_setup, 2)
            setup = Chain(dve, sem, "dve_setup", 0)
            for dst, value in ((ABS, 0.0), (EPS_LN, 1e-5), (EPS_RMS, 1e-6), (ONE1, 1.0),
                               (V1, 0.0), (V2, 0.0), (KS1, 0.0), (QS1, 0.0), (KS2, 0.0), (QS2, 0.0),
                               (CIN, 0.0)):
                setup(dve.memset(dst[:], value))
            for r in range(2):
                setup(dve.memset(KS2[64 * r + M_ROW:64 * r + M_ROW + 3, 4 * r:4 * r + 4, :], 1.0))
            setup(dve.tensor_copy(identB[:], identF[:]))
            setup(dve.tensor_copy(identH[:], identF[:]))
            for v in (V1, V2):
                setup(dve.memset(v[:, :, :, DH:DH + 1], 1.0))
            for v in (*Z, *S, M, ACC, MISC):
                setup(dve.memset(v[:], 0.0))
            for col, rows, i in ((0, slice(0, P), 0), (1, slice(0, 64), 1), (2, slice(64, P), 1),
                                 (3, slice(0, P), 2)):
                dve.tensor_reduce(out=ABS[rows, col:col + 1], in_=W2[rows, i, :], axis=AX.X,
                                  op=ALU.add, apply_absolute_value=True).then_inc(abs_ready, 1)
            dve.wait_ge(abs_sums, 1)
            for col, n in ((0, P * D), (1, 64 * D), (2, 64 * D), (3, P * D)):
                setup(dve.tensor_scalar(WSC[:, col:col + 1], MISC[:, col:col + 1], 1.0 / n, 1e-5,
                                        ALU.mult, ALU.max))
            setup(dve.reciprocal(WINV[:], WSC[:]))
            for rows, i, col in ((slice(0, P), 0, 0), (slice(0, 64), 1, 1), (slice(64, P), 1, 2),
                                 (slice(0, P), 2, 3)):
                setup(dve.tensor_scalar(W2[rows, i, :], W2[rows, i, :], WINV[rows, col:col + 1], MAGIC,
                                        ALU.mult, ALU.add))
            setup(dve.tensor_scalar(W2, W2, MAGIC, None, ALU.subtract))
            dve.tensor_scalar(W2N[:], W2, -1.0, 1.0, ALU.max, ALU.min).then_inc(ternary, 1)
            setup(dve.tensor_tensor(QC[:], WSC[:, 0:1], WSC[:, 1:2], ALU.mult))
            setup(dve.tensor_scalar(QC[:], QC[:], DH ** -0.5, None, ALU.mult))
            setup(dve.tensor_scalar(SINKS[:], SINKS[:], GATE, None, ALU.mult))
            setup(dve.tensor_scalar(SINKD[:], SINKS[:], GATE * 1e-6, None, ALU.add))
            setup(dve.tensor_tensor(SV[:], SV[:], bcast(SINKS[:], DH), ALU.mult))
            setup(dve.tensor_tensor(BMEAN[:], WOB[:, 0, :], WOB[:, 1, :], ALU.add))
            setup(dve.tensor_tensor(BMEAN[:], BMEAN[:], WOB[:, 2, :], ALU.add))
            setup(dve.tensor_tensor(BMEAN[:], BMEAN[:], WOB[:, 3, :], ALU.add))
            setup(dve.tensor_scalar(BMEAN[:], BMEAN[:], 1.0 / BR, None, ALU.mult))
            dve.wait_ge(ternary_T, 1)
            dve.tensor_copy(W2T[:].rearrange("p n d -> p (n d)"), MISC[:].bitcast(BF16)[:, 0:3 * P]
                            ).then_inc(setup_done, 1)
            setup.end()

            def layer_norm(b, link, src, stats, dst, var_ready, rstd_ready, done):
                for t in range(TH):
                    link(dve.bn_stats(BN[:, t, :], src[:, t, :]), carrier=sem["bn_steps"])
                for t in range(TH):
                    link(dve.bn_aggr(BA[:, t, :], BN[:, t, :]), carrier=sem["bn_steps"])
                dve.tensor_copy(stats[:, 2, :], BA[:, :, 1]).then_inc(sem[var_ready], 1)
                dve.wait_ge(sem[rstd_ready], at(rstd_ready, b, 1))
                for t in range(TH):
                    last = dve.tensor_scalar(dst[:, t, :], src[:, t, :], BA[:, t, 0:1], stats[:, 3, t:t + 1],
                                             ALU.subtract, ALU.mult)
                    if t < TH - 1:
                        link(last)
                last.then_inc(sem[done], 1)

            def mean_square(link, src, stats, ready):
                link(dve.tensor_reduce(out=stats[:, 0, :], in_=src[:], axis=AX.X, op=ALU.max,
                                       apply_absolute_value=True))
                link(dve.tensor_tensor(QSQ[:], src[:], src[:], ALU.mult))
                dve.tensor_reduce(out=stats[:, 1, :], in_=QSQ[:], axis=AX.X, op=ALU.add).then_inc(sem[ready], 1)

            def quant_scales(link, stats, root):
                link(dve.tensor_tensor(stats[:, 5, :], stats[:, 0, :], stats[:, root, :], ALU.mult))
                link(dve.tensor_scalar(stats[:, 5, :], stats[:, 5, :], 1e-5, None, ALU.max))
                link(dve.reciprocal(stats[:, 6, :], stats[:, 5, :]))
                link(dve.tensor_tensor(stats[:, 6, :], stats[:, 6, :], stats[:, root, :], ALU.mult))
                link(dve.tensor_scalar(stats[:, 6, :], stats[:, 6, :], 127.0, None, ALU.mult))
                link(dve.tensor_scalar(stats[:, 7, :], stats[:, 5, :], 1.0 / 127.0, None, ALU.mult))

            link = {}

            def rope(psum, bias_a, bias_b, dst, done):
                chain = link["prep"]
                chain(dve.scalar_tensor_tensor(out=TB[:, 0, :], in0=psum[:, 0:T], scalar=bias_a, in1=COS[:],
                                               op0=ALU.add, op1=ALU.mult))
                chain(dve.scalar_tensor_tensor(out=TB[:, 1, :], in0=psum[:, T:2 * T], scalar=bias_b,
                                               in1=SIN[:], op0=ALU.add, op1=ALU.mult))
                cos_part, sin_part = TB[:, 0, :], TB[:, 1, :]
                if len(dst.shape) == 3:
                    cos_part, sin_part = (v.rearrange("p (h t) -> p h t", h=TH) for v in (cos_part, sin_part))
                ins = dve.tensor_tensor(dst, cos_part, sin_part, ALU.add)
                if done:
                    ins.then_inc(sem[done], 1)
                else:
                    chain(ins)

            def queries(b, br):
                dve.wait_ge(sem["qproj"], at("qproj", b, br + 1))
                rope(Z[br % 2], BQA[:, br:br + 1], BQB[:, br:br + 1], QR[:, :, br, :], "qproj_read")
                dve.wait_ge(sem["qproj_read"], at("qproj_read", b, br + 1))

            def context_projections(b, c):
                i0, i1 = 4 * c, min(4 * c + 4, NT)
                n = i1 - i0
                src = KV_BANKS[c][:, 0:n * P].rearrange("p (n d) -> p n d", d=P)
                dve.wait_ge(sem["kvn"], at("kvn", b, c + 1))
                dve.tensor_tensor(K32[:, i0:i1, :], src[:, :, 0:64], bcast(CST[:, 7, i0:i1], 64), ALU.mult)
                dve.tensor_tensor(V2N[:, i0:i1, :, :],
                                  src[:, :, 64:P].rearrange("p n (h d) -> p n h d", d=DH),
                                  CST[:, 4, i0:i1].unsqueeze(2).unsqueeze(3).to_broadcast(
                                      [P, n, KV, DH]), ALU.mult).then_inc(sem["kvn_read"], 1)

            def prepare(b, k):
                if k == 0:
                    link["prep"] = Chain(dve, sem, "dve_prep", b)
                    dve.wait_ge(sem["x_in"], at("x_in", b, 16))
                    for t in range(TH):
                        link["prep"](dve.tensor_tensor(XB[:, t, :], XIN[:, t, :], BMEAN[:], ALU.add))
                elif k == 3:
                    dve.wait_ge(sem["kproj"], at("kproj", b, 1))
                    rope(Z[1], BKA[:], BKB[:], KR[:], None)
                    dve.tensor_tensor(KSQ[:], KR[:], KR[:], ALU.mult).then_inc(sem["ksq_sb"], 1)
                    dve.wait_ge(sem["vproj"], at("vproj", b, 1))
                    for t in range(TH):
                        last = dve.tensor_tensor(V1[:, t, :, 0:DH],
                                                 Z[2][:, ts(t)].rearrange("p (h d) -> p h d", d=DH),
                                                 BV[:].rearrange("p (h d) -> p h d", d=DH), ALU.add)
                    last.then_inc(sem["v1_ready"], 1)
                elif k == 5:
                    queries(b, 0)
                    dve.wait_ge(sem["knorm_ps"], at("knorm_ps", b, 1))
                    dve.tensor_scalar(KSQ[:], Z[2][:, 0:T], 1e-6, None, ALU.max).then_inc(sem["knorm_sb"], 1)
                    queries(b, 1)
                elif k == 9:
                    queries(b, 2)
                    queries(b, 3)
                    context_projections(b, 0)
                    dve.wait_ge(sem["krs"], at("krs", b, 1))
                    link["prep"](dve.scalar_tensor_tensor(out=TB[:, 0, :], in0=KR[:], scalar=KGAIN, in1=KRS[:],
                                                          op0=ALU.mult, op1=ALU.mult))
                    link["prep"](dve.tensor_copy(KHL[:, 0, :], TB[:, 0, :]))
                    dve.tensor_tensor(KHL[:, 1, :], TB[:, 0, :], KHL[:, 0, :], ALU.subtract).then_inc(sem["kparts"], 1)
                elif k == 11:
                    context_projections(b, 1)
                    context_projections(b, 2)
                elif k == 13:
                    context_projections(b, 3)
                    dve.wait_ge(sem["kvn_read"], at("kvn_read", b, 4))
                    link["prep"](dve.tensor_copy(KHN[:, :, 0, :], K32[:]))
                    dve.tensor_tensor(KHN[:, :, 1, :], K32[:], KHN[:, :, 0, :], ALU.subtract).then_inc(sem["khl"], 1)
                elif k == 16:
                    link["prep"](dve.tensor_copy(QABC[:, 0], QR[:]))
                    link["prep"](dve.tensor_tensor(QRES[:], QR[:], QABC[:, 0], ALU.subtract))
                    link["prep"](dve.tensor_copy(QABC[:, 1], QRES[:]))
                    dve.tensor_tensor(QABC[:, 2], QRES[:], QABC[:, 1], ALU.subtract).then_inc(sem["qparts"], 1)
                    link["prep"].end()

            def quantise_context(b, k):
                if k == 0:
                    link["ctx"] = Chain(dve, sem, "dve_ctx", b)
                    dve.wait_ge(sem["csq"], at("csq", b, 1))
                    dve.tensor_reduce(out=CST[:, 1, :], in_=CSQ[:], axis=AX.X, op=ALU.add).then_inc(sem["cn_ms"], 1)
                    link["ctx"](dve.tensor_reduce(out=CST[:, 0, :], in_=CIN[:], axis=AX.X, op=ALU.max,
                                                  apply_absolute_value=True))
                elif k == 2:
                    dve.wait_ge(sem["cn_r"], at("cn_r", b, 1))
                    quant_scales(link["ctx"], CST, 2)
                    link["ctx"](dve.tensor_scalar(CST[:, 4, :], CST[:, 7, :], WSC[:, 2:3], None, ALU.mult))
                elif k == 3:
                    link["ctx"](dve.tensor_tensor(CIN[:], CIN[:], bcast(CST[:, 6, :], D), ALU.mult))
                elif k == 4:
                    dve.tensor_scalar(CQB[:], CIN[:], MAGIC, MAGIC, ALU.add, ALU.subtract).then_inc(sem["yq"], 1)
                    link["ctx"].end()

            def attention1(b, first):
                def z_tile(u):
                    return PRB[:, (u // 3) % 8, u % 3, :, :].rearrange("p b t -> p (b t)")

                def z_cap(u):
                    dve.wait_ge(sem["zexp"], at("zexp", b, u + 1))
                    dve.tensor_scalar(z_tile(u), z_tile(u), CAP, None, ALU.min).then_inc(sem["zcap"], 1)

                def z_max(u):
                    dve.wait_ge(sem["zln"], at("zln", b, u + 1))
                    dve.scalar_tensor_tensor(out=z_tile(u), in0=ZR[u % 4][:], scalar=ZSCALE, in1=z_tile(u),
                                             op0=ALU.mult, op1=ALU.max).then_inc(sem["zmax"], 1)

                def threshold(h, br):
                    dve.wait_ge(sem["gated"], at("gated", b, h + 1))
                    v = PRB[:, h % 8, :, br, :]
                    dve.scalar_tensor_tensor(out=v, in0=v, scalar=SINKS[:, NH * br + h:NH * br + h + 1],
                                             in1=v, op0=ALU.is_ge, op1=ALU.mult).then_inc(sem["thr"], 1)

                nat = Chain(dve, sem, "dve_nat", b)

                def copies(g):
                    dve.wait_ge(sem["av1"], at("av1", b, g + 1))
                    if g:
                        dve.wait_ge(sem["nat1"], at("nat1", b, 2 * g))
                    dve.tensor_copy(O1[:, 0, :], ACC[:]).then_inc(sem["av1_sb"], 1)
                    dve.tensor_copy(O1[:, 1, :], M[:]).then_inc(sem["av1_sb"], 1)

                def normalise(g, t):
                    dve.wait_ge(sem["nat1"], at("nat1", b, 2 * g + t + 1))
                    src = (MISC, S[1])[t][:].rearrange("p (n h c) -> p n h c", n=BR, c=32)
                    sink = SINKD[:].rearrange("p (n h) -> p n h", n=BR)[:, :, 4 * g:4 * g + 4]
                    null = SV[:].rearrange("p (n h) d -> p n h d", n=BR)[:, :, 4 * g:4 * g + 4, :]
                    dst = CTX[:, t, :, :].rearrange("p n (h d) -> p n h d", d=DH)[:, :, 4 * g:4 * g + 4, :]
                    nat(dve.tensor_tensor(DEN[:, t], src[:, :, :, DH], sink, ALU.add))
                    nat(dve.reciprocal(DEN[:, t], DEN[:, t]))
                    nat(dve.tensor_tensor(dst, src[:, :, :, 0:DH], null, ALU.add))
                    dve.tensor_tensor(dst, dst, DEN[:, t].unsqueeze(3).to_broadcast([P, BR, 4, DH]),
                                      ALU.mult).then_inc(sem["nat1_read"], 1)

                for g in range(NH // 4):
                    for i in range(12):
                        for k in TAIL_AT.get(12 * g + i, ()) if not first else ():
                            tail(b - 1, k)
                        if not first and 12 * g + i in ROUTE_AT:
                            route(b - 1, ROUTE_AT[12 * g + i])
                        z_cap(12 * g + i)
                        if i > 1:
                            z_max(12 * g + i - 2)
                        if g and i < DVE_TO_TILE:
                            threshold(*DVE_BRANCHES[DVE_TO_TILE * (g - 1) + i])
                    z_max(12 * g + 10)
                    z_max(12 * g + 11)
                    if 0 < g < NH // 4 - 1:
                        copies(g - 1)
                        for t in range(TH):
                            normalise(g - 1, t)
                for h, br in DVE_BRANCHES[3 * DVE_TO_TILE:]:
                    threshold(h, br)
                    if br == BR - 1 and h == NH - 4:
                        copies(NH // 4 - 2)
                    if br == BR - 1 and not first:
                        for k in range(*BESIDE[h]):
                            ffn(b - 1, k)
                for t in range(TH):
                    normalise(NH // 4 - 2, t)
                for r in range(2):
                    dve.memset(QS2[64 * r + M_ROW:64 * r + M_ROW + 3, :, :, :], 0.0).then_inc(sem["mzero"], 1)
                copies(NH // 4 - 1)
                for t in range(TH):
                    normalise(NH // 4 - 1, t)
                nat.end()

            def output1(b):
                link = Chain(dve, sem, "dve_ln1", b)
                dve.wait_ge(sem["y1"], at("y1", b, 1))
                link(dve.scalar_tensor_tensor(out=RES[:].rearrange("p h d -> p (h d)"), in0=ACC[:, 0:T],
                                              scalar=1.0 / BR, in1=XB[:].rearrange("p h d -> p (h d)"),
                                              op0=ALU.mult, op1=ALU.add))
                layer_norm(b, link, RES, LST, X1, "ln1_var", "ln1_rstd", "x1")
                dve.wait_ge(sem["x1"], at("x1", b, 1))
                link.end()


            def queries2(b):
                link = Chain(dve, sem, "dve_q", b)
                mean_square(link, X1, QST, "qn_ms")
                dve.wait_ge(sem["qn_r"], at("qn_r", b, 1))
                quant_scales(link, QST, 2)
                link(dve.tensor_scalar(QST[:, 7, :], QST[:, 7, :], QC[:], None, ALU.mult))
                link(dve.tensor_tensor(QSQ[:], X1[:], bcast(QST[:, 6, :], D), ALU.mult))
                dve.tensor_scalar(QQB[:], QSQ[:], MAGIC, MAGIC, ALU.add, ALU.subtract).then_inc(sem["xq"], 1)
                dve.wait_ge(sem["qn"], at("qn", b, 1))
                link(dve.tensor_tensor(Q32[:], S[1][:, 0:T].rearrange("p (h d) -> p h d", d=D),
                                       bcast(QST[:, 7, :], D), ALU.mult))
                link(dve.tensor_copy(QP[:, :, 0, :], Q32[:]))
                link(dve.tensor_tensor(Q32[:], Q32[:], QP[:, :, 0, :], ALU.subtract))
                link(dve.tensor_copy(QP[:, :, 1, :], Q32[:]))
                dve.tensor_tensor(QP[:, :, 2, :], Q32[:], QP[:, :, 1, :], ALU.subtract).then_inc(sem["q2parts"], 1)
                link.end()


            def maxima(b, with_ffn, nxt):
                chain = Chain(dve, sem, "dve_m", b)

                def batch(k):
                    place = 8 * (k // 2 % 2) + 2 * (k // 4) + k % 2
                    slots = MSCAN[:, 4 * (k % 4):4 * (k % 4) + 4, MCOLS - 1:MCOLS].rearrange(
                        "p (t c) o -> p t (c o)", t=TH)
                    dve.tensor_reduce(out=MX[:, :, place:place + 1], in_=slots, axis=AX.X, op=ALU.max, negate=True
                                      ).then_inc(sem["mx_head"], 1)

                for k in range(FFN_BESIDE, FFN_FIRST) if with_ffn else ():
                    ffn(b - 1, k)
                for u in range(NM):
                    if nxt and u in CTX_AT:
                        quantise_context(b + 1, CTX_AT[u])
                    if with_ffn and u + FFN_FIRST < FFN_STEPS:
                        ffn(b - 1, u + FFN_FIRST)
                    if u % 2:
                        h = u // 8
                        dve.wait_ge(sem["mx_copy"], at("mx_copy", b, u // 2 + 1))
                        dve.wait_ge(sem["mx"], at("mx", b, u + 1))
                        dve.tensor_tensor_scan(out=MSCAN[:, u // 2 % 16, :], data0=MR[u][:, 0:MCOLS],
                                               data1=MCOPY[:, u // 2 % 4, :], initial=LOWEST,
                                               op0=ALU.max, op1=ALU.max).then_inc(sem["mx_read"], 1)
                        if h and u % 8 == 1:
                            dve.wait_ge(sem["mx_read"], at("mx_read", b, 4 * h))
                            batch(h - 1)
                dve.wait_ge(sem["mx_read"], at("mx_read", b, NM // 2))
                batch(NH - 1)
                dve.wait_ge(sem["mx_head"], at("mx_head", b, NH))
                link = chain
                link(dve.tensor_copy(MP[:, :, 0, :], MX[:]))
                link(dve.tensor_tensor(MX[:], MX[:], MP[:, :, 0, :], ALU.subtract))
                link(dve.tensor_copy(MP[:, :, 1, :], MX[:]))
                dve.tensor_tensor(MP[:, :, 2, :], MX[:], MP[:, :, 1, :], ALU.subtract).then_inc(sem["mparts"], 1)
                link.end()


            def softmax2(b, nxt):
                if nxt:
                    for k in range(PREP_STEPS):
                        prepare(b + 1, k)
                normalise2(b, 0)

            def normalise2(b, q):
                if q == 0:
                    link["out"] = Chain(dve, sem, "dve_o", b)
                dve.wait_ge(sem["nat2"], at("nat2", b, q + 1))
                src = MISC[:].rearrange("p (g h k c) -> p g h k c", g=2, h=TH, c=32)
                link["out"](dve.reciprocal(DEN[:].rearrange("p a b c -> p (a b c)")[:, 0:16],
                                           MISC[:].rearrange("p (k c) -> p k c", c=32)[:, :, DH]))
                for g in range(2):
                    den = DEN[:].rearrange("p a b c -> p (a b c)")[:, 8 * g:8 * g + 8].rearrange(
                        "p (h k) -> p h k", h=TH)
                    last = dve.tensor_tensor(ON[:, :, 8 * q + g:8 * q + g + 7:2, :], src[:, g, :, :, 0:DH],
                                             den.unsqueeze(3).to_broadcast([P, TH, 4, DH]), ALU.mult)
                    if g:
                        last.then_inc(sem["nat2_read"], 1)
                dve.wait_ge(sem["nat2_read"], at("nat2_read", b, q + 1))

            def tail(b, k):
                on = ON[:].rearrange("p h n d -> p h (n d)")
                out = link["out"]
                out.b = b
                if k == 0:
                    normalise2(b, 1)
                    for t in range(TH):
                        out(dve.bn_stats(BN[:, t, :], on[:, t, :]), carrier=sem["bn_steps"])
                    for t in range(TH):
                        out(dve.bn_aggr(BA[:, t, :], BN[:, t, :]), carrier=sem["bn_steps"])
                    dve.tensor_copy(OST[:, 1, :], BA[:, :, 1]).then_inc(sem["on_var"], 1)
                elif k == 2:
                    dve.wait_ge(sem["on_rstd"], at("on_rstd", b, 1))
                    for t in range(TH):
                        out(dve.tensor_scalar(on[:, t, :], on[:, t, :], BA[:, t, 0:1], OST[:, 2, t:t + 1],
                                               ALU.subtract, ALU.mult))
                    out(dve.tensor_tensor(on, on, GAM[:].unsqueeze(1).to_broadcast([P, TH, D]), ALU.mult))
                    out(dve.tensor_tensor(on, on, BET[:].unsqueeze(1).to_broadcast([P, TH, D]), ALU.add))
                    out(dve.tensor_reduce(out=OST[:, 0, :], in_=on, axis=AX.X, op=ALU.max,
                                           apply_absolute_value=True))
                    out(dve.tensor_tensor(OSQ[:], on, on, ALU.mult))
                    dve.tensor_reduce(out=OST[:, 3, :], in_=OSQ[:], axis=AX.X, op=ALU.add).then_inc(sem["on_ms"], 1)
                elif k == 4:
                    dve.wait_ge(sem["on_r"], at("on_r", b, 1))
                    quant_scales(out, OST, 4)
                    out(dve.tensor_scalar(OST[:, 7, :], OST[:, 7, :], WSC[:, 3:4], None, ALU.mult))
                    out(dve.tensor_tensor(OSQ[:], on, bcast(OST[:, 6, :], D), ALU.mult))
                    dve.tensor_scalar(OQB[:], OSQ[:], MAGIC, MAGIC, ALU.add, ALU.subtract).then_inc(sem["oq"], 1)
                elif k == 8:
                    dve.wait_ge(sem["y2"], at("y2", b, 1))
                    out(dve.tensor_tensor(RES[:], S[1][:, 0:T].rearrange("p (h d) -> p h d", d=D),
                                           bcast(OST[:, 7, :], D), ALU.mult))
                    out(dve.tensor_tensor(RES[:], RES[:], X1[:], ALU.add))
                    layer_norm(b, out, RES, LST, X2, "ln2_var", "ln2_rstd", "x2")
                    out.end()

            def ffn(b, k):
                e = expert(k, "inputs")
                if e:
                    dve.wait_ge(sem["bc"], at("bc", b, e))
                    if e >= 3:
                        dve.wait_ge(sem["up"], at("up", b, e - 1))
                    dve.tensor_tensor(XE[:, e % 2, :], Z[1][:, 0:T], X2T[:], ALU.mult).then_inc(sem["xe"], 1)
                e = expert(k, "hidden")
                if e is not None:
                    dve.wait_ge(sem["silu"], at("silu", b, e + 1))
                    dve.wait_ge(sem["up"], at("up", b, e + 1))
                    if e >= 2:
                        dve.wait_ge(sem["down"], at("down", b, e - 1))
                    dve.tensor_tensor(HT[:, e % 2, :], Z[2][:], SG[:, e % 2, :], ALU.mult).then_inc(sem["hT"], 1)
                if k == FFN_STEPS - 1:
                    chain = Chain(dve, sem, "dve_ln3", b)
                    dve.wait_ge(sem["down"], at("down", b, E))
                    chain(dve.tensor_tensor(RES[:].rearrange("p h d -> p (h d)"), S[0][:, 0:T],
                                            X2[:].rearrange("p h d -> p (h d)"), ALU.add))
                    dve.wait_ge(sem["out_free"], at("out_free", b, 1))
                    layer_norm(b, chain, RES, LST3, OUT, "ln3_var", "ln3_rstd", "out_ready")
                    chain.end()

            def route(b, k):
                if k == 3:
                    link["route"] = Chain(dve, sem, "dve_route", b)
                    dve.wait_ge(sem["logits"], at("logits", b, 1))
                    dve.tensor_copy(LG[:, 1], MISC[:, 0:8 * TH].rearrange("p (h e) -> p h e", e=8)
                                    ).then_inc(sem["lg_sb"], 1)
                    dve.wait_ge(sem["lg_sb"], at("lg_sb", b, 1))
                    dve.tensor_reduce(out=LM[:, 0, :], in_=LG[:, 1], axis=AX.X, op=ALU.max).then_inc(sem["lmax"], 1)
                    dve.wait_ge(sem["lmax"], at("lmax", b, 1))
                    link["route"](dve.tensor_tensor(LG[:, 0], LG[:, 1], bcast(LM[:, 0, :], 8), ALU.is_equal))
                    link["route"](dve.tensor_tensor(LG[:, 0], LG[:, 0], IOTA8[:], ALU.mult))
                    link["route"](dve.tensor_reduce(out=LM[:, 2, :], in_=LG[:, 0], axis=AX.X, op=ALU.max))
                    link["route"](dve.tensor_tensor(LG[:, 0], IOTA8[:], bcast(LM[:, 2, :], 8), ALU.is_equal))
                elif k == 5:
                    dve.wait_ge(sem["lexp"], at("lexp", b, 1))
                    link["route"](dve.tensor_scalar(LM[:, 3, :], LM[:, 1, :], 1.0, None, ALU.add))
                    link["route"](dve.reciprocal(LM[:, 3, :], LM[:, 3, :]))
                    dve.tensor_tensor(CR[:], LG[:, 0], bcast(LM[:, 3, :], 8), ALU.mult).then_inc(sem["route"], 1)
                    link["route"].end()

            def row(b, first=False, last=False):
                attention1(b, first)
                output1(b)
                queries2(b)
                maxima(b, with_ffn=not first, nxt=not last)
                softmax2(b, nxt=not last)

            for k in range(CTX_STEPS):
                quantise_context(0, k)
            for k in range(PREP_STEPS):
                prepare(0, k)
            row(0, first=True)
            with dve.Fori(1, B - 1) as b:
                row(b)
            row(B - 1, last=True)
            for k in range(TAIL_STEPS):
                tail(B - 1, k)
            for k in range(len(ROUTE_AT)):
                route(B - 1, k)
            for k in range(FFN_STEPS):
                ffn(B - 1, k)


def _layout(inputs):
    f = {k: np.ascontiguousarray(np.asarray(v)) for k, v in inputs.items()}
    perm_a = np.concatenate([np.arange(0, DH, 2), np.arange(1, DH, 2)])
    perm_b = np.concatenate([np.arange(1, DH, 2), np.arange(0, DH, 2)])

    def cols(w, perm):
        w = w.reshape(w.shape[:-1] + (-1, NH // 2, 2, DH))[..., perm]
        return np.moveaxis(w, -3, -1).reshape(w.shape[:-4] + (-1,))

    def rows(w, group):
        return w.reshape(-1, 2, group, DH, D).transpose(1, 3, 0, 2, 4).reshape(w.shape)

    wq, bq, wk, bk = (f["L0_attn_" + n] for n in ("W_Q", "b_Q", "W_K", "b_K"))
    inv_freq = (1.0 / 10000.0 ** (np.arange(0, DH, 2, dtype=np.float32) / DH)).astype(np.float32)
    angle = (np.arange(T, dtype=np.float32)[:, None] * inv_freq[None, :]).astype(np.float32)
    cos, sin = np.cos(angle).T, np.sin(angle).T
    rope_cos = np.tile(np.repeat(np.concatenate([cos, cos]), NH // 2, axis=0), (2, 1)).astype(np.float32)
    rope_sin = np.tile(np.repeat(np.concatenate([-sin, sin]), NH // 2, axis=0), (2, 1)).astype(np.float32)
    r_of, n_of = np.arange(P) // 64, np.arange(P) % (NH // 2)
    heads = ((r_of[:, None] == r_of) & (n_of[:, None] == n_of)).astype(np.float32)

    def experts(shared, routed):
        return np.concatenate([shared[None], routed])

    g, u = (experts(f["L0_ffn_shared_" + n], f["L0_ffn_r_" + n]) for n in ("gate", "up"))
    dn = experts(f["L0_ffn_shared_down"], f["L0_ffn_r_down"])
    return dict(
        x=f["x"], ctx_t=f["ctx_1024"],
        wqA=cols(wq, perm_a), wqB=cols(wq, perm_b), wkA=cols(wk, perm_a), wkB=cols(wk, perm_b),
        wv=f["L0_attn_W_V"],
        bqA=cols(bq, perm_a).reshape(BR, P).T, bqB=cols(bq, perm_b).reshape(BR, P).T,
        bkA=cols(bk, perm_a).reshape(P, 1), bkB=cols(bk, perm_b).reshape(P, 1),
        bv=f["L0_attn_b_V"], sinks=f["L0_attn_sink_scalars"], vnull=f["L0_attn_v_nulls"].reshape(-1),
        wo=f["L0_attn_W_O"].transpose(1, 0, 2), wob=f["L0_attn_W_O_bias"].reshape(-1),
        w2q=rows(f["L0_xattn_wq"], 2), w2kv=np.concatenate([rows(f["L0_xattn_wk"], 1), f["L0_xattn_wv"]]),
        w2o=f["L0_xattn_wo"], gamma=f["L0_xattn_ln_gamma"], beta=f["L0_xattn_ln_beta"],
        gate_w=f["L0_ffn_gate_w"].T,
        ffn_g=g.transpose(2, 0, 1), ffn_u=u.transpose(2, 0, 1),
        ffn_d=dn.reshape(E, D, FC, P).transpose(3, 0, 2, 1),
        rope_cos=rope_cos, rope_sin=rope_sin, heads=heads, ident=np.eye(P, dtype=np.float32),
    )


def kernel(**inputs):
    import concourse.bacc as _bacc
    from concourse.bass_utils import run_bass_kernel_spmd as _run

    nc = _bacc.Bacc("TRN2", target_bir_lowering=False, num_devices=1, dynamic_dma_scratch_size=1024)
    arrays, args = {}, {}
    for name, a in _layout(inputs).items():
        a = np.ascontiguousarray(a)
        arrays["in_" + name] = a
        args[name] = nc.dram_tensor("in_" + name, a.shape, mybir.dt.from_np(a.dtype), kind="ExternalInput").ap()
    args["out"] = nc.dram_tensor("out_0", (B, T, D), F32, kind="ExternalOutput").ap()
    build(nc, **args)
    r = _run(nc, [arrays], core_ids=[0])
    return r.results[0]["out_0"]
```
